# Optimizing a Trainium2 kernel written in Bass

```python
import numpy as np
import jax
import jax.numpy as jnp

def _softmax(x, axis=-1):
    return jax.nn.softmax(x, axis=axis)

def _gelu(x):
    return jax.nn.gelu(x, approximate=True)

def _silu(x):
    return jax.nn.silu(x)

def _sigmoid(x):
    return jax.nn.sigmoid(x)

def _layernorm(x, axis=-1, eps=1e-05):
    m = jnp.mean(x, axis=axis, keepdims=True)
    v = jnp.var(x, axis=axis, keepdims=True)
    return (x - m) / jnp.sqrt(v + eps)

def _scatter_add(tgt, idx, src, axis=0):
    return tgt.at[idx].add(src)

def _segment_sum(src, seg, n):
    return jax.ops.segment_sum(src, seg, n)
kernel_name = 'mk_decoder_postln_d4_seqx_r4_11e1e7'

def setup_inputs(seed: int=0):
    np.random.seed(seed)
    _w = jnp.asarray

    def _rec_inputs():
        import jax
        import jax.numpy as jnp
        _rk = jax.random.key(seed)
        x = -0.0003929 + 0.9999 * jax.random.normal(jax.random.fold_in(_rk, 1), (2, 1024, 256), jnp.float32)
        _lenS = 1024 - jax.random.randint(jax.random.fold_in(_rk, 7), (2,), 0, max(1, 1024 // 4) + 1, jnp.int32)
        _lenS2 = 77 - jax.random.randint(jax.random.fold_in(_rk, 8), (2,), 0, max(1, 77 // 4) + 1, jnp.int32)
        _ctx_1024P = jax.random.normal(jax.random.fold_in(_rk, 11), (2, 16, 256), jnp.float32)
        _ctx_1024c = jax.random.dirichlet(jax.random.fold_in(_rk, 511), 0.3 * jnp.ones((16,), jnp.float32), (2, 77))
        _ctx_1024t = jnp.einsum('bsk,bkd->bsd', _ctx_1024c, _ctx_1024P)
        _ctx_1024t = _ctx_1024t * jax.lax.rsqrt(jnp.mean(jnp.square(_ctx_1024t)) + 1e-12) * 0.953939
        ctx_1024 = 2.81802e-05 + 1.00001 * (_ctx_1024t + 0.3 * jax.random.normal(jax.random.fold_in(_rk, 611), (2, 77, 256), jnp.float32))
        _validS = jnp.arange(1024)[None, :] < _lenS[:, None]
        _validS2 = jnp.arange(77)[None, :] < _lenS2[:, None]
        _causal = jnp.tril(jnp.ones((1024, 1024), dtype=bool))
        mask_S2_ik0 = jnp.where(_validS2[0], 0, 1).astype(jnp.int32)
        mask_BxS2_bf0 = jnp.logical_not(jnp.ones((2, 77), dtype=bool))
        mask_Bx1xSxS2_ik1 = jnp.where(jnp.broadcast_to(_validS2[:, None, None, :], (2, 1, 1024, 77)), 1, 0).astype(jnp.int32)
        return (x, ctx_1024, mask_S2_ik0, mask_BxS2_bf0, mask_Bx1xSxS2_ik1)
    x, ctx_1024, mask_S2_ik0, mask_BxS2_bf0, mask_Bx1xSxS2_ik1 = _rec_inputs()

    def _L0_attn_setup():
        import jax, jax.numpy as jnp
        import numpy as np
        B, S, D = (4, 2048, 256)

        def log_g(x):
            return jnp.where(x >= 0, jnp.log(jax.nn.relu(x) + 0.5), -jax.nn.softplus(-x))

        def parallel_scan_log(log_coeffs, log_values):
            a_star = jnp.cumsum(log_coeffs, axis=1)
            log_h = a_star + jax.lax.cumlogsumexp(log_values - a_star, axis=1)
            return jnp.exp(log_h)
        key = jax.random.key(seed)
        k1, k2, k3, k4 = jax.random.split(key, 4)
        x_t = jax.random.normal(k1, (B, S, D), dtype=jnp.float32)
        w_i = jax.random.normal(k2, (D,), dtype=jnp.float32) * 0.1
        w_f = jax.random.normal(k3, (D,), dtype=jnp.float32) * 0.1
        w_h = jax.random.normal(k4, (D,), dtype=jnp.float32) * 0.1
        return {'x_t': x_t, 'w_i': w_i, 'w_f': w_f, 'w_h': w_h}
    _L0_attn_all = _L0_attn_setup()
    _L0_attn_in = {k: v for k, v in _L0_attn_all.items() if k in ('w_i', 'w_f', 'w_h')}
    del _L0_attn_all

    def _L0_xattn_setup():
        import jax, jax.numpy as jnp
        import numpy as np
        DIM = 256
        NUM_HEADS = 8
        SCALE = (DIM // NUM_HEADS) ** (-0.5)
        key = jax.random.key(seed)
        k1, k2, k3, k4, k5, k6 = jax.random.split(key, 6)
        B, N, M, C = (8, 512, 512, DIM)
        x = jax.random.normal(k1, (B, N, C), dtype=jnp.float32)
        support = jax.random.normal(k2, (B, M, C), dtype=jnp.float32)
        attn_mask = jax.random.randint(k3, (M,), 0, 2, dtype=jnp.int32)
        qkv_w = jax.random.normal(k4, (3 * C, C), dtype=jnp.float32) * C ** (-0.5)
        proj_w = jax.random.normal(k5, (C, C), dtype=jnp.float32) * C ** (-0.5)
        proj_b = jax.random.normal(k6, (C,), dtype=jnp.float32) * 0.01
        return {'x': x, 'support': support, 'attn_mask': attn_mask, 'qkv_w': qkv_w, 'proj_w': proj_w, 'proj_b': proj_b}
    _L0_xattn_all = _L0_xattn_setup()
    _L0_xattn_in = {k: v for k, v in _L0_xattn_all.items() if k in ('qkv_w', 'proj_w', 'proj_b')}
    del _L0_xattn_all

    def _L0_ffn_setup():
        import jax, jax.numpy as jnp
        import numpy as np
        D_MODEL = 256
        EXPANSION = 4
        D_HIDDEN = D_MODEL * EXPANSION
        NUM_STAGES = int(np.log2(D_HIDDEN))

        def butterfly(y, weights, dim):
            lead = y.shape[:-1]
            for stage in range(weights.shape[0]):
                s = 2 ** stage
                nb = dim // (2 * s)
                yr = y.reshape(*lead, nb, 2, s)
                a = yr[..., 0, :]
                b = yr[..., 1, :]
                w = weights[stage].reshape(nb, s, 2, 2)
                na = w[..., 0, 0] * a + w[..., 0, 1] * b
                nb2 = w[..., 1, 0] * a + w[..., 1, 1] * b
                y = jnp.stack([na, nb2], axis=-2).reshape(*lead, dim)
            return y
        key = jax.random.key(seed)
        ks = jax.random.split(key, 6)
        B, S = (4, 512)
        x = jax.random.normal(ks[0], (B, S, D_MODEL), jnp.float32)
        W_exp = jax.random.normal(ks[1], (D_MODEL, D_HIDDEN), jnp.float32) * 0.02
        b_exp = jnp.zeros((D_HIDDEN,), jnp.float32)
        up_weights = jax.random.normal(ks[2], (NUM_STAGES, D_HIDDEN // 2, 2, 2), jnp.float32) * 0.02
        up_bias = jnp.zeros((D_HIDDEN,), jnp.float32)
        down_weights = jax.random.normal(ks[3], (NUM_STAGES, D_HIDDEN // 2, 2, 2), jnp.float32) * 0.02
        W_con = jax.random.normal(ks[4], (D_HIDDEN, D_MODEL), jnp.float32) * 0.02
        b_con = jnp.zeros((D_MODEL,), jnp.float32)
        down_bias = jnp.zeros((D_MODEL,), jnp.float32)
        return dict(x=x, W_exp=W_exp, b_exp=b_exp, up_weights=up_weights, up_bias=up_bias, down_weights=down_weights, W_con=W_con, b_con=b_con, down_bias=down_bias)
    _L0_ffn_all = _L0_ffn_setup()
    _L0_ffn_in = {k: v for k, v in _L0_ffn_all.items() if k in ('W_exp', 'b_exp', 'up_weights', 'up_bias', 'down_weights', 'W_con', 'b_con', 'down_bias')}
    del _L0_ffn_all

    def _L1_attn_setup():
        import jax, jax.numpy as jnp
        import numpy as np
        import math
        DIM = 256
        NUM_HEADS = 16
        HEAD_DIM = DIM // NUM_HEADS
        B, S = (2, 512)
        key = jax.random.key(seed)
        ks = jax.random.split(key, 9)
        sc = 0.02
        return {'x': jax.random.normal(ks[0], (B, S, DIM), jnp.float32), 'Wq': jax.random.normal(ks[1], (DIM, DIM), jnp.float32) * sc, 'bq': jax.random.normal(ks[2], (DIM,), jnp.float32) * sc, 'Wk': jax.random.normal(ks[3], (DIM, DIM), jnp.float32) * sc, 'bk': jax.random.normal(ks[4], (DIM,), jnp.float32) * sc, 'Wv': jax.random.normal(ks[5], (DIM, DIM), jnp.float32) * sc, 'bv': jax.random.normal(ks[6], (DIM,), jnp.float32) * sc, 'Wo': jax.random.normal(ks[7], (DIM, DIM), jnp.float32) * sc, 'bo': jax.random.normal(ks[8], (DIM,), jnp.float32) * sc}
    _L1_attn_all = _L1_attn_setup()
    _L1_attn_in = {k: v for k, v in _L1_attn_all.items() if k in ('Wq', 'bq', 'Wk', 'bk', 'Wv', 'bv', 'Wo', 'bo')}
    del _L1_attn_all

    def _L1_xattn_setup():
        import jax, jax.numpy as jnp
        import numpy as np
        B, S, D, H = (2, 512, 256, 16)
        HD = D // H
        SCALE = HD ** (-0.5)
        NEG = -1000000000.0
        key = jax.random.key(seed)
        ks = jax.random.split(key, 7)
        w_std = 1.0 / np.sqrt(D)
        return {'query': jax.random.normal(ks[0], (B, S, D), dtype=jnp.float32), 'key': jax.random.normal(ks[1], (B, S, D), dtype=jnp.float32), 'value': jax.random.normal(ks[2], (B, S, D), dtype=jnp.float32), 'Wq': jax.random.normal(ks[3], (D, D), dtype=jnp.float32) * w_std, 'Wk': jax.random.normal(ks[4], (D, D), dtype=jnp.float32) * w_std, 'Wv': jax.random.normal(ks[5], (D, D), dtype=jnp.float32) * w_std, 'Wo': jax.random.normal(ks[6], (D, D), dtype=jnp.float32) * w_std}
    _L1_xattn_all = _L1_xattn_setup()
    _L1_xattn_in = {k: v for k, v in _L1_xattn_all.items() if k in ('Wq', 'Wk', 'Wv', 'Wo')}
    del _L1_xattn_all

    def _L1_ffn_setup():
        import jax, jax.numpy as jnp
        import numpy as np
        TOP_K = 2
        EPS = 1e-20
        key = jax.random.key(seed)
        ks = jax.random.split(key, 8)
        B, S, H, E, D = (4, 512, 256, 8, 512)
        s = 0.02
        return {'x': jax.random.normal(ks[0], (B, S, H), dtype=jnp.float32), 'Wr': jax.random.normal(ks[1], (H, E), dtype=jnp.float32) * s, 'Wg': jax.random.normal(ks[2], (E, H, D), dtype=jnp.float32) * s, 'Wu': jax.random.normal(ks[3], (E, H, D), dtype=jnp.float32) * s, 'Wd': jax.random.normal(ks[4], (E, D, H), dtype=jnp.float32) * s, 'Sg': jax.random.normal(ks[5], (H, D), dtype=jnp.float32) * s, 'Su': jax.random.normal(ks[6], (H, D), dtype=jnp.float32) * s, 'Sd': jax.random.normal(ks[7], (D, H), dtype=jnp.float32) * s}
    _L1_ffn_all = _L1_ffn_setup()
    _L1_ffn_in = {k: v for k, v in _L1_ffn_all.items() if k in ('Wr', 'Wg', 'Wu', 'Wd', 'Sg', 'Su', 'Sd')}
    del _L1_ffn_all

    def _L2_attn_setup():
        import jax, jax.numpy as jnp
        import numpy as np
        import math
        B, S, E, H = (2, 512, 256, 16)
        D = E // H
        key = jax.random.key(seed)
        ks = jax.random.split(key, 5)
        scale_p = 1.0 / math.sqrt(D)
        return {'x': jax.random.normal(ks[0], (B, S, E), dtype=jnp.float32), 'Wq': jax.random.normal(ks[1], (D, D), dtype=jnp.float32) * scale_p, 'Wk': jax.random.normal(ks[2], (D, D), dtype=jnp.float32) * scale_p, 'Wv': jax.random.normal(ks[3], (D, D), dtype=jnp.float32) * scale_p, 'W_out': jax.random.normal(ks[4], (E, E), dtype=jnp.float32) * (1.0 / math.sqrt(E)), 'b_out': jnp.zeros((E,), dtype=jnp.float32)}
    _L2_attn_all = _L2_attn_setup()
    _L2_attn_in = {k: v for k, v in _L2_attn_all.items() if k in ('Wq', 'Wk', 'Wv', 'W_out', 'b_out')}
    del _L2_attn_all

    def _L2_xattn_setup():
        import jax, jax.numpy as jnp
        import numpy as np
        H = 8
        QK_DIM = 64
        HEAD_QK = QK_DIM // H
        TEMP = 1.0
        key = jax.random.key(seed)
        ks = jax.random.split(key, 6)
        B, Tq, Tk, D = (4, 512, 512, 256)
        w_scale = 1.0 / np.sqrt(D)
        return {'Q': jax.random.normal(ks[0], (B, Tq, D), jnp.float32), 'K': jax.random.normal(ks[1], (B, Tk, D), jnp.float32), 'V': jax.random.normal(ks[2], (B, Tk, D), jnp.float32), 'Wq': jax.random.normal(ks[3], (D, QK_DIM), jnp.float32) * w_scale, 'bq': jnp.zeros((QK_DIM,), jnp.float32), 'Wk': jax.random.normal(ks[4], (D, QK_DIM), jnp.float32) * w_scale, 'bk': jnp.zeros((QK_DIM,), jnp.float32), 'key_padding_mask': jnp.zeros((B, Tk), dtype=bool)}
    _L2_xattn_all = _L2_xattn_setup()
    _L2_xattn_in = {k: v for k, v in _L2_xattn_all.items() if k in ('Wq', 'bq', 'Wk', 'bk')}
    del _L2_xattn_all

    def _L2_ffn_setup():
        import jax, jax.numpy as jnp
        import numpy as np
        B, S, D, E, H, K = (4, 512, 256, 8, 128, 2)
        key = jax.random.key(seed)
        ks = jax.random.split(key, 11)
        sc = 0.02
        return {'x': jax.random.normal(ks[0], (B, S, D), dtype=jnp.float32), 'gate_W': jax.random.normal(ks[1], (D, E), dtype=jnp.float32) * sc, 'W1': jax.random.normal(ks[2], (E, D, H), dtype=jnp.float32) * sc, 'b1': jnp.zeros((E, H), dtype=jnp.float32), 'W2': jax.random.normal(ks[3], (E, H, D), dtype=jnp.float32) * sc, 'b2': jnp.zeros((E, D), dtype=jnp.float32), 'Ws1': jax.random.normal(ks[4], (D, H), dtype=jnp.float32) * sc, 'bs1': jnp.zeros((H,), dtype=jnp.float32), 'Ws2': jax.random.normal(ks[5], (H, D), dtype=jnp.float32) * sc, 'bs2': jnp.zeros((D,), dtype=jnp.float32), 'route_scale': jnp.ones((), dtype=jnp.float32)}
    _L2_ffn_all = _L2_ffn_setup()
    _L2_ffn_in = {k: v for k, v in _L2_ffn_all.items() if k in ('gate_W', 'W1', 'b1', 'W2', 'b2', 'Ws1', 'bs1', 'Ws2', 'bs2', 'route_scale')}
    del _L2_ffn_all

    def _L3_attn_setup():
        import jax, jax.numpy as jnp
        import numpy as np
        D_MODEL = 256
        NHEAD = 16
        HEAD_DIM = D_MODEL // NHEAD
        WINDOW = 64

        def _sliding_window_mask(seq_len):
            pos = jnp.arange(seq_len)
            qpos = pos[:, None]
            kpos = pos[None, :]
            valid = (kpos >= qpos - WINDOW + 1) & (kpos <= qpos)
            return jnp.where(valid, 0.0, -jnp.inf).astype(jnp.float32)
        key = jax.random.key(seed)
        kx, kq, kk, kv, ko = jax.random.split(key, 5)
        B, S = (2, 512)
        scale = 1.0 / np.sqrt(D_MODEL)
        x = jax.random.normal(kx, (B, S, D_MODEL), dtype=jnp.float32)
        Wq = jax.random.normal(kq, (D_MODEL, D_MODEL), dtype=jnp.float32) * scale
        Wk = jax.random.normal(kk, (D_MODEL, D_MODEL), dtype=jnp.float32) * scale
        Wv = jax.random.normal(kv, (D_MODEL, D_MODEL), dtype=jnp.float32) * scale
        Wo = jax.random.normal(ko, (D_MODEL, D_MODEL), dtype=jnp.float32) * scale
        return {'x': x, 'Wq': Wq, 'Wk': Wk, 'Wv': Wv, 'Wo': Wo}
    _L3_attn_all = _L3_attn_setup()
    _L3_attn_in = {k: v for k, v in _L3_attn_all.items() if k in ('Wq', 'Wk', 'Wv', 'Wo')}
    del _L3_attn_all

    def _L3_xattn_setup():
        import jax, jax.numpy as jnp
        import numpy as np
        B, S, D, H = (4, 512, 256, 16)
        HD = D // H
        SCALE = 1.0 / np.sqrt(HD)
        NEG = -1000000000.0

        def _split_heads(x):
            b, s, _ = x.shape
            return x.reshape(b, s, H, HD).transpose(0, 2, 1, 3)
        key = jax.random.key(seed)
        ks = jax.random.split(key, 8)
        return {'query': jax.random.normal(ks[0], (B, S, D), jnp.float32), 'key': jax.random.normal(ks[1], (B, S, D), jnp.float32), 'value': jax.random.normal(ks[2], (B, S, D), jnp.float32), 'mask': jax.random.randint(ks[3], (B, 1, S, S), 0, 2, jnp.int32), 'Wq': jax.random.normal(ks[4], (D, D), jnp.float32) * 0.02, 'Wk': jax.random.normal(ks[5], (D, D), jnp.float32) * 0.02, 'Wv': jax.random.normal(ks[6], (D, D), jnp.float32) * 0.02, 'Wo': jax.random.normal(ks[7], (D, D), jnp.float32) * 0.02}
    _L3_xattn_all = _L3_xattn_setup()
    _L3_xattn_in = {k: v for k, v in _L3_xattn_all.items() if k in ('Wq', 'Wk', 'Wv', 'Wo')}
    del _L3_xattn_all

    def _L3_ffn_setup():
        import jax, jax.numpy as jnp
        import numpy as np
        E = 16
        K = 4
        B, S, H, I = (4, 256, 256, 512)
        key = jax.random.key(seed)
        k0, k1, k2, k3 = jax.random.split(key, 4)
        scale = 0.02
        return {'hidden_states': jax.random.normal(k0, (B, S, H), jnp.float32), 'router_w': jax.random.normal(k1, (H, E), jnp.float32) * scale, 'router_b': jnp.zeros((E,), jnp.float32), 'w1': jax.random.normal(k2, (E, H, I), jnp.float32) * scale, 'b1': jnp.zeros((E, I), jnp.float32), 'w2': jax.random.normal(k3, (E, I, H), jnp.float32) * scale, 'b2': jnp.zeros((E, H), jnp.float32)}
    _L3_ffn_all = _L3_ffn_setup()
    _L3_ffn_in = {k: v for k, v in _L3_ffn_all.items() if k in ('router_w', 'router_b', 'w1', 'b1', 'w2', 'b2')}
    del _L3_ffn_all
    return {'x': x, 'ctx_1024': ctx_1024, 'mask_S2_ik0': mask_S2_ik0, 'mask_BxS2_bf0': mask_BxS2_bf0, 'mask_Bx1xSxS2_ik1': mask_Bx1xSxS2_ik1, 'L0_attn_w_i': _L0_attn_in['w_i'], 'L0_attn_w_f': _L0_attn_in['w_f'], 'L0_attn_w_h': _L0_attn_in['w_h'], 'L0_xattn_qkv_w': _L0_xattn_in['qkv_w'], 'L0_xattn_proj_w': _L0_xattn_in['proj_w'], 'L0_xattn_proj_b': _L0_xattn_in['proj_b'], 'L0_ffn_W_exp': _L0_ffn_in['W_exp'], 'L0_ffn_b_exp': _L0_ffn_in['b_exp'], 'L0_ffn_up_weights': _L0_ffn_in['up_weights'], 'L0_ffn_up_bias': _L0_ffn_in['up_bias'], 'L0_ffn_down_weights': _L0_ffn_in['down_weights'], 'L0_ffn_W_con': _L0_ffn_in['W_con'], 'L0_ffn_b_con': _L0_ffn_in['b_con'], 'L0_ffn_down_bias': _L0_ffn_in['down_bias'], 'L1_attn_Wq': _L1_attn_in['Wq'], 'L1_attn_bq': _L1_attn_in['bq'], 'L1_attn_Wk': _L1_attn_in['Wk'], 'L1_attn_bk': _L1_attn_in['bk'], 'L1_attn_Wv': _L1_attn_in['Wv'], 'L1_attn_bv': _L1_attn_in['bv'], 'L1_attn_Wo': _L1_attn_in['Wo'], 'L1_attn_bo': _L1_attn_in['bo'], 'L1_xattn_Wq': _L1_xattn_in['Wq'], 'L1_xattn_Wk': _L1_xattn_in['Wk'], 'L1_xattn_Wv': _L1_xattn_in['Wv'], 'L1_xattn_Wo': _L1_xattn_in['Wo'], 'L1_ffn_Wr': _L1_ffn_in['Wr'], 'L1_ffn_Wg': _L1_ffn_in['Wg'], 'L1_ffn_Wu': _L1_ffn_in['Wu'], 'L1_ffn_Wd': _L1_ffn_in['Wd'], 'L1_ffn_Sg': _L1_ffn_in['Sg'], 'L1_ffn_Su': _L1_ffn_in['Su'], 'L1_ffn_Sd': _L1_ffn_in['Sd'], 'L2_attn_Wq': _L2_attn_in['Wq'], 'L2_attn_Wk': _L2_attn_in['Wk'], 'L2_attn_Wv': _L2_attn_in['Wv'], 'L2_attn_W_out': _L2_attn_in['W_out'], 'L2_attn_b_out': _L2_attn_in['b_out'], 'L2_xattn_Wq': _L2_xattn_in['Wq'], 'L2_xattn_bq': _L2_xattn_in['bq'], 'L2_xattn_Wk': _L2_xattn_in['Wk'], 'L2_xattn_bk': _L2_xattn_in['bk'], 'L2_ffn_gate_W': _L2_ffn_in['gate_W'], 'L2_ffn_W1': _L2_ffn_in['W1'], 'L2_ffn_b1': _L2_ffn_in['b1'], 'L2_ffn_W2': _L2_ffn_in['W2'], 'L2_ffn_b2': _L2_ffn_in['b2'], 'L2_ffn_Ws1': _L2_ffn_in['Ws1'], 'L2_ffn_bs1': _L2_ffn_in['bs1'], 'L2_ffn_Ws2': _L2_ffn_in['Ws2'], 'L2_ffn_bs2': _L2_ffn_in['bs2'], 'L2_ffn_route_scale': _L2_ffn_in['route_scale'], 'L3_attn_Wq': _L3_attn_in['Wq'], 'L3_attn_Wk': _L3_attn_in['Wk'], 'L3_attn_Wv': _L3_attn_in['Wv'], 'L3_attn_Wo': _L3_attn_in['Wo'], 'L3_xattn_Wq': _L3_xattn_in['Wq'], 'L3_xattn_Wk': _L3_xattn_in['Wk'], 'L3_xattn_Wv': _L3_xattn_in['Wv'], 'L3_xattn_Wo': _L3_xattn_in['Wo'], 'L3_ffn_router_w': _L3_ffn_in['router_w'], 'L3_ffn_router_b': _L3_ffn_in['router_b'], 'L3_ffn_w1': _L3_ffn_in['w1'], 'L3_ffn_b1': _L3_ffn_in['b1'], 'L3_ffn_w2': _L3_ffn_in['w2'], 'L3_ffn_b2': _L3_ffn_in['b2']}

def reference(x, ctx_1024, mask_S2_ik0, mask_BxS2_bf0, mask_Bx1xSxS2_ik1, L0_attn_w_i, L0_attn_w_f, L0_attn_w_h, L0_xattn_qkv_w, L0_xattn_proj_w, L0_xattn_proj_b, L0_ffn_W_exp, L0_ffn_b_exp, L0_ffn_up_weights, L0_ffn_up_bias, L0_ffn_down_weights, L0_ffn_W_con, L0_ffn_b_con, L0_ffn_down_bias, L1_attn_Wq, L1_attn_bq, L1_attn_Wk, L1_attn_bk, L1_attn_Wv, L1_attn_bv, L1_attn_Wo, L1_attn_bo, L1_xattn_Wq, L1_xattn_Wk, L1_xattn_Wv, L1_xattn_Wo, L1_ffn_Wr, L1_ffn_Wg, L1_ffn_Wu, L1_ffn_Wd, L1_ffn_Sg, L1_ffn_Su, L1_ffn_Sd, L2_attn_Wq, L2_attn_Wk, L2_attn_Wv, L2_attn_W_out, L2_attn_b_out, L2_xattn_Wq, L2_xattn_bq, L2_xattn_Wk, L2_xattn_bk, L2_ffn_gate_W, L2_ffn_W1, L2_ffn_b1, L2_ffn_W2, L2_ffn_b2, L2_ffn_Ws1, L2_ffn_bs1, L2_ffn_Ws2, L2_ffn_bs2, L2_ffn_route_scale, L3_attn_Wq, L3_attn_Wk, L3_attn_Wv, L3_attn_Wo, L3_xattn_Wq, L3_xattn_Wk, L3_xattn_Wv, L3_xattn_Wo, L3_ffn_router_w, L3_ffn_router_b, L3_ffn_w1, L3_ffn_b1, L3_ffn_w2, L3_ffn_b2):
    import jax
    import jax.numpy as jnp

    def _L0_attn_ref(x_t, w_i, w_f, w_h):
        import jax, jax.numpy as jnp
        import numpy as np
        B, S, D = (4, 2048, 256)

        def log_g(x):
            return jnp.where(x >= 0, jnp.log(jax.nn.relu(x) + 0.5), -jax.nn.softplus(-x))

        def parallel_scan_log(log_coeffs, log_values):
            a_star = jnp.cumsum(log_coeffs, axis=1)
            log_h = a_star + jax.lax.cumlogsumexp(log_values - a_star, axis=1)
            return jnp.exp(log_h)
        f_gate = x_t * w_f
        i_gate = x_t * w_i
        hidden = x_t * w_h
        diff = jax.nn.softplus(-f_gate) - jax.nn.softplus(-i_gate)
        log_f = -jax.nn.softplus(diff)
        log_i = -jax.nn.softplus(-diff)
        log_values = log_i + log_g(hidden)
        h_t = parallel_scan_log(log_f, log_values)
        return h_t

    def _L0_xattn_ref(x, support, attn_mask, qkv_w, proj_w, proj_b):
        import jax, jax.numpy as jnp
        import numpy as np
        DIM = 256
        NUM_HEADS = 8
        SCALE = (DIM // NUM_HEADS) ** (-0.5)
        B, N, C = x.shape
        wq, wk, wv = (qkv_w[:C], qkv_w[C:2 * C], qkv_w[2 * C:])
        q = jnp.einsum('bnc,dc->bnd', x, wq)
        k = jnp.einsum('bmc,dc->bmd', support, wk)
        v = jnp.einsum('bmc,dc->bmd', support, wv)
        attn = jnp.einsum('bnd,bmd->bnm', q, k) * SCALE
        attn = jax.nn.softmax(attn, axis=-1)
        attn = jnp.where(attn_mask[None, None, :] == 0, 0.0, attn)
        out = jnp.einsum('bnm,bmd->bnd', attn, v)
        out = jnp.swapaxes(out, 1, 2).reshape(B, N, C)
        out = jnp.einsum('bnc,dc->bnd', out, proj_w) + proj_b
        return out

    def _L0_ffn_ref(x, W_exp, b_exp, up_weights, up_bias, down_weights, W_con, b_con, down_bias):
        import jax, jax.numpy as jnp
        import numpy as np
        D_MODEL = 256
        EXPANSION = 4
        D_HIDDEN = D_MODEL * EXPANSION
        NUM_STAGES = int(np.log2(D_HIDDEN))

        def butterfly(y, weights, dim):
            lead = y.shape[:-1]
            for stage in range(weights.shape[0]):
                s = 2 ** stage
                nb = dim // (2 * s)
                yr = y.reshape(*lead, nb, 2, s)
                a = yr[..., 0, :]
                b = yr[..., 1, :]
                w = weights[stage].reshape(nb, s, 2, 2)
                na = w[..., 0, 0] * a + w[..., 0, 1] * b
                nb2 = w[..., 1, 0] * a + w[..., 1, 1] * b
                y = jnp.stack([na, nb2], axis=-2).reshape(*lead, dim)
            return y
        h = jnp.einsum('bsd,dh->bsh', x, W_exp) + b_exp
        h = butterfly(h, up_weights, D_HIDDEN)
        h = jax.nn.gelu(h + up_bias, approximate=False)
        h = butterfly(h, down_weights, D_HIDDEN)
        y = jnp.einsum('bsh,hd->bsd', h, W_con) + b_con
        return y + down_bias

    def _L1_attn_ref(x, Wq, bq, Wk, bk, Wv, bv, Wo, bo):
        import jax, jax.numpy as jnp
        import numpy as np
        import math
        DIM = 256
        NUM_HEADS = 16
        HEAD_DIM = DIM // NUM_HEADS
        B, S = (2, 512)
        b, s, d = x.shape
        h, hd = (NUM_HEADS, HEAD_DIM)

        def split_heads(t):
            return t.reshape(b, s, h, hd).transpose(0, 2, 1, 3)
        q = split_heads(x @ Wq + bq)
        k = split_heads(x @ Wk + bk)
        v = split_heads(x @ Wv + bv)
        scores = jnp.einsum('bhqd,bhkd->bhqk', q, k) / math.sqrt(hd)
        causal = jnp.tril(jnp.ones((s, s), dtype=bool))
        scores = jnp.where(causal[None, None], scores, jnp.asarray(-10000.0, scores.dtype))
        probs = jax.nn.softmax(scores, axis=-1)
        ctx = jnp.einsum('bhqk,bhkd->bhqd', probs, v)
        ctx = ctx.transpose(0, 2, 1, 3).reshape(b, s, d)
        return ctx @ Wo + bo

    def _L1_xattn_ref(query, key, value, Wq, Wk, Wv, Wo):
        import jax, jax.numpy as jnp
        import numpy as np
        B, S, D, H = (2, 512, 256, 16)
        HD = D // H
        SCALE = HD ** (-0.5)
        NEG = -1000000000.0
        b, sq, d = query.shape
        sk = key.shape[1]
        q = (query @ Wq.T).reshape(b, sq, H, HD).transpose(0, 2, 1, 3)
        k = (key @ Wk.T).reshape(b, sk, H, HD).transpose(0, 2, 1, 3)
        v = (value @ Wv.T).reshape(b, sk, H, HD).transpose(0, 2, 1, 3)
        scores = jnp.einsum('bhqd,bhkd->bhqk', q, k) * SCALE
        causal = jnp.arange(sq)[:, None] >= jnp.arange(sk)[None, :]
        scores = jnp.where(causal[None, None], scores, NEG)
        attn = jax.nn.softmax(scores, axis=-1)
        out = jnp.einsum('bhqk,bhkd->bhqd', attn, v)
        out = out.transpose(0, 2, 1, 3).reshape(b, sq, d)
        return out @ Wo.T

    def _L1_ffn_ref(x, Wr, Wg, Wu, Wd, Sg, Su, Sd):
        import jax, jax.numpy as jnp
        import numpy as np
        TOP_K = 2
        EPS = 1e-20
        B, S, H = x.shape
        T = B * S
        xt = x.reshape(T, H)
        scores = jax.nn.softmax(xt @ Wr, axis=-1)
        topk_w, topk_idx = jax.lax.top_k(scores, TOP_K)
        topk_w = topk_w / (topk_w.sum(axis=-1, keepdims=True) + EPS)
        g = jax.nn.silu(jnp.einsum('th,ehd->etd', xt, Wg))
        u = jnp.einsum('th,ehd->etd', xt, Wu)
        out_all = jnp.einsum('etd,edh->eth', g * u, Wd)
        tok = jnp.arange(T)[:, None]
        gathered = out_all[topk_idx, tok, :]
        out = jnp.sum(gathered * topk_w[..., None], axis=1).reshape(B, S, H)
        shared = jax.nn.silu(x @ Sg) * (x @ Su) @ Sd
        return out + shared

    def _L2_attn_ref(x, Wq, Wk, Wv, W_out, b_out):
        import jax, jax.numpy as jnp
        import numpy as np
        import math
        B, S, E, H = (2, 512, 256, 16)
        D = E // H
        b, s, e = x.shape
        xh = x.reshape(b, s, H, D)
        q = jnp.einsum('bshd,ed->bshe', xh, Wq)
        k = jnp.einsum('bshd,ed->bshe', xh, Wk)
        v = jnp.einsum('bshd,ed->bshe', xh, Wv)
        energy = jnp.einsum('bqhd,bkhd->bhqk', q, k) / jnp.sqrt(jnp.float32(e))
        attn = jax.nn.softmax(energy, axis=-1)
        out = jnp.einsum('bhqk,bkhd->bqhd', attn, v).reshape(b, s, e)
        return out @ W_out.T + b_out

    def _L2_xattn_ref(Q, K, V, Wq, bq, Wk, bk, key_padding_mask):
        import jax, jax.numpy as jnp
        import numpy as np
        H = 8
        QK_DIM = 64
        HEAD_QK = QK_DIM // H
        TEMP = 1.0
        B, Tq, D = Q.shape
        Tk = K.shape[1]
        head_v = D // H
        q = (Q @ Wq + bq).reshape(B, Tq, H, HEAD_QK)
        k = (K @ Wk + bk).reshape(B, Tk, H, HEAD_QK)
        v = V.reshape(B, Tk, H, head_v)
        scale = np.sqrt(HEAD_QK) * TEMP
        scores = jnp.einsum('bqhd,bkhd->bhqk', q, k) / scale
        neg_inf = jnp.float32(-jnp.inf)
        scores = jnp.where(jnp.isnan(scores), neg_inf, scores)
        scores = jnp.where(key_padding_mask[:, None, None, :], neg_inf, scores)
        attn = jax.nn.softmax(scores, axis=-1)
        out = jnp.einsum('bhqk,bkhd->bqhd', attn, v).reshape(B, Tq, D)
        return out

    def _L2_ffn_ref(x, gate_W, W1, b1, W2, b2, Ws1, bs1, Ws2, bs2, route_scale):
        import jax, jax.numpy as jnp
        import numpy as np
        B, S, D, E, H, K = (4, 512, 256, 8, 128, 2)
        scores = jax.nn.sigmoid(x @ gate_W) * route_scale
        topk_scores, topk_idx = jax.lax.top_k(scores, K)
        topk_w = topk_scores / topk_scores.sum(-1, keepdims=True)
        onehot = jax.nn.one_hot(topk_idx, E, dtype=x.dtype)
        gate_full = jnp.einsum('bsk,bske->bse', topk_w, onehot)
        h = jax.nn.gelu(jnp.einsum('bsd,edh->bseh', x, W1) + b1, approximate=False)
        y = jnp.einsum('bseh,ehd->bsed', h, W2) + b2
        expert_out = jnp.einsum('bse,bsed->bsd', gate_full, y)
        shared = jax.nn.gelu(x @ Ws1 + bs1, approximate=False) @ Ws2 + bs2
        return expert_out + shared

    def _L3_attn_ref(x, Wq, Wk, Wv, Wo):
        import jax, jax.numpy as jnp
        import numpy as np
        D_MODEL = 256
        NHEAD = 16
        HEAD_DIM = D_MODEL // NHEAD
        WINDOW = 64

        def _sliding_window_mask(seq_len):
            pos = jnp.arange(seq_len)
            qpos = pos[:, None]
            kpos = pos[None, :]
            valid = (kpos >= qpos - WINDOW + 1) & (kpos <= qpos)
            return jnp.where(valid, 0.0, -jnp.inf).astype(jnp.float32)
        B, S, D = x.shape
        q = jnp.einsum('bsd,ed->bse', x, Wq)
        k = jnp.einsum('bsd,ed->bse', x, Wk)
        v = jnp.einsum('bsd,ed->bse', x, Wv)
        q = q.reshape(B, S, NHEAD, HEAD_DIM).transpose(0, 2, 1, 3)
        k = k.reshape(B, S, NHEAD, HEAD_DIM).transpose(0, 2, 1, 3)
        v = v.reshape(B, S, NHEAD, HEAD_DIM).transpose(0, 2, 1, 3)
        mask = _sliding_window_mask(S)
        scale = 1.0 / np.sqrt(HEAD_DIM)
        scores = jnp.einsum('bhqd,bhkd->bhqk', q, k) * scale + mask
        attn = jax.nn.softmax(scores, axis=-1)
        out = jnp.einsum('bhqk,bhkd->bhqd', attn, v)
        out = out.transpose(0, 2, 1, 3).reshape(B, S, D)
        return jnp.einsum('bsd,ed->bse', out, Wo)

    def _L3_xattn_ref(query, key, value, mask, Wq, Wk, Wv, Wo):
        import jax, jax.numpy as jnp
        import numpy as np
        B, S, D, H = (4, 512, 256, 16)
        HD = D // H
        SCALE = 1.0 / np.sqrt(HD)
        NEG = -1000000000.0

        def _split_heads(x):
            b, s, _ = x.shape
            return x.reshape(b, s, H, HD).transpose(0, 2, 1, 3)
        q = _split_heads(query @ Wq.T)
        k = _split_heads(key @ Wk.T)
        v = _split_heads(value @ Wv.T)
        scores = jnp.einsum('bhqd,bhkd->bhqk', q, k) * SCALE
        scores = jnp.where(mask == 0, NEG, scores)
        probs = jax.nn.softmax(scores, axis=-1)
        attn = jnp.einsum('bhqk,bhkd->bhqd', probs, v)
        attn = attn.transpose(0, 2, 1, 3).reshape(query.shape[0], query.shape[1], D)
        return attn @ Wo.T

    def _L3_ffn_ref(hidden_states, router_w, router_b, w1, b1, w2, b2):
        import jax, jax.numpy as jnp
        import numpy as np
        E = 16
        K = 4
        B, S, H, I = (4, 256, 256, 512)
        b, s, h = hidden_states.shape
        logits = hidden_states @ router_w + router_b
        probs = jax.nn.softmax(logits, axis=-1)
        topw, topi = jax.lax.top_k(probs, K)
        topw = topw / jnp.sum(topw, axis=-1, keepdims=True)
        combine = jnp.sum(jax.nn.one_hot(topi, E, dtype=hidden_states.dtype) * topw[..., None], axis=2)
        x = hidden_states.reshape(b * s, h)
        c = combine.reshape(b * s, E)

        def body(acc, expert):
            w1e, b1e, w2e, b2e, ce = expert
            hmid = jax.nn.gelu(x @ w1e + b1e, approximate=False)
            return (acc + (hmid @ w2e + b2e) * ce[:, None], None)
        out, _ = jax.lax.scan(body, jnp.zeros_like(x), (w1, b1, w2, b2, c.T))
        return out.reshape(b, s, h)
    x = _layernorm(x + _L0_attn_ref(x, L0_attn_w_i, L0_attn_w_f, L0_attn_w_h), axis=-1)
    x = _layernorm(x + _L0_xattn_ref(x, ctx_1024, mask_S2_ik0, L0_xattn_qkv_w, L0_xattn_proj_w, L0_xattn_proj_b), axis=-1)
    x = _layernorm(x + _L0_ffn_ref(x, L0_ffn_W_exp, L0_ffn_b_exp, L0_ffn_up_weights, L0_ffn_up_bias, L0_ffn_down_weights, L0_ffn_W_con, L0_ffn_b_con, L0_ffn_down_bias), axis=-1)
    x = _layernorm(x + _L1_attn_ref(x, L1_attn_Wq, L1_attn_bq, L1_attn_Wk, L1_attn_bk, L1_attn_Wv, L1_attn_bv, L1_attn_Wo, L1_attn_bo), axis=-1)
    x = _layernorm(x + _L1_xattn_ref(x, ctx_1024, ctx_1024, L1_xattn_Wq, L1_xattn_Wk, L1_xattn_Wv, L1_xattn_Wo), axis=-1)
    x = _layernorm(x + _L1_ffn_ref(x, L1_ffn_Wr, L1_ffn_Wg, L1_ffn_Wu, L1_ffn_Wd, L1_ffn_Sg, L1_ffn_Su, L1_ffn_Sd), axis=-1)
    x = _layernorm(x + _L2_attn_ref(x, L2_attn_Wq, L2_attn_Wk, L2_attn_Wv, L2_attn_W_out, L2_attn_b_out), axis=-1)
    x = _layernorm(x + _L2_xattn_ref(x, ctx_1024, ctx_1024, L2_xattn_Wq, L2_xattn_bq, L2_xattn_Wk, L2_xattn_bk, mask_BxS2_bf0), axis=-1)
    x = _layernorm(x + _L2_ffn_ref(x, L2_ffn_gate_W, L2_ffn_W1, L2_ffn_b1, L2_ffn_W2, L2_ffn_b2, L2_ffn_Ws1, L2_ffn_bs1, L2_ffn_Ws2, L2_ffn_bs2, L2_ffn_route_scale), axis=-1)
    x = _layernorm(x + _L3_attn_ref(x, L3_attn_Wq, L3_attn_Wk, L3_attn_Wv, L3_attn_Wo), axis=-1)
    x = _layernorm(x + _L3_xattn_ref(x, ctx_1024, ctx_1024, mask_Bx1xSxS2_ik1, L3_xattn_Wq, L3_xattn_Wk, L3_xattn_Wv, L3_xattn_Wo), axis=-1)
    x = _layernorm(x + _L3_ffn_ref(x, L3_ffn_router_w, L3_ffn_router_b, L3_ffn_w1, L3_ffn_b1, L3_ffn_w2, L3_ffn_b2), axis=-1)
    return x

_drawn_inputs = setup_inputs


def setup_inputs(seed=0):
    import zlib

    import numpy as np

    out = dict(_drawn_inputs(seed))
    spreads = {'L0_ffn_b_exp': (0.0, 0.1),
     'L0_ffn_up_bias': (0.0, 0.1),
     'L0_ffn_b_con': (0.0, 0.1),
     'L0_ffn_down_bias': (0.0, 0.1),
     'L2_attn_b_out': (0.0, 0.1),
     'L2_xattn_bq': (0.0, 0.329),
     'L2_xattn_bk': (0.0, 0.8),
     'L2_ffn_b1': (0.0, 0.8),
     'L2_ffn_b2': (0.0, 0.1),
     'L2_ffn_bs1': (0.0, 0.507),
     'L2_ffn_bs2': (0.0, 0.1),
     'L3_ffn_router_b': (0.0, 0.32),
     'L3_ffn_b1': (0.0, 0.598),
     'L3_ffn_b2': (0.0, 0.1)}
    factors = {'L0_attn_w_i': 8.0,
     'L0_attn_w_f': 8.0,
     'L0_xattn_proj_b': 4.015,
     'L1_attn_Wq': 8.0,
     'L1_attn_bq': 8.0,
     'L1_attn_Wk': 8.0,
     'L1_attn_bk': 8.0,
     'L1_attn_Wv': 2.733,
     'L1_attn_bv': 5.234,
     'L1_ffn_Wr': 4.425,
     'L1_ffn_Wg': 3.793,
     'L1_ffn_Wu': 3.748,
     'L1_ffn_Wd': 3.882,
     'L1_ffn_Sg': 2.75,
     'L1_ffn_Su': 2.689,
     'L3_xattn_Wq': 8.0,
     'L3_xattn_Wk': 8.0}
    for name, (base, spread) in spreads.items():
        noise = np.random.default_rng([zlib.crc32(name.encode()), seed]).standard_normal(out[name].shape)
        drawn = base * np.exp(spread * noise) if base else spread * noise
        out[name] = jnp.asarray(drawn.astype(out[name].dtype))
    for name, factor in factors.items():
        out[name] = (out[name] * factor).astype(out[name].dtype)
    return out
```

```python
from contextlib import ExitStack

import concourse.bass as bass
from concourse import mybir

F32 = mybir.dt.float32
F32R = mybir.dt.float32r
BF16 = mybir.dt.bfloat16
I32 = mybir.dt.int32
U8 = mybir.dt.uint8
ALU = mybir.AluOpType
ACT = mybir.ActivationFunctionType
AX = mybir.AxisListType

P = 128
D = 256
KT = D // P
NB = 2
S = 1024
T = NB * S
NT = T // P
CH = 512
NCH = T // CH
M = 77
H = 16
HD = D // H
HU = 4
NU = H // HU
WIN = 64
WINQ = P + WIN
EPS = 1e-5
MASKED = -1e30
NEG = -1e9
STACK = 4 * HD
STAGES = 12
TAGS = []


def tag():
    TAGS.append(0)
    return len(TAGS)


def named(**items):
    return type("Named", (), items)


def sems(nc, names):
    return named(**{n: nc.alloc_semaphore(f"{n}_{tag()}") for n in names.split()})


def sbuf(nc, st, name, shape, dt=F32):
    return st.enter_context(nc.sbuf_tensor(f"{name}_{tag()}", shape, dt))


def psum(nc, st, name, shape, dt=F32):
    return st.enter_context(nc.psum_tensor(f"{name}_{tag()}", shape, dt))


def over(ap, n):
    return ap.unsqueeze(1).broadcast_to([ap.shape[0], n, ap.shape[1]])


def last(ap, n):
    return ap.unsqueeze(2).broadcast_to([ap.shape[0], ap.shape[1], n])


def setup(nc, env, dram):
    with ExitStack() as st:
        s = sems(nc, "loaded cleared shaped")
        block = st.enter_context(nc.Block())

        @block.sync
        def _(sp):
            sp.dma_start(env.xT[:, :, :], dram.xT.rearrange("(k p) t -> p k t", p=P)).then_inc(s.loaded, 16)
            sp.dma_start(env.ctxT[:, :, :], dram.ctxT.rearrange("(k p) t -> p k t", p=P)).then_inc(s.loaded, 16)
            sp.wait_ge(s.loaded, 32)

        @block.gpsimd
        def _(pool):
            tiles = (env.ident, env.identb, env.causal_qk, env.causal_kq, env.window_qk, env.window_kq)
            for t in tiles:
                pool.memset(t[:, :], 0.0).then_inc(s.cleared, 1)
            pool.memset(env.avg[:, :], 1.0 / D).then_inc(s.cleared, 1)
            pool.memset(env.eps[:, :], EPS).then_inc(s.cleared, 1)
            pool.memset(env.ones[:, :], 1.0).then_inc(s.cleared, 1)
            pool.wait_ge(s.cleared, len(tiles) + 3)
            for t in (env.ident, env.identb):
                pool.affine_select(out=t[:, :], in_=t[:, :], compare_op=ALU.not_equal, fill=1.0, base=0,
                                   pattern=[[-1, P]], channel_multiplier=1).then_inc(s.shaped, 1)
            pool.affine_select(out=env.causal_qk[:, :], in_=env.causal_qk[:, :], compare_op=ALU.is_ge, fill=MASKED,
                               base=0, pattern=[[-1, P]], channel_multiplier=1).then_inc(s.shaped, 1)
            pool.affine_select(out=env.causal_kq[:, :], in_=env.causal_kq[:, :], compare_op=ALU.is_ge, fill=MASKED,
                               base=0, pattern=[[1, P]], channel_multiplier=-1).then_inc(s.shaped, 1)
            pool.affine_select(out=env.window_qk[:, :], in_=env.window_qk[:, :], compare_op=ALU.is_ge, fill=MASKED,
                               base=-1, pattern=[[1, WINQ]], channel_multiplier=-1).then_inc(s.shaped, 1)
            pool.affine_select(out=env.window_kq[:, :], in_=env.window_kq[:, :], compare_op=ALU.is_ge, fill=MASKED,
                               base=0, pattern=[[1, WINQ]], channel_multiplier=-1).then_inc(s.shaped, 1)
            pool.wait_ge(s.shaped, 6)
            pool.affine_select(out=env.window_qk[:, :], in_=env.window_qk[:, :], compare_op=ALU.is_ge, fill=MASKED,
                               base=WIN, pattern=[[-1, WINQ]], channel_multiplier=1).then_inc(s.shaped, 1)
            pool.affine_select(out=env.window_kq[:, :], in_=env.window_kq[:, :], compare_op=ALU.is_ge, fill=MASKED,
                               base=WIN - 1, pattern=[[-1, WINQ]], channel_multiplier=1).then_inc(s.shaped, 1)


def residual_norm(nc, env, branch_matmuls=None, branch=None, bias=None):
    TC = CH // P
    with ExitStack() as st:
        s = sems(nc, "y_ready summed mean_ready centred squared var_ready rooted inverted spread rstd_ready normed")
        y_ps = psum(nc, st, "y_ps", [P, 2, KT, CH])
        mean_ps = psum(nc, st, "mean_ps", [P, CH])
        var_ps = psum(nc, st, "var_ps", [P, 2, TC])
        rstd_ps = psum(nc, st, "rstd_ps", [P, 2, CH])
        dev = sbuf(nc, st, "dev", [P, NCH, KT, CH])
        sq = sbuf(nc, st, "sq", [P, 2, KT, CH])
        std = sbuf(nc, st, "std", [P, NCH, TC])
        rstd = sbuf(nc, st, "rstd", [P, NCH, TC])
        diag = sbuf(nc, st, "diag", [P, 2, TC, P])
        block = st.enter_context(nc.Block())

        @block.tensor
        def _(pe):
            for n in range(NCH + 3):
                if n < NCH and branch_matmuls:
                    if n >= 2:
                        pe.wait_ge(s.summed, n - 1)
                    branch_matmuls(pe, n, y_ps[:, n % 2]).then_inc(s.y_ready, 1)
                if 1 <= n <= NCH:
                    m = n - 1
                    pe.wait_ge(s.summed, m + 1)
                    if m >= 1:
                        pe.wait_ge(s.centred, m)
                    for k in range(KT):
                        mm = pe.matmul(mean_ps[:, :], env.avg[:, :], env.xT[:, k, m * CH:(m + 1) * CH],
                                       start=(k == 0), stop=(k == KT - 1))
                    mm.then_inc(s.mean_ready, 1)
                if 2 <= n <= NCH + 1:
                    m = n - 2
                    pe.wait_ge(s.squared, m + 1)
                    if m >= 1:
                        pe.wait_ge(s.rooted, m)
                    for t in range(TC):
                        for k in range(KT):
                            mm = pe.matmul(var_ps[:, m % 2, t:t + 1], sq[:, m % 2, k, t * P:(t + 1) * P], env.avg[:, 0:1],
                                           start=(k == 0), stop=(k == KT - 1))
                    mm.then_inc(s.var_ready, 1)
                if n >= 3:
                    m = n - 3
                    pe.wait_ge(s.spread, TC * (m + 1))
                    if m >= 2:
                        pe.wait_ge(s.normed, m - 1)
                    for t in range(TC):
                        mm = pe.matmul(rstd_ps[:, m % 2, t * P:(t + 1) * P], env.ones[:, :], diag[:, m % 2, t, :],
                                       start=True, stop=True)
                    mm.then_inc(s.rstd_ready, 1)

        @block.scalar
        def _(act):
            for n in range(NCH):
                act.wait_ge(s.centred, n + 1)
                if n >= 2:
                    act.wait_ge(s.var_ready, n - 1)
                act.activation(sq[:, n % 2], dev[:, n], ACT.Square).then_inc(s.squared, 1)
                act.wait_ge(s.var_ready, n + 1)
                act.activation(std[:, n, :], var_ps[:, n % 2, :], ACT.Sqrt, bias=env.eps[:, 0:1]).then_inc(s.rooted, 1)

        @block.gpsimd
        def _(pool):
            for n in range(NCH):
                pool.wait_ge(s.inverted, n + 1)
                if n >= 2:
                    pool.wait_ge(s.rstd_ready, n - 1)
                for t in range(TC):
                    pool.tensor_scalar(diag[:, n % 2, t, :], env.ident[:, :], rstd[:, n, t:t + 1], None, ALU.mult)\
                        .then_inc(s.spread, 1)

        @block.vector
        def _(dve):
            for n in range(NCH + 3):
                if n < NCH:
                    x = env.xT[:, :, n * CH:(n + 1) * CH]
                    if branch_matmuls:
                        dve.wait_ge(s.y_ready, n + 1)
                        y = y_ps[:, n % 2]
                    else:
                        y = branch[:, :, n * CH:(n + 1) * CH]
                    if bias is None:
                        dve.tensor_tensor(x, y, x, ALU.add).then_inc(s.summed, 1)
                    else:
                        for k in range(KT):
                            add = dve.scalar_tensor_tensor(out=x[:, k], in0=y[:, k], scalar=bias[:, k:k + 1],
                                                           in1=x[:, k], op0=ALU.add, op1=ALU.add)
                        add.then_inc(s.summed, 1)
                if 1 <= n <= NCH:
                    m = n - 1
                    dve.wait_ge(s.mean_ready, m + 1)
                    dve.tensor_tensor(dev[:, m], env.xT[:, :, m * CH:(m + 1) * CH], over(mean_ps[:, :], KT),
                                      ALU.subtract).then_inc(s.centred, 1)
                if 2 <= n <= NCH + 1:
                    m = n - 2
                    dve.wait_ge(s.rooted, m + 1)
                    dve.reciprocal(rstd[:, m, :], std[:, m, :]).then_inc(s.inverted, 1)
                if n >= 3:
                    m = n - 3
                    dve.wait_ge(s.rstd_ready, m + 1)
                    dve.tensor_tensor(env.xT[:, :, m * CH:(m + 1) * CH], dev[:, m], over(rstd_ps[:, m % 2, :], KT),
                                      ALU.mult).then_inc(s.normed, 1)


def min_gru(nc, env, dram):
    with ExitStack() as st:
        w = {n: sbuf(nc, st, f"w_{n}", [P, KT]) for n in "fih"}
        neg = {n: sbuf(nc, st, f"neg_{n}", [P, KT]) for n in "fi"}
        h_out = sbuf(nc, st, "h_out", [P, KT, T])
        s = sems(nc, "loaded negated abs_done exp_done ln_done relu_done soft_done diff_done gates_done low_done sig_done "
                         "g_done v_done scanned")
        mag = sbuf(nc, st, "mag", [P, 2, 2, S])
        soft = sbuf(nc, st, "soft", [P, 2, 2, S])
        relu = sbuf(nc, st, "relu", [P, 2, 2, S])
        diff = sbuf(nc, st, "diff", [P, 2, S])
        gate = sbuf(nc, st, "gate", [P, 2, 2, S])
        low = sbuf(nc, st, "low", [P, 2, S])
        hid = sbuf(nc, st, "hid", [P, 2, S])
        with nc.Block() as block:
            items = [(k, b) for k in range(KT) for b in range(NB)]

            @block.sync
            def _(sp):
                for n in "fih":
                    sp.dma_start(w[n][:, :], dram["w_" + n]).then_inc(s.loaded, 16)

            @block.scalar
            def _(act):
                act.wait_ge(s.loaded, 48)
                for n, (k, b) in enumerate(items):
                    x = env.xT[:, k, b * S:(b + 1) * S]
                    z = n % 2
                    if n >= 2:
                        act.wait_ge(s.soft_done, 2 * (n - 1))
                    for a, g in enumerate("fi"):
                        act.activation(mag[:, z, a, :], x, ACT.Abs, scale=w[g][:, k:k + 1]).then_inc(s.abs_done, 1)
                    act.wait_ge(s.abs_done, 2 * (n + 1))
                    act.activation(mag[:, z], mag[:, z], ACT.Exp, scale=-1.0).then_inc(s.exp_done, 1)
                    act.wait_ge(s.exp_done, n + 1)
                    act.activation(soft[:, z], mag[:, z], ACT.Ln, bias=1.0).then_inc(s.ln_done, 1)
                for n, (k, b) in enumerate(items):
                    z = n % 2
                    act.wait_ge(s.diff_done, n + 1)
                    if n >= 2:
                        act.wait_ge(s.scanned, n - 1)
                    act.activation(gate[:, z, 0, :], diff[:, z, :], ACT.Sigmoid, scale=-1.0).then_inc(s.gates_done, 1)
                    act.activation(gate[:, z, 1, :], diff[:, z, :], ACT.Sigmoid).then_inc(s.gates_done, 1)
                    act.wait_ge(s.low_done, n + 1)
                    act.activation(low[:, z, :], low[:, z, :], ACT.Sigmoid).then_inc(s.sig_done, 1)

            @block.vector
            def _(dve):
                dve.wait_ge(s.loaded, 48)
                for g in "fi":
                    dve.tensor_scalar(neg[g][:, :], w[g][:, :], -1.0, None, ALU.mult).then_inc(s.negated, 1)
                dve.wait_ge(s.negated, 2)

                def softplus_gap(n):
                    k, b = items[n]
                    z = n % 2
                    x = env.xT[:, k, b * S:(b + 1) * S]
                    for a, g in enumerate("fi"):
                        dve.tensor_scalar(relu[:, z, a, :], x, neg[g][:, k:k + 1], 0.0, ALU.mult, ALU.max)\
                           .then_inc(s.relu_done, 1)
                    dve.wait_ge(s.relu_done, 2 * (n + 1))
                    dve.wait_ge(s.ln_done, n + 1)
                    for a in range(2):
                        dve.tensor_tensor(relu[:, z, a, :], relu[:, z, a, :], soft[:, z, a, :], ALU.add)\
                           .then_inc(s.soft_done, 1)
                    dve.wait_ge(s.soft_done, 2 * (n + 1))
                    if n >= 2:
                        dve.wait_ge(s.gates_done, 2 * (n - 1))
                    dve.tensor_tensor(diff[:, z, :], relu[:, z, 0, :], relu[:, z, 1, :], ALU.subtract)\
                       .then_inc(s.diff_done, 1)

                def hidden(n):
                    k, b = items[n]
                    z = n % 2
                    x = env.xT[:, k, b * S:(b + 1) * S]
                    dve.tensor_scalar(low[:, z, :], x, w["h"][:, k:k + 1], 0.0, ALU.mult, ALU.min).then_inc(s.low_done, 1)
                    dve.tensor_scalar(hid[:, z, :], x, w["h"][:, k:k + 1], 0.0, ALU.mult, ALU.max).then_inc(s.g_done, 1)

                def scan(n):
                    k, b = items[n]
                    z = n % 2
                    dve.wait_ge(s.sig_done, n + 1)
                    dve.wait_ge(s.g_done, 3 * n + 1)
                    dve.tensor_tensor(hid[:, z, :], hid[:, z, :], low[:, z, :], ALU.add).then_inc(s.g_done, 1)
                    dve.wait_ge(s.gates_done, 2 * (n + 1))
                    dve.wait_ge(s.g_done, 3 * n + 2)
                    dve.tensor_tensor(hid[:, z, :], hid[:, z, :], gate[:, z, 1, :], ALU.mult).then_inc(s.g_done, 1)
                    dve.wait_ge(s.g_done, 3 * n + 3)
                    dve.tensor_tensor_scan(h_out[:, k, b * S:(b + 1) * S], gate[:, z, 0, :], hid[:, z, :], 0.0,
                                           ALU.mult, ALU.add).then_inc(s.scanned, 1)

                for n in range(len(items)):
                    if n >= 2:
                        hidden(n - 2)
                    softplus_gap(n) if n < 2 else (scan(n - 2), softplus_gap(n))
                for n in range(len(items) - 2, len(items)):
                    hidden(n)
                    scan(n)
        residual_norm(nc, env, branch=h_out)


def wide_cross(nc, env, dram):
    scale = float(32 ** -0.5)
    NK = NB * M
    HT = NT // NB
    with ExitStack() as st:
        wq = sbuf(nc, st, "wq", [P, KT, D])
        wkT = sbuf(nc, st, "wkT", [P, KT, D])
        wvT = sbuf(nc, st, "wvT", [P, KT, D])
        projT = sbuf(nc, st, "projT", [P, KT, D])
        proj_b = sbuf(nc, st, "proj_b", [P, KT])
        mask_i = sbuf(nc, st, "mask_i", [M, 1], I32)
        keep = sbuf(nc, st, "keep", [M, 1])
        keyT = sbuf(nc, st, "keyT", [P, KT, NK])
        qkT = sbuf(nc, st, "qkT", [P, KT, NK])
        v = sbuf(nc, st, "v", [M, NB, D])
        sc = sbuf(nc, st, "sc", [P, HT, M])
        rowmax = sbuf(nc, st, "rowmax", [P, NB, HT])
        rowsum = sbuf(nc, st, "rowsum", [P, NB, HT])
        inv = sbuf(nc, st, "inv", [P, NB, HT])
        pr = sbuf(nc, st, "pr", [P, NB, HT, M])
        prT = sbuf(nc, st, "prT", [M, NB, HT, P])
        o = sbuf(nc, st, "o", [P, NT, D])
        with ExitStack() as inner:
            s = sems(nc, "loaded kept key_ready key_kept qk_ready qk_kept v_ready v_kept score_ready max_done sub_done "
                                "exp_done sum_done inv_done prob_done turned turned_kept out_ready out_kept")
            small_ps = psum(nc, inner, "small_ps", [P, 2, CH])
            score_ps = psum(nc, inner, "score_ps", [P, HT, P])
            turn_ps = psum(nc, inner, "turn_ps", [P, 2, HT // 2, P])
            out_ps = psum(nc, inner, "out_ps", [P, 2, CH])
            block = inner.enter_context(nc.Block())

            @block.sync
            def _(sp):
                sp.dma_start(wkT[:, :, :], dram.wkT.rearrange("(k p) n -> p k n", p=P)).then_inc(s.loaded, 16)
                sp.dma_start(wq[:, :, :], dram.wq.rearrange("(k p) n -> p k n", p=P)).then_inc(s.loaded, 16)
                sp.dma_start(wvT[:, :, :], dram.wvT.rearrange("(k p) n -> p k n", p=P)).then_inc(s.loaded, 16)
                sp.dma_start(projT[:, :, :], dram.projT.rearrange("(k p) n -> p k n", p=P)).then_inc(s.loaded, 16)
                sp.dma_start(proj_b[:, :], dram.proj_b).then_inc(s.loaded, 16)
                sp.dma_start(mask_i[:, :], dram.mask.rearrange("(m a) -> m a", a=1)).then_inc(s.loaded, 16)

            @block.tensor
            def _(pe):
                pe.wait_ge(s.loaded, 96)
                for m in range(KT):
                    for k in range(KT):
                        mm = pe.matmul(small_ps[:, m, 0:NK], wkT[:, k, m * P:(m + 1) * P], env.ctxT[:, k, :],
                                       start=(k == 0), stop=(k == KT - 1))
                mm.then_inc(s.key_ready, 1)
                pe.wait_ge(s.key_kept, 1)
                for m in range(KT):
                    for k in range(KT):
                        mm = pe.matmul(small_ps[:, m, 0:NK], wq[:, k, m * P:(m + 1) * P], keyT[:, k, :],
                                       start=(k == 0), stop=(k == KT - 1))
                mm.then_inc(s.qk_ready, 1)
                pe.wait_ge(s.qk_kept, 1)
                for b in range(NB):
                    for k in range(KT):
                        mm = pe.matmul(small_ps[0:M, b, 0:D], env.ctxT[:, k, b * M:(b + 1) * M], wvT[:, k, :],
                                       start=(k == 0), stop=(k == KT - 1))
                mm.then_inc(s.v_ready, 1)
                for b in range(NB):
                    if b:
                        pe.wait_ge(s.sub_done, b)
                    for t in range(HT):
                        tok = (b * HT + t) * P
                        for k in range(KT):
                            mm = pe.matmul(score_ps[:, t, 0:M], env.xT[:, k, tok:tok + P], qkT[:, k, b * M:(b + 1) * M],
                                           start=(k == 0), stop=(k == KT - 1))
                    mm.then_inc(s.score_ready, 1)
                for b in range(NB):
                    pe.wait_ge(s.prob_done, b + 1)
                    if b:
                        pe.wait_ge(s.turned_kept, b)
                    for t in range(HT):
                        mm = pe.transpose(turn_ps[0:M, t // (HT // 2), t % (HT // 2), :], pr[:, b, t, :], env.ident[:, :])
                    mm.then_inc(s.turned, 1)
                    pe.wait_ge(s.turned_kept, b + 1)
                    pe.wait_ge(s.v_kept, 1)
                    for t in range(HT):
                        i = b * HT + t
                        if i >= 2:
                            pe.wait_ge(s.out_kept, i - 1)
                        pe.matmul(out_ps[:, i % 2, 0:D], prT[:, b, t, :], v[:, b, :], start=True, stop=True)\
                          .then_inc(s.out_ready, 1)

            @block.scalar
            def _(act):
                for b in range(NB):
                    act.wait_ge(s.sub_done, b + 1)
                    act.activation(pr[:, b], sc[:, :, :], ACT.Exp, scale=scale).then_inc(s.exp_done, 1)
                for i in range(NT):
                    act.wait_ge(s.out_ready, i + 1)
                    act.activation(o[:, i, :], out_ps[:, i % 2, 0:D], ACT.Copy).then_inc(s.out_kept, 1)

            @block.vector
            def _(dve):
                dve.wait_ge(s.loaded, 96)
                dve.tensor_scalar(keep[:, :], mask_i[:, :], 0, None, ALU.not_equal).then_inc(s.kept, 1)
                dve.wait_ge(s.key_ready, 1)
                dve.tensor_copy(keyT[:, :, :], small_ps[:, :, 0:NK]).then_inc(s.key_kept, 1)
                dve.wait_ge(s.qk_ready, 1)
                dve.tensor_copy(qkT[:, :, :], small_ps[:, :, 0:NK]).then_inc(s.qk_kept, 1)
                dve.wait_ge(s.v_ready, 1)
                dve.wait_ge(s.kept, 1)
                dve.tensor_scalar(v[:, :, :], small_ps[0:M, :, 0:D], keep[:, 0:1], None, ALU.mult).then_inc(s.v_kept, 1)
                for b in range(NB):
                    dve.wait_ge(s.score_ready, b + 1)
                    dve.tensor_reduce(rowmax[:, b, :], score_ps[:, :, 0:M], AX.X, ALU.max).then_inc(s.max_done, 1)
                    dve.wait_ge(s.max_done, b + 1)
                    if b:
                        dve.wait_ge(s.exp_done, b)
                    dve.tensor_tensor(sc[:, :, :], score_ps[:, :, 0:M], last(rowmax[:, b, :], M), ALU.subtract)\
                       .then_inc(s.sub_done, 1)
                for b in range(NB):
                    dve.wait_ge(s.exp_done, b + 1)
                    dve.tensor_reduce(rowsum[:, b, :], pr[:, b], AX.X, ALU.add).then_inc(s.sum_done, 1)
                    dve.wait_ge(s.sum_done, b + 1)
                    dve.reciprocal(inv[:, b, :], rowsum[:, b, :]).then_inc(s.inv_done, 1)
                    dve.wait_ge(s.inv_done, b + 1)
                    dve.tensor_tensor(pr[:, b], pr[:, b], last(inv[:, b, :], M), ALU.mult).then_inc(s.prob_done, 1)
                    dve.wait_ge(s.turned, b + 1)
                    dve.tensor_copy(prT[:, b].rearrange("m t p -> m (t p)"),
                                    turn_ps[0:M].rearrange("m a t p -> m (a t p)")).then_inc(s.turned_kept, 1)

        J = S // D

        def proj(pe, n, out):
            b, half = n // 2, n % 2
            for m in range(KT):
                for j in range(J):
                    for k in range(KT):
                        mm = pe.matmul(out[:, m, j:CH:J], projT[:, k, m * P:(m + 1) * P],
                                       o[:, b * HT + KT * j + k, half * P:(half + 1) * P],
                                       start=(j == 0 and k == 0), stop=(j == J - 1 and k == KT - 1), skip_group_check=True)
            return mm

        residual_norm(nc, env, branch_matmuls=proj, bias=proj_b)


def butterfly_ffn(nc, env, dram):
    F = 1024
    NF = F // P
    NS = 10
    with ExitStack() as st:
        up_w = sbuf(nc, st, "up_w", [P, KT, F])
        up_b = sbuf(nc, st, "up_b", [P, NF])
        conW = sbuf(nc, st, "conW", [P, NF, D])
        y_bias = sbuf(nc, st, "y_bias", [P, KT])
        with ExitStack() as inner:
            down_w = sbuf(nc, inner, "down_w", [P, KT, F])
            brow = sbuf(nc, inner, "brow", [1, F])
            tmp_u = sbuf(nc, inner, "tmp_u", [P, KT, F])
            tmp_d = sbuf(nc, inner, "tmp_d", [P, KT, F])
            tmp_b = sbuf(nc, inner, "tmp_b", [1, F])
            coef_u = sbuf(nc, inner, "coef_u", [P, 2, 2, F])
            coef_d = sbuf(nc, inner, "coef_d", [P, 2, 2, F])
            bias2 = sbuf(nc, inner, "bias2", [P, NF + 2 * KT])
            s = sems(nc, "loaded coef_u0 coef_u1 coef_d0 coef_d1 u_step d_step b_step con_ready con_kept bias_ready bias_kept "
                                "side_bias")
            con_ps = psum(nc, inner, "con_ps", [P, NF, D])
            bias_ps = psum(nc, inner, "bias_ps", [P, NF])
            coef_u_ready, coef_d_ready = (s.coef_u0, s.coef_u1), (s.coef_d0, s.coef_d1)
            block = inner.enter_context(nc.Block())

            def stage(eng, y, tmp, coef, stride, step, n0):
                def pairs(a, i):
                    ap = a.rearrange("p k (n two s) -> p k n two s", two=2, s=stride)[:, :, :, i, :]
                    return ap
                own = coef[:, 0, :].unsqueeze(1).broadcast_to(list(y.shape))
                par = coef[:, 1, :].unsqueeze(1).broadcast_to(list(y.shape))
                for i in range(2):
                    eng.tensor_tensor(pairs(tmp, i), pairs(y, 1 - i), pairs(par, i), ALU.mult).then_inc(step, 1)
                eng.wait_ge(step, n0 + 2)
                eng.tensor_tensor(y, y, own, ALU.mult).then_inc(step, 1)
                eng.wait_ge(step, n0 + 3)
                eng.tensor_tensor(y, y, tmp, ALU.add).then_inc(step, 1)
                eng.wait_ge(step, n0 + 4)
                return n0 + 4

            @block.sync
            def _(sp):
                sp.dma_start(up_w[:, :, :], dram.W_exp.rearrange("(k p) n -> p k n", p=P)).then_inc(s.loaded, 16)
                sp.dma_start(brow[:, :], dram.b_exp.rearrange("(a n) -> a n", a=1)).then_inc(s.loaded, 16)
                sp.dma_start(down_w[:, :, :], dram.W_conT.rearrange("(k p) n -> p k n", p=P)).then_inc(s.loaded, 16)
                sp.dma_start(bias2[:, 0:NF], dram.up_bias).then_inc(s.side_bias, 16)
                sp.dma_start(bias2[:, NF:NF + KT], dram.b_con).then_inc(s.side_bias, 16)
                sp.dma_start(bias2[:, NF + KT:], dram.down_bias).then_inc(s.side_bias, 16)
                for i in range(NS):
                    if i >= 2:
                        sp.wait_ge(s.u_step, 4 * (i - 1))
                        sp.wait_ge(s.b_step, 4 * (i - 1))
                    sp.dma_start(coef_u[:, i % 2], dram.up_coef[i].partition_broadcast(P)).then_inc(coef_u_ready[i % 2], 16)
                    if i >= 2:
                        sp.wait_ge(s.d_step, 4 * (i - 1))
                    sp.dma_start(coef_d[:, i % 2], dram.down_coef[NS - 1 - i].partition_broadcast(P)).then_inc(coef_d_ready[i % 2], 16)

            @block.vector
            def _(dve):
                dve.wait_ge(s.loaded, 48)
                n = nb = 0
                for i in range(NS):
                    dve.wait_ge(coef_u_ready[i % 2], 16 * (i // 2 + 1))
                    n = stage(dve, up_w[:, :, :], tmp_u[:, :, :], coef_u[:, i % 2], 2 ** i, s.u_step, n)
                    nb = stage(dve, brow[:, :].unsqueeze(1), tmp_b[:, :].unsqueeze(1), coef_u[0:1, i % 2], 2 ** i, s.b_step, nb)
                dve.wait_ge(s.side_bias, 48)
                dve.wait_ge(s.bias_ready, 1)
                dve.tensor_tensor(up_b[:, :], bias_ps[:, :], bias2[:, 0:NF], ALU.add).then_inc(s.bias_kept, 1)
                dve.tensor_tensor(y_bias[:, :], bias2[:, NF:NF + KT], bias2[:, NF + KT:], ALU.add).then_inc(s.bias_kept, 1)
                dve.wait_ge(s.con_ready, 1)
                dve.tensor_copy(conW[:, :, :], con_ps[:, :, :]).then_inc(s.con_kept, 1)

            @block.gpsimd
            def _(pool):
                pool.wait_ge(s.loaded, 48)
                n = 0
                for i in range(NS):
                    pool.wait_ge(coef_d_ready[i % 2], 16 * (i // 2 + 1))
                    n = stage(pool, down_w[:, :, :], tmp_d[:, :, :], coef_d[:, i % 2], 2 ** (NS - 1 - i), s.d_step, n)

            @block.tensor
            def _(pe):
                pe.wait_ge(s.b_step, 4 * NS)
                for f in range(NF):
                    mm = pe.matmul(bias_ps[:, f:f + 1], brow[:, f * P:(f + 1) * P], env.ident[0:1, 0:1], start=True, stop=True)
                mm.then_inc(s.bias_ready, 1)
                pe.wait_ge(s.d_step, 4 * NS)
                for f in range(NF):
                    for k in range(KT):
                        mm = pe.transpose(con_ps[:, f, k * P:(k + 1) * P], down_w[:, k, f * P:(f + 1) * P], env.ident[:, :])
                mm.then_inc(s.con_ready, 1)

        y = sbuf(nc, st, "y", [P, KT, T])
        with ExitStack() as inner:
            hid = sbuf(nc, inner, "hid", [P, 2, NF, CH])
            s = sems(nc, "hid_ready gelu_done y_ready y_kept")
            hid_ps = psum(nc, inner, "hid_ps", [P, 4, CH])
            y_ps = psum(nc, inner, "y_ps", [P, 2, KT, CH])
            block = inner.enter_context(nc.Block())

            @block.tensor
            def _(pe):
                for n in range(NCH + 1):
                    if n < NCH:
                        for f in range(NF):
                            i = n * NF + f
                            if i >= 4:
                                pe.wait_ge(s.gelu_done, i - 3)
                            for k in range(KT):
                                mm = pe.matmul(hid_ps[:, i % 4, :], up_w[:, k, f * P:(f + 1) * P],
                                               env.xT[:, k, n * CH:(n + 1) * CH], start=(k == 0), stop=(k == KT - 1))
                            mm.then_inc(s.hid_ready, 1)
                    if n >= 1:
                        c = n - 1
                        pe.wait_ge(s.gelu_done, (c + 1) * NF)
                        if c >= 2:
                            pe.wait_ge(s.y_kept, c - 1)
                        for m in range(KT):
                            for f in range(NF):
                                mm = pe.matmul(y_ps[:, c % 2, m, :], conW[:, f, m * P:(m + 1) * P], hid[:, c % 2, f, :],
                                               start=(f == 0), stop=(f == NF - 1))
                        mm.then_inc(s.y_ready, 1)

            @block.scalar
            def _(act):
                for i in range(NCH * NF):
                    n, f = i // NF, i % NF
                    act.wait_ge(s.hid_ready, i + 1)
                    if n >= 2:
                        act.wait_ge(s.y_ready, n - 1)
                    act.activation(hid[:, n % 2, f, :], hid_ps[:, i % 4, :], ACT.Gelu, bias=up_b[:, f:f + 1])\
                       .then_inc(s.gelu_done, 1)

            @block.vector
            def _(dve):
                for n in range(NCH):
                    dve.wait_ge(s.y_ready, n + 1)
                    dve.tensor_copy(y[:, :, n * CH:(n + 1) * CH], y_ps[:, n % 2]).then_inc(s.y_kept, 1)

        residual_norm(nc, env, branch=y, bias=y_bias)


def steps_of(kind, half):
    lo, hi = half * CH, (half + 1) * CH
    if kind == "full":
        return [(j, lo, hi) for j in range(S // P)]
    if kind == "causal":
        return [(j, max(lo, j * P), hi) for j in range(hi // P)]
    if kind == "window":
        tiles = [(j, max(lo, j * P), min(hi, j * P + WINQ)) for j in range(S // P)]
        return [t for t in tiles if t[1] < t[2]]
    return [(0, lo, hi)]


def max_pieces(kind):
    out = []
    for t in range(S // P):
        if kind in ("full", "causal"):
            keys = S if kind == "full" else (t + 1) * P
            out += [(t, h, 1, k, min(CH, keys - k), k // CH) for h in range(HU) for k in range(0, keys, CH)]
        elif kind == "window":
            first = max(0, t * P - WIN)
            out += [(t, h, 2, first, (t + 1) * P - first, 0) for h in range(0, HU, 2)]
        else:
            out += [(t, h, 2, 0, M, 0) for h in range(0, HU, 2)]
    return out


def attention(nc, env, dram, kind, scale, mask=None):
    cross = kind in ("cross", "xcausal", "xmask")
    nk = M if cross else S
    nkp = M + 1 if cross else S
    kp = M if cross else P
    nkt = 1 if cross else S // P
    halves = S // CH
    steps = [(half, i == 0, i == len(steps_of(kind, half)) - 1, *t)
             for half in range(halves) for i, t in enumerate(steps_of(kind, half))]
    pieces = max_pieces(kind)
    NP = max(p[5] for p in pieces) + 1
    per_unit = len(pieces) + 1
    hold = len(steps) // 4

    def pieces_at(i):
        n = len(steps) - hold
        i -= hold
        return pieces[i * len(pieces) // n:(i + 1) * len(pieces) // n] if i >= 0 else []

    with ExitStack() as st:
        wq = sbuf(nc, st, "wq", [P, KT, D])
        wk = sbuf(nc, st, "wk", [P, KT, D])
        wv = sbuf(nc, st, "wv", [P, KT, D])
        wo = sbuf(nc, st, "wo", [P, NU, D])
        bq = sbuf(nc, st, "bq", [P, KT])
        bk = sbuf(nc, st, "bk", [P, KT])
        bo = sbuf(nc, st, "bo", [P, KT])
        bv = sbuf(nc, st, "bv", [P, D])
        o = sbuf(nc, st, "o", [P, NU, T])
        inner = st.enter_context(ExitStack())
        q_hi = sbuf(nc, inner, "q_hi", [P, KT, S], F32R)
        q_lo = sbuf(nc, inner, "q_lo", [P, KT, S], F32R)
        k_hi = sbuf(nc, inner, "k_hi", [P, KT, nkp], F32R)
        k_lo = sbuf(nc, inner, "k_lo", [P, KT, nkp], F32R)
        v = sbuf(nc, inner, "v", [kp, nkt, H, 2 * HD])
        qst = sbuf(nc, inner, "qst", [P, 2, HU, S], F32R)
        kst = sbuf(nc, inner, "kst", [P, 2, HU, nkp], F32R)
        zrow = sbuf(nc, inner, "zrow", [1, S], F32R)
        prob = sbuf(nc, inner, "prob", [kp, 2, HU, CH])
        cmax = sbuf(nc, inner, "cmax", [P, HU, S // P, NP])
        negc = sbuf(nc, inner, "negc", [P, HU * S // P])
        crow = sbuf(nc, inner, "crow", [HU * S // P, P], F32R)
        byq = sbuf(nc, inner, "byq", [P, CH])
        inv = sbuf(nc, inner, "inv", [P, CH // (2 * HD)])
        for b in range(NB):
            with ExitStack() as stage:
                s = sems(nc, "loaded biased cleared proj_ready hi_kept kept")
                ps = psum(nc, stage, "ps", [P, 4, CH])
                src = env.ctxT if cross else env.xT
                items = [("q", m, c * CH, CH) for m in range(KT) for c in range(S // CH)]
                if cross:
                    items += [("k", m, 0, M) for m in range(KT)]
                else:
                    items += [("k", m, c * CH, CH) for m in range(KT) for c in range(S // CH)]
                items += [("v", j, 0, 0) for j in range(nkt)]
                nqk = len(items) - nkt
                block = stage.enter_context(nc.Block())

                if b == 0:
                    @block.sync
                    def _(sp):
                        for t, n in ((wq, "Wq"), (wk, "Wk"), (wv, "Wv")):
                            sp.dma_start(t[:, :, :], dram[n].rearrange("(k p) n -> p k n", p=P)).then_inc(s.loaded, 16)
                        sp.dma_start(wo[:, :, :], dram["Wo"].rearrange("(g p) n -> p g n", p=P)).then_inc(s.loaded, 16)
                        for t, n in ((bq, "bq"), (bk, "bk"), (bo, "bo")):
                            if n in dram:
                                sp.dma_start(t[:, :], dram[n]).then_inc(s.loaded, 16)
                        if "bv" in dram:
                            sp.dma_start(bv[:, :], dram["bv"].partition_broadcast(P)).then_inc(s.loaded, 16)
                    nload = 4 + sum(n in dram for n in ("bq", "bk", "bo", "bv"))
                else:
                    nload = 0

                nbias = 0
                if b == 0:
                    nbias = sum(n not in dram for n in ("bq", "bk", "bo", "bv"))

                    @block.gpsimd
                    def _(pool):
                        for t, n in ((bq, "bq"), (bk, "bk"), (bo, "bo"), (bv, "bv")):
                            if n not in dram:
                                pool.memset(t[:, :], 0.0).then_inc(s.biased, 1)
                        pool.memset(v[:, :, :, :], 1.0).then_inc(s.cleared, 1)
                        pool.memset(cmax[:, :, :, :], -3e38)
                        pool.memset(zrow[:, :].bitcast(F32), 0.0)
                        pool.memset(qst[:, :, :, :].bitcast(F32), 0.0)
                        pool.memset(kst[:, :, :, :].bitcast(F32), 0.0).then_inc(s.cleared, 1)
                        if cross:
                            pool.memset(k_hi[:, :, :].bitcast(F32), 0.0).then_inc(s.cleared, 1)
                            pool.memset(k_lo[:, :, :].bitcast(F32), 0.0).then_inc(s.cleared, 1)
                        pool.wait_ge(s.cleared, 4 if cross else 2)
                        pool.memset(kst[STACK:STACK + 1, :, :, :].bitcast(F32), 1.0)

                @block.tensor
                def _(pe):
                    if nload:
                        pe.wait_ge(s.loaded, 16 * nload)
                    for i, (what, m, c, n) in enumerate(items):
                        if i >= 4:
                            pe.wait_ge(s.kept, i - 3)
                        for k in range(KT):
                            if what == "q":
                                mm = pe.matmul(ps[:, i % 4, 0:n], wq[:, k, m * P:(m + 1) * P],
                                               env.xT[:, k, b * S + c:b * S + c + n], start=(k == 0), stop=(k == KT - 1))
                            elif what == "k":
                                mm = pe.matmul(ps[:, i % 4, 0:n], wk[:, k, m * P:(m + 1) * P],
                                               src[:, k, b * nk + c:b * nk + c + n], start=(k == 0), stop=(k == KT - 1))
                            else:
                                mm = pe.matmul(ps[0:kp, i % 4, 0:D], src[:, k, b * nk + m * kp:b * nk + (m + 1) * kp],
                                               wv[:, k, :], start=(k == 0), stop=(k == KT - 1))
                        mm.then_inc(s.proj_ready, 1)

                @block.scalar
                def _(act):
                    if nload:
                        act.wait_ge(s.loaded, 16 * nload)
                    if nbias:
                        act.wait_ge(s.biased, nbias)
                    if cross and b == 0:
                        act.wait_ge(s.cleared, 4)
                    for i, (what, m, c, n) in enumerate(items[:nqk]):
                        hi, bias = (q_hi, bq) if what == "q" else (k_hi, bk)
                        act.wait_ge(s.proj_ready, i + 1)
                        act.activation(hi[:, m, c:c + n], ps[:, i % 4, 0:n], ACT.Identity, bias=bias[:, m:m + 1])\
                           .then_inc(s.hi_kept, 1)

                @block.vector
                def _(dve):
                    if nload:
                        dve.wait_ge(s.loaded, 16 * nload)
                    if nbias:
                        dve.wait_ge(s.biased, nbias)
                    if b == 0:
                        dve.wait_ge(s.cleared, 4 if cross else 2)
                    for i, (what, m, c, n) in enumerate(items):
                        if i < nqk:
                            hi, lo, bias = (q_hi, q_lo, bq) if what == "q" else (k_hi, k_lo, bk)
                            dve.wait_ge(s.hi_kept, i + 1)
                            dve.scalar_tensor_tensor(out=lo[:, m, c:c + n], in0=ps[:, i % 4, 0:n], scalar=bias[:, m:m + 1],
                                                     in1=hi[:, m, c:c + n].bitcast(F32), op0=ALU.add, op1=ALU.subtract)\
                               .then_inc(s.kept, 1)
                        else:
                            dve.wait_ge(s.proj_ready, i + 1)
                            dve.tensor_tensor(v[:, m, :, 0:HD], ps[0:kp, i % 4, 0:D].rearrange("p (h d) -> p h d", h=H),
                                              bv[0:kp, :].rearrange("p (h d) -> p h d", h=H), ALU.add).then_inc(s.kept, 1)

            with ExitStack() as stage:
                s = sems(nc, "written0 written1 stacked0 stacked1 max_ready max_done neg_ready c_loaded s_ready exp_done av_done turned inverted "
                                    "divided evacuated")
                max_ps = psum(nc, stage, "max_ps", [P, 2, CH])
                st_ps = psum(nc, stage, "st_ps", [P, 2, 2, CH])
                acc = psum(nc, stage, "acc", [P, 2, CH])
                block = stage.enter_context(nc.Block())
                stacked = (s.stacked0, s.stacked1)
                written = (s.written0, s.written1)
                PARTS = 4 * 2 + 1
                nsteps = len(steps)

                @block.sync
                def _(sp):
                    for m in range(KT):
                        rows = slice(m * P, (m + 1) * P)
                        for part, (q, k) in enumerate(((q_hi, k_hi), (q_lo, k_lo))):
                            sp.dma_start(env.q_dram[part, rows, :], q[:, m, :].bitcast(F32)).then_inc(written[m], 16)
                            sp.dma_start(env.k_dram[part, rows, 0:nkp], k[:, m, :].bitcast(F32)).then_inc(written[m], 16)
                    for u in range(NU):
                        if u >= 2:
                            sp.wait_ge(s.av_done, nsteps * (u - 1))
                        if u in (0, NU // 2):
                            sp.wait_ge(written[u // (NU // 2)], 64)
                        rows = slice(u * HU * HD, (u + 1) * HU * HD)
                        for part in range(4):
                            d = slice(part * HD, (part + 1) * HD)
                            for stack, source in ((qst, env.q_dram[part // 2, rows, :]), (kst, env.k_dram[part % 2, rows, 0:nkp])):
                                sp.dma_start(stack[d, u % 2, :, :].bitcast(F32), source.rearrange("(h d) n -> d h n", d=HD))\
                                  .then_inc(stacked[u % 2], 16)
                        sp.dma_start(qst[STACK:STACK + 1, u % 2, :, :].bitcast(F32),
                                     zrow[:, :].bitcast(F32).unsqueeze(1).broadcast_to([1, HU, S])).then_inc(stacked[u % 2], 16)

                @block.gpsimd
                def _(pool):
                    for u in range(NU):
                        pool.wait_ge(s.max_done, per_unit * (u + 1))
                        pool.dma_start(qst[STACK:STACK + 1, u % 2, :, :].bitcast(F32), crow[:, :].bitcast(F32)).then_inc(s.c_loaded, 16)

                @block.tensor
                def _(pe):
                    def piece(u, i):
                        t, h, nh, k0, n, _ = pieces[i]
                        g = u * per_unit + i
                        if g >= 2:
                            pe.wait_ge(s.max_done, g - 1)
                        if i == 0:
                            pe.wait_ge(stacked[u % 2], 16 * PARTS * (u // 2 + 1))
                        masked = (kind == "causal" and k0 + n == (t + 1) * P) or kind in ("window", "xmask") or \
                                 (kind == "xcausal" and t == 0)
                        for a in range(nh):
                            at = a * (CH // 2)
                            ne = n + n % 2
                            mm = pe.matmul(max_ps[:, g % 2, at:at + ne], qst[:, u % 2, h + a, t * P:(t + 1) * P],
                                           kst[:, u % 2, h + a, k0:k0 + ne], start=(a == 0), stop=(not masked),
                                           skip_group_check=True)
                            if kind == "causal" and masked:
                                mm = pe.matmul(max_ps[:, g % 2, n - P:n], env.identb[:, :], env.causal_qk[:, :],
                                               start=False, stop=True, skip_group_check=True)
                            elif kind == "window":
                                mm = pe.matmul(max_ps[:, g % 2, at:at + n], env.identb[:, :], env.window_qk[:, WINQ - n:],
                                               start=False, stop=True, skip_group_check=True)
                            elif masked:
                                rows = env.causal_qk[:, 0:M] if kind == "xcausal" else mask.qk[:, b, t, :]
                                mm = pe.matmul(max_ps[:, g % 2, at:at + n], env.identb[:, :], rows,
                                               start=False, stop=True, skip_group_check=True)
                        mm.then_inc(s.max_ready, 1)

                    def turn(u):
                        g = u * per_unit + len(pieces)
                        pe.wait_ge(s.max_done, g - 1)
                        pe.wait_ge(s.neg_ready, u + 1)
                        pe.transpose(max_ps[0:HU * S // P, g % 2, 0:P], negc[:, :], env.ident[:, :]).then_inc(s.max_ready, 1)

                    def scores(u, i):
                        half, _, _, j, lo, hi = steps[i]
                        g = u * nsteps + i
                        masked = (kind == "causal" and lo == j * P) or kind in ("window", "xmask") or \
                                 (kind == "xcausal" and half == 0)
                        for p in range(2):
                            if g >= 1:
                                pe.wait_ge(s.exp_done, 2 * (g - 1) + p + 1)
                            for a in range(2):
                                h = 2 * p + a
                                out = st_ps[0:kp, p, a, 0:hi - lo]
                                mm = pe.matmul(out, kst[:, u % 2, h, j * P:j * P + kp], qst[:, u % 2, h, lo:hi],
                                               start=True, stop=(not masked), skip_group_check=True)
                                if masked and kind in ("causal", "xcausal"):
                                    mm = pe.matmul(out[:, 0:P], env.identb[:, 0:kp], env.causal_kq[:, :],
                                                   start=False, stop=True, skip_group_check=True)
                                elif kind == "window":
                                    mm = pe.matmul(out, env.identb[:, :], env.window_kq[:, lo - j * P:hi - j * P],
                                                   start=False, stop=True, skip_group_check=True)
                                elif masked:
                                    mm = pe.matmul(out, env.identb[0:M, 0:M], mask.kq[:, b, lo:hi],
                                                   start=False, stop=True, skip_group_check=True)
                            mm.then_inc(s.s_ready, 1)

                    def values(u, i):
                        half, first, final, j, lo, hi = steps[i]
                        g = u * nsteps + i
                        hc = u * halves + half
                        pe.wait_ge(s.exp_done, 2 * (g + 1))
                        if first and hc >= 2:
                            pe.wait_ge(s.evacuated, hc - 1)
                        for a in range(HU):
                            mm = pe.matmul(acc[32 * a:32 * a + 32, hc % 2, lo - half * CH:hi - half * CH],
                                           v[:, j, u * HU + a, :], prob[:, g % 2, a, 0:hi - lo],
                                           start=first, stop=final, skip_group_check=True)
                        mm.then_inc(s.av_done, 1)

                    for i in range(len(pieces)):
                        piece(0, i)
                    turn(0)
                    for u in range(NU):
                        pe.wait_ge(s.c_loaded, 16 * (u + 1))
                        done = 0
                        for i in range(nsteps):
                            scores(u, i)
                            if i:
                                values(u, i - 1)
                            if u + 1 < NU:
                                for _ in pieces_at(i):
                                    piece(u + 1, done)
                                    done += 1
                        values(u, nsteps - 1)
                        if u + 1 < NU:
                            turn(u + 1)

                @block.scalar
                def _(act):
                    for u in range(NU):
                        for i, (_, _, _, _, lo, hi) in enumerate(steps):
                            g = u * nsteps + i
                            for p in range(2):
                                if g >= 2:
                                    act.wait_ge(s.av_done, g - 1)
                                act.wait_ge(s.s_ready, 2 * g + p + 1)
                                act.activation(prob[:, g % 2, 2 * p:2 * p + 2, 0:hi - lo], st_ps[0:kp, p, :, 0:hi - lo],
                                               ACT.Exp, scale=scale).then_inc(s.exp_done, 1)

                @block.vector
                def _(dve):
                    def piece(u, i):
                        t, h, nh, _, n, part = pieces[i]
                        g = u * per_unit + i
                        dve.wait_ge(s.max_ready, g + 1)
                        if i == 0 and u >= 1:
                            dve.wait_ge(s.neg_ready, u)
                        dve.tensor_reduce(cmax[:, h:h + nh, t, part],
                                          max_ps[:, g % 2, :].rearrange("p (a n) -> p a n", a=nh)[:, :, 0:n],
                                          AX.X, ALU.max).then_inc(s.max_done, 1)

                    def turn(u):
                        g = u * per_unit + len(pieces)
                        dve.wait_ge(s.max_done, g)
                        if u >= 1:
                            dve.wait_ge(s.max_ready, g - per_unit + 1)
                        dve.tensor_reduce(negc[:, :], cmax[:, :, :, :].rearrange("p h t a -> p (h t) a"), AX.X, ALU.max,
                                          negate=True).then_inc(s.neg_ready, 1)
                        dve.wait_ge(s.max_ready, g + 1)
                        if u >= 1:
                            dve.wait_ge(s.c_loaded, 16 * u)
                        dve.tensor_copy(crow[:, :], max_ps[0:HU * S // P, g % 2, 0:P]).then_inc(s.max_done, 1)

                    def evacuate(u, half, step):
                        hc = u * halves + half
                        dve.wait_ge(s.av_done, u * nsteps + step + 1)
                        if hc >= 1:
                            dve.wait_ge(s.evacuated, hc)
                        dve.transpose(byq[:, :], acc[:, hc % 2, :]).then_inc(s.turned, 1)
                        dve.wait_ge(s.turned, hc + 1)
                        blocks = byq[:, :].rearrange("p (n r) -> p n r", r=2 * HD)
                        dve.reciprocal(inv[:, :], blocks[:, :, HD]).then_inc(s.inverted, 1)
                        dve.wait_ge(s.inverted, hc + 1)
                        dve.tensor_tensor(blocks, blocks, last(inv[:, :], 2 * HD), ALU.mult).then_inc(s.divided, 1)
                        dve.wait_ge(s.divided, hc + 1)
                        dve.transpose(o[:, u, b * S + half * CH:b * S + (half + 1) * CH], byq[:, :]).then_inc(s.evacuated, 1)

                    for i in range(len(pieces)):
                        piece(0, i)
                    turn(0)
                    for u in range(NU):
                        done = 0
                        for i in range(nsteps):
                            if i and steps[i - 1][2]:
                                evacuate(u, steps[i - 1][0], i - 1)
                            if u + 1 < NU:
                                for _ in pieces_at(i):
                                    piece(u + 1, done)
                                    done += 1
                        if u + 1 < NU:
                            turn(u + 1)
                        evacuate(u, steps[-1][0], nsteps - 1)
        inner.close()

        def project(pe, n, out):
            for m in range(KT):
                for g in range(NU):
                    mm = pe.matmul(out[:, m, :], wo[:, g, m * P:(m + 1) * P], o[:, g, n * CH:(n + 1) * CH],
                                   start=(g == 0), stop=(g == NU - 1))
            return mm

        residual_norm(nc, env, branch_matmuls=project, bias=bo)


def mask_tiles(nc, st, env, m_qk, m_kq, cols, dt, op, value, name):
    t = named(qk=sbuf(nc, st, name + "_qk", [P, NB, S // P, M], BF16), kq=sbuf(nc, st, name + "_kq", [M, NB, S], BF16))
    with ExitStack() as inner:
        raw_qk = sbuf(nc, inner, "raw_qk", [P, NB, S // P, M], dt)
        raw_kq = sbuf(nc, inner, "raw_kq", [M, NB, cols], dt)
        s = sems(nc, "loaded")
        block = inner.enter_context(nc.Block())

        @block.sync
        def _(sp):
            for b in range(NB):
                sp.dma_start(raw_qk[:, b], m_qk(b)).then_inc(s.loaded, 16)
                sp.dma_start(raw_kq[:, b], m_kq(b)).then_inc(s.loaded, 16)

        @block.vector
        def _(dve):
            dve.wait_ge(s.loaded, 64)
            for b in range(NB):
                dve.tensor_scalar(t.qk[:, b], raw_qk[:, b], 0, value, op, ALU.mult)
                dve.tensor_scalar(t.kq[:, b], raw_kq[:, b].broadcast_to([M, S]), 0, value, op, ALU.mult)
    return t


def moe(nc, env, dram, E, F, topk, glu, score, shared):
    NF = F // P
    NKX = E + shared
    CT = 1024
    HV = CT // CH
    peel = NKX - 2 * ((NKX - 2) // 2)
    biased = "b1" in dram
    with ExitStack() as st:
        gT = sbuf(nc, st, "gT", [E, T])
        y = sbuf(nc, st, "y", [P, KT, T])
        y_bias = sbuf(nc, st, "y_bias", [P, KT])
        b2 = sbuf(nc, st, "b2", [E, D])
        with ExitStack() as inner:
            wr = sbuf(nc, inner, "wr", [P, KT, E])
            rb = sbuf(nc, inner, "rb", [P, E])
            rs = sbuf(nc, inner, "rs", [P, 1])
            sc = sbuf(nc, inner, "sc", [P, NT, E])
            rowmax = sbuf(nc, inner, "rowmax", [P, NT])
            before = sbuf(nc, inner, "before", [P, E, E])
            beats = sbuf(nc, inner, "beats", [P, NT, E, E])
            ties = sbuf(nc, inner, "ties", [P, NT, E, E])
            rank = sbuf(nc, inner, "rank", [P, NT, E])
            total = sbuf(nc, inner, "total", [P, NT])
            s = sems(nc, "loaded ones_ready before_ready logit_ready chain acted gate_ready turned kept stored")
            log_ps = psum(nc, inner, "log_ps", [P, NT, E])
            gT_ps = psum(nc, inner, "gT_ps", [E, T])
            block = inner.enter_context(nc.Block())
            loads = 1 + ("router_b" in dram) + ("route_scale" in dram) + ("b2" in dram) + ("bs2" in dram)

            @block.sync
            def _(sp):
                sp.dma_start(wr[:, :, :], dram["Wr"].rearrange("(k p) n -> p k n", p=P)).then_inc(s.loaded, 16)
                if "router_b" in dram:
                    sp.dma_start(rb[:, :], dram["router_b"].partition_broadcast(P)).then_inc(s.loaded, 16)
                if "route_scale" in dram:
                    sp.dma_start(rs[:, :], dram["route_scale"].partition_broadcast(P)).then_inc(s.loaded, 16)
                if "b2" in dram:
                    sp.dma_start(b2[:, :], dram["b2"]).then_inc(s.loaded, 16)
                if "bs2" in dram:
                    sp.dma_start(y_bias[:, :], dram["bs2"]).then_inc(s.loaded, 16)
                sp.wait_ge(s.kept, 1)
                sp.dma_start(dram["gates"][0:E, :], gT[:, :]).then_inc(s.stored, 16)
                sp.wait_ge(s.stored, 16)

            @block.gpsimd
            def _(pool):
                pool.memset(before[:, :, :], 1.0).then_inc(s.ones_ready, 1)
                pool.wait_ge(s.ones_ready, 1)
                pool.affine_select(out=before[:, :, :], in_=before[:, :, :], compare_op=ALU.is_gt, fill=0.0, base=0,
                                   pattern=[[1, E], [-1, E]], channel_multiplier=0).then_inc(s.before_ready, 1)

            @block.tensor
            def _(pe):
                pe.wait_ge(s.loaded, 16 * loads)
                for t in range(NT):
                    for k in range(KT):
                        mm = pe.matmul(log_ps[:, t, :], env.xT[:, k, t * P:(t + 1) * P], wr[:, k, :],
                                       start=(k == 0), stop=(k == KT - 1))
                mm.then_inc(s.logit_ready, 1)
                pe.wait_ge(s.gate_ready, 1)
                for t in range(NT):
                    mm = pe.transpose(gT_ps[:, t * P:(t + 1) * P], sc[:, t, :], env.ident[:, :])
                mm.then_inc(s.turned, 1)

            @block.scalar
            def _(act):
                act.wait_ge(s.chain, 3 if score == "softmax" else 1)
                act.activation(sc[:, :, :], sc[:, :, :], ACT.Exp if score == "softmax" else ACT.Sigmoid).then_inc(s.acted, 1)

            @block.vector
            def _(dve):
                done = [0]

                def link(ins):
                    done[0] += 1
                    ins.then_inc(s.chain, 1)
                    dve.wait_ge(s.chain, done[0])

                dve.wait_ge(s.loaded, 16 * loads)
                dve.wait_ge(s.logit_ready, 1)
                if "router_b" in dram:
                    link(dve.tensor_tensor(sc[:, :, :], log_ps[:, :, :], over(rb[:, :], NT), ALU.add))
                else:
                    link(dve.tensor_copy(sc[:, :, :], log_ps[:, :, :]))
                if score == "softmax":
                    link(dve.tensor_reduce(rowmax[:, :], sc[:, :, :], AX.X, ALU.max))
                    link(dve.tensor_tensor(sc[:, :, :], sc[:, :, :], last(rowmax[:, :], E), ALU.subtract))
                dve.wait_ge(s.acted, 1)
                if "route_scale" in dram:
                    link(dve.tensor_scalar(sc[:, :, :], sc[:, :, :], rs[:, 0:1], None, ALU.mult))
                own = sc[:, :, :].unsqueeze(3).broadcast_to([P, NT, E, E])
                other = sc[:, :, :].unsqueeze(2).broadcast_to([P, NT, E, E])
                dve.wait_ge(s.before_ready, 1)
                link(dve.tensor_tensor(beats[:, :, :, :], other, own, ALU.is_gt))
                link(dve.tensor_tensor(ties[:, :, :, :], other, own, ALU.is_equal))
                link(dve.tensor_tensor(ties[:, :, :, :], ties[:, :, :, :],
                                       before[:, :, :].unsqueeze(1).broadcast_to([P, NT, E, E]), ALU.mult))
                link(dve.tensor_tensor(beats[:, :, :, :], beats[:, :, :, :], ties[:, :, :, :], ALU.add))
                link(dve.tensor_reduce(rank[:, :, :], beats[:, :, :, :], AX.X, ALU.add))
                link(dve.tensor_scalar(rank[:, :, :], rank[:, :, :], float(topk), None, ALU.is_lt))
                link(dve.tensor_tensor(sc[:, :, :], sc[:, :, :], rank[:, :, :], ALU.mult))
                link(dve.tensor_reduce(total[:, :], sc[:, :, :], AX.X, ALU.add))
                link(dve.reciprocal(total[:, :], total[:, :]))
                dve.tensor_tensor(sc[:, :, :], sc[:, :, :], last(total[:, :], E), ALU.mult).then_inc(s.gate_ready, 1)
                dve.wait_ge(s.turned, 1)
                dve.tensor_copy(gT[:, :], gT_ps[:, :]).then_inc(s.kept, 1)

        with ExitStack() as inner:
            NW = 2 if glu else 1
            w1 = sbuf(nc, inner, "w1", [P, 2, NW, KT, F])
            w2 = sbuf(nc, inner, "w2", [P, 2, NF, D])
            gate = sbuf(nc, inner, "gate", [P, 2, CT])
            b1 = sbuf(nc, inner, "b1", [P, 2, NF])
            lift = sbuf(nc, inner, "lift", [P, 4, CH])
            hid = sbuf(nc, inner, "hid", [P, HV, NF, CH])
            R = 2 if glu else 4
            s = sems(nc, "w_ready0 w_ready1 hid_ready hid_free act_ready mul_done y_done chunk_done")
            hid_ps = psum(nc, inner, "hid_ps", [P, R, NW, CH])
            y_ps = psum(nc, inner, "y_ps", [P, HV, KT, CH])
            block = inner.enter_context(nc.Block())
            nd = NW + 2 + biased
            w_ready = (s.w_ready0, s.w_ready1)

            def bank(slot, half, f, ring):
                return ((slot * HV + half) * NF + f) % ring

            def turns(eng, first, turn):
                for i in range(peel):
                    turn(first + i, i - shared, (first + i) % 2, (first + i) // 2 + 1)
                with eng.Fori(0, (NKX - peel) // 2) as i:
                    for j in range(2):
                        k = i * 2 + (first + peel + j)
                        turn(k, i * 2 + (peel + j - shared), (first + peel + j) % 2, i + ((first + peel + j) // 2 + 1))

            @block.sync
            def _(sp):
                for c in range(T // CT):
                    def turn(k, e, slot, uses):
                        common = not isinstance(e, bass.RuntimeValue) and isinstance(e, int) and e < 0
                        sp.wait_ge(s.y_done, k * HV)
                        for a, n in enumerate(("W1", "Wu")[:NW]):
                            src = dram["S" + n] if common else dram[n][e]
                            sp.dma_start(w1[:, slot, a], src.rearrange("(k p) f -> p k f", p=P)).then_inc(w_ready[slot], 16)
                        src = dram["SW2"] if common else dram["W2"][e]
                        sp.dma_start(w2[:, slot], src.rearrange("(f p) n -> p f n", p=P)).then_inc(w_ready[slot], 16)
                        if biased:
                            src = dram["Sb1"] if common else dram["b1"][e]
                            sp.dma_start(b1[:, slot], src).then_inc(w_ready[slot], 16)
                        src = dram["one_row"] if common else dram["gates"][e, c * CT:(c + 1) * CT]
                        sp.dma_start(gate[:, slot], src.partition_broadcast(P)).then_inc(w_ready[slot], 16)
                    turns(sp, c * NKX, turn)

            @block.gpsimd
            def _(pool):
                pool.sem_inc(s.y_done, 2)
                pool.sem_inc(s.hid_free if glu else s.act_ready, R)
                pool.sem_inc(s.mul_done, 4)

            @block.tensor
            def _(pe):
                for c in range(T // CT):
                    def hidden(k, slot, half):
                        for f in range(NF):
                            n = (k * HV + half) * NF + f
                            pe.wait_ge(s.hid_free if glu else s.act_ready, n + 1)
                            for a in range(NW):
                                for kk in range(KT):
                                    mm = pe.matmul(hid_ps[:, bank(slot, half, f, R), a, :], w1[:, slot, a, kk, f * P:(f + 1) * P],
                                                   env.xT[:, kk, c * CT + half * CH:c * CT + (half + 1) * CH],
                                                   start=(kk == 0), stop=(kk == KT - 1))
                            mm.then_inc(s.hid_ready, 1)

                    def down(k, slot, half, opens, closes):
                        pe.wait_ge(s.mul_done, (k * HV + half) * NF + (NF + 4))
                        for m in range(KT):
                            for f in range(NF):
                                mm = pe.matmul(y_ps[:, half, m, :], w2[:, slot, f, m * P:(m + 1) * P], hid[:, half, f, :],
                                               start=(opens and f == 0), stop=(closes and f == NF - 1), skip_group_check=True)
                        mm.then_inc(s.y_done, 1)
                        return mm

                    if c:
                        pe.wait_ge(s.chunk_done, HV * c)
                    if "b2" in dram:
                        for half in range(HV):
                            for m in range(KT):
                                pe.matmul(y_ps[:, half, m, :], b2[:, m * P:(m + 1) * P],
                                          gT[:, c * CT + half * CH:c * CT + (half + 1) * CH], start=True, stop=False,
                                          skip_group_check=True)
                    opens_with = "b2" not in dram
                    first = [True]

                    def turn(k, e, slot, uses):
                        pe.wait_ge(w_ready[slot], uses * (16 * nd))
                        hidden(k, slot, 0)
                        if not first[0]:
                            down(k - 1, 1 - slot, 1, opens_with and first_down[0], False)
                            first_down[0] = False
                        hidden(k, slot, 1)
                        down(k, slot, 0, opens_with and first[0], False)
                        first[0] = False

                    first_down = [True]
                    turns(pe, c * NKX, turn)
                    k = (c + 1) * NKX - 1
                    down(k, k % 2, 1, False, True)

            @block.scalar
            def _(act):
                for c in range(T // CT):
                    def turn(k, e, slot, uses):
                        act.wait_ge(w_ready[slot], uses * (16 * nd))
                        for half in range(HV):
                            for f in range(NF):
                                n = (k * HV + half) * NF + f
                                act.wait_ge(s.hid_ready, n + 1)
                                act.wait_ge(s.mul_done, n + 1)
                                ins = hid_ps[:, bank(slot, half, f, R), 0, :]
                                out = lift[:, bank(slot, half, f, 4), :]
                                if glu:
                                    act.activation(out, ins, ACT.Silu).then_inc(s.act_ready, 1)
                                else:
                                    act.activation(out, ins, ACT.Gelu, bias=b1[:, slot, f:f + 1]).then_inc(s.act_ready, 1)
                    turns(act, c * NKX, turn)

            @block.vector
            def _(dve):
                for c in range(T // CT):
                    def turn(k, e, slot, uses):
                        dve.wait_ge(w_ready[slot], uses * (16 * nd))
                        for half in range(HV):
                            dve.wait_ge(s.y_done, k * HV + (half + 1))
                            for f in range(NF):
                                n = (k * HV + half) * NF + f
                                dve.wait_ge(s.act_ready, n + (1 if glu else R + 1))
                                up = lift[:, bank(slot, half, f, 4), :]
                                if glu:
                                    dve.tensor_tensor(up, up, hid_ps[:, bank(slot, half, f, R), 1, :], ALU.mult).then_inc(s.hid_free, 1)
                                    dve.wait_ge(s.hid_free, n + (R + 1))
                                mul = dve.tensor_tensor(hid[:, half, f, :], up, gate[:, slot, half * CH:(half + 1) * CH], ALU.mult)
                                mul.then_inc(s.mul_done, 1)
                    turns(dve, c * NKX, turn)
                    dve.wait_ge(s.y_done, (c + 1) * NKX * HV + 2)
                    for half in range(HV):
                        at = c * CT + half * CH
                        dve.tensor_copy(y[:, :, at:at + CH], y_ps[:, half]).then_inc(s.chunk_done, 1)

        residual_norm(nc, env, branch=y, bias=y_bias if "bs2" in dram else None)


def decoder(nc, d, out, stages=STAGES):
    def group(prefix):
        return {n[len(prefix):]: a for n, a in d.items() if n.startswith(prefix)}

    def space(prefix):
        return named(**group(prefix))

    with ExitStack() as st:
        env = named(
            q_dram=d["q_dram"], k_dram=d["k_dram"],
            xT=sbuf(nc, st, "xT", [P, KT, T]), ctxT=sbuf(nc, st, "ctxT", [P, KT, NB * M]),
            ident=sbuf(nc, st, "ident", [P, P]), identb=sbuf(nc, st, "identb", [P, P], BF16),
            avg=sbuf(nc, st, "avg", [P, P]), eps=sbuf(nc, st, "eps", [P, 1]), ones=sbuf(nc, st, "ones", [P, P]),
            causal_qk=sbuf(nc, st, "causal_qk", [P, P], BF16), causal_kq=sbuf(nc, st, "causal_kq", [P, P], BF16),
            window_qk=sbuf(nc, st, "window_qk", [P, WINQ], BF16), window_kq=sbuf(nc, st, "window_kq", [P, WINQ], BF16))
        stored = st.enter_context(nc.semaphore("stored"))
        setup(nc, env, space("in_"))

        def pad_attention():
            def pad_mask(b):
                return d["pad_mask"][b].unsqueeze(0).unsqueeze(0).broadcast_to([P, S // P, M])
            with ExitStack() as ms:
                t = mask_tiles(nc, ms, env, pad_mask, lambda b: d["pad_mask"][b].unsqueeze(1), 1, U8,
                               ALU.not_equal, MASKED, "pad")
                attention(nc, env, group("L2x_"), "xmask", float(8 ** -0.5), t)

        def masked_attention():
            with ExitStack() as ms:
                t = mask_tiles(nc, ms, env, lambda b: d["mask_qk"][b].rearrange("(t p) m -> p t m", p=P),
                               lambda b: d["mask_kq"][b], S, I32, ALU.is_equal, NEG, "seen")
                attention(nc, env, group("L3x_"), "xmask", float(HD ** -0.5), t)

        plan = [
            lambda: min_gru(nc, env, group("L0a_")),
            lambda: wide_cross(nc, env, space("L0x_")),
            lambda: butterfly_ffn(nc, env, space("L0f_")),
            lambda: attention(nc, env, group("L1a_"), "causal", float(HD ** -0.5)),
            lambda: attention(nc, env, group("L1x_"), "xcausal", float(HD ** -0.5)),
            lambda: moe(nc, env, group("L1f_"), 8, 512, 2, True, "softmax", 1),
            lambda: attention(nc, env, group("L2a_"), "full", float(D ** -0.5)),
            pad_attention,
            lambda: moe(nc, env, group("L2f_"), 8, 128, 2, False, "sigmoid", 1),
            lambda: attention(nc, env, group("L3a_"), "window", float(HD ** -0.5)),
            masked_attention,
            lambda: moe(nc, env, group("L3f_"), 16, 512, 4, False, "softmax", 0),
        ]
        for stage in plan[:stages] if isinstance(stages, int) else [plan[i] for i in stages]:
            with nc.cleanup_on_exit():
                stage()
        with nc.Block() as block:
            @block.sync
            def _(sp):
                sp.dma_start(out.rearrange("(k p) t -> p k t", p=P), env.xT[:, :, :]).then_inc(stored, 16)
                sp.wait_ge(stored, 16)


def layouts(i):
    import numpy as np

    c = np.ascontiguousarray
    a = {n: np.asarray(x) for n, x in i.items()}
    r = {}

    def columns(b):
        return c(np.swapaxes(b.reshape(*b.shape[:-1], -1, P), -1, -2))

    r["in_xT"] = c(a["x"].reshape(T, D).T)
    r["in_ctxT"] = c(a["ctx_1024"].reshape(NB * M, D).T)
    r["pad_mask"] = c(a["mask_BxS2_bf0"])
    r["mask_qk"] = c(a["mask_Bx1xSxS2_ik1"][:, 0])
    r["mask_kq"] = c(a["mask_Bx1xSxS2_ik1"][:, 0].transpose(0, 2, 1))
    for n in "ifh":
        r["L0a_w_" + n] = columns(a["L0_attn_w_" + n])
    qkv = a["L0_xattn_qkv_w"]
    r["L0x_wq"], r["L0x_wkT"], r["L0x_wvT"] = c(qkv[:D]), c(qkv[D:2 * D].T), c(qkv[2 * D:].T)
    r["L0x_projT"], r["L0x_proj_b"], r["L0x_mask"] = c(a["L0_xattn_proj_w"].T), columns(a["L0_xattn_proj_b"]), a["mask_S2_ik0"]
    for n in ("W_exp", "b_exp"):
        r["L0f_" + n] = a["L0_ffn_" + n]
    for n in ("up_bias", "b_con", "down_bias"):
        r["L0f_" + n] = columns(a["L0_ffn_" + n])
    r["L0f_W_conT"] = c(a["L0_ffn_W_con"].T)
    for n, w, flip in (("up", a["L0_ffn_up_weights"], False), ("down", a["L0_ffn_down_weights"], True)):
        coef = np.empty((w.shape[0], 2, 2 * w.shape[1]), w.dtype)
        for s in range(w.shape[0]):
            ws = w[s].reshape(-1, 2 ** s, 2, 2)
            own = np.stack([ws[..., 0, 0], ws[..., 1, 1]], 1)
            par = np.stack([ws[..., 1, 0], ws[..., 0, 1]] if flip else [ws[..., 0, 1], ws[..., 1, 0]], 1)
            coef[s, 0], coef[s, 1] = own.reshape(-1), par.reshape(-1)
        r[f"L0f_{n}_coef"] = coef

    def padded_rows(w):
        out = np.zeros((2 * D, w.shape[1]), w.dtype)
        out.reshape(H, 2 * HD, -1)[:, :HD] = w.reshape(H, HD, -1)
        return out

    for n in ("Wq", "Wk", "Wv", "bv"):
        r["L1a_" + n] = a["L1_attn_" + n]
    for n in ("bq", "bk", "bo"):
        r["L1a_" + n] = columns(a["L1_attn_" + n])
    r["L1a_Wo"] = padded_rows(a["L1_attn_Wo"])
    for p, q in (("L1x_", "L1_xattn_"), ("L3a_", "L3_attn_"), ("L3x_", "L3_xattn_")):
        for n in ("Wq", "Wk", "Wv"):
            r[p + n] = c(a[q + n].T)
        r[p + "Wo"] = padded_rows(a[q + "Wo"].T)
    for n in ("Wq", "Wk", "Wv"):
        big = np.zeros((H, HD, H, HD), a["L2_attn_" + n].dtype)
        for h in range(H):
            big[h, :, h, :] = a["L2_attn_" + n].T
        r["L2a_" + n] = big.reshape(D, D)
    r["L2a_Wo"], r["L2a_bo"] = padded_rows(a["L2_attn_W_out"].T), columns(a["L2_attn_b_out"])
    for n in ("q", "k"):
        w, bias = a["L2_xattn_W" + n], a["L2_xattn_b" + n]
        big, bb = np.zeros((D, H, HD), w.dtype), np.zeros((H, HD), bias.dtype)
        hq = w.shape[1] // (H // 2)
        big[:, :, :hq] = np.repeat(w.reshape(D, H // 2, hq), 2, 1)
        bb[:, :hq] = np.repeat(bias.reshape(H // 2, hq), 2, 0)
        r["L2x_W" + n], r["L2x_b" + n] = big.reshape(D, D), columns(bb.reshape(D))
    r["L2x_Wv"] = np.eye(D, dtype=np.float32)
    r["L2x_Wo"] = padded_rows(np.eye(D, dtype=np.float32))

    for n, m in (("Wr", "Wr"), ("W1", "Wg"), ("Wu", "Wu"), ("W2", "Wd"), ("SW1", "Sg"), ("SWu", "Su"), ("SW2", "Sd")):
        r["L1f_" + n] = c(a["L1_ffn_" + m])

    for n, m in (("Wr", "gate_W"), ("W1", "W1"), ("W2", "W2"), ("SW1", "Ws1"), ("SW2", "Ws2"), ("b2", "b2")):
        r["L2f_" + n] = c(a["L2_ffn_" + m])
    r["L2f_bs2"] = columns(a["L2_ffn_bs2"])
    r["L2f_b1"], r["L2f_Sb1"] = columns(a["L2_ffn_b1"]), columns(a["L2_ffn_bs1"])
    r["L2f_route_scale"] = a["L2_ffn_route_scale"].reshape(1)
    for n, m in (("Wr", "router_w"), ("router_b", "router_b"), ("W1", "w1"), ("W2", "w2"), ("b2", "b2")):
        r["L3f_" + n] = c(a["L3_ffn_" + m])
    r["L3f_b1"] = columns(a["L3_ffn_b1"])
    for p in ("L1f_", "L2f_"):
        r[p + "one_row"] = np.ones(1024, np.float32)
    return r


def kernel(**inputs):
    import numpy as np
    import concourse.bacc as bacc
    from concourse.bass_utils import run_bass_kernel_spmd

    nc = bacc.Bacc("TRN2", target_bir_lowering=False, num_devices=1)
    arrays, aps = {}, {}
    for name, a in layouts(inputs).items():
        arrays[name + "_dram"] = a
        aps[name] = nc.dram_tensor(name + "_dram", a.shape, mybir.dt.from_np(a.dtype), kind="ExternalInput").ap()
    for p, e in (("L1f_", 8), ("L2f_", 8), ("L3f_", 16)):
        aps[p + "gates"] = nc.dram_tensor(p + "gates_dram", [e, T], F32, kind="Internal").ap()
    for n in "qk":
        aps[n + "_dram"] = nc.dram_tensor(n + "_parts_dram", [2, D, S], F32, kind="Internal").ap()
    out = nc.dram_tensor("out_dram", [D, T], F32, kind="ExternalOutput").ap()
    decoder(nc, aps, out)
    r = run_bass_kernel_spmd(nc, [arrays], core_ids=[0])
    return np.ascontiguousarray(r.results[0]["out_dram"].T).reshape(NB, S, D)
```

```python
from contextlib import ExitStack

import concourse.bass as bass
from concourse import mybir

F32 = mybir.dt.float32
F32R = mybir.dt.float32r
BF16 = mybir.dt.bfloat16
I32 = mybir.dt.int32
U8 = mybir.dt.uint8
ALU = mybir.AluOpType
ACT = mybir.ActivationFunctionType
AX = mybir.AxisListType

P = 128
D = 256
KT = D // P
NB = 2
S = 1024
T = NB * S
NT = T // P
CH = 512
NCH = T // CH
M = 77
H = 16
HD = D // H
HU = 4
NU = H // HU
WIN = 64
WINQ = P + WIN
EPS = 1e-5
MASKED = -1e30
NEG = -1e9
STACK = 4 * HD
STAGES = 12
TAGS = []


def tag():
    TAGS.append(0)
    return len(TAGS)


def named(**items):
    return type("Named", (), items)


def sems(nc, names):
    return named(**{n: nc.alloc_semaphore(f"{n}_{tag()}") for n in names.split()})


def sbuf(nc, st, name, shape, dt=F32):
    return st.enter_context(nc.sbuf_tensor(f"{name}_{tag()}", shape, dt))


def psum(nc, st, name, shape, dt=F32):
    return st.enter_context(nc.psum_tensor(f"{name}_{tag()}", shape, dt))


def over(ap, n):
    return ap.unsqueeze(1).broadcast_to([ap.shape[0], n, ap.shape[1]])


def last(ap, n):
    return ap.unsqueeze(2).broadcast_to([ap.shape[0], ap.shape[1], n])


def setup(nc, env, dram):
    with ExitStack() as st:
        s = sems(nc, "loaded cleared shaped")
        block = st.enter_context(nc.Block())

        @block.sync
        def _(sp):
            sp.dma_start(env.xT[:, :, :], dram.xT.rearrange("(k p) t -> p k t", p=P)).then_inc(s.loaded, 16)
            sp.dma_start(env.ctxT[:, :, :], dram.ctxT.rearrange("(k p) t -> p k t", p=P)).then_inc(s.loaded, 16)
            sp.wait_ge(s.loaded, 32)

        @block.gpsimd
        def _(pool):
            tiles = (env.ident, env.identb, env.causal_qk, env.causal_kq, env.window_qk, env.window_kq)
            for t in tiles:
                pool.memset(t[:, :], 0.0).then_inc(s.cleared, 1)
            pool.memset(env.avg[:, :], 1.0 / D).then_inc(s.cleared, 1)
            pool.memset(env.eps[:, :], EPS).then_inc(s.cleared, 1)
            pool.memset(env.ones[:, :], 1.0).then_inc(s.cleared, 1)
            pool.wait_ge(s.cleared, len(tiles) + 3)
            for t in (env.ident, env.identb):
                pool.affine_select(out=t[:, :], in_=t[:, :], compare_op=ALU.not_equal, fill=1.0, base=0,
                                   pattern=[[-1, P]], channel_multiplier=1).then_inc(s.shaped, 1)
            pool.affine_select(out=env.causal_qk[:, :], in_=env.causal_qk[:, :], compare_op=ALU.is_ge, fill=MASKED,
                               base=0, pattern=[[-1, P]], channel_multiplier=1).then_inc(s.shaped, 1)
            pool.affine_select(out=env.causal_kq[:, :], in_=env.causal_kq[:, :], compare_op=ALU.is_ge, fill=MASKED,
                               base=0, pattern=[[1, P]], channel_multiplier=-1).then_inc(s.shaped, 1)
            pool.affine_select(out=env.window_qk[:, :], in_=env.window_qk[:, :], compare_op=ALU.is_ge, fill=MASKED,
                               base=-1, pattern=[[1, WINQ]], channel_multiplier=-1).then_inc(s.shaped, 1)
            pool.affine_select(out=env.window_kq[:, :], in_=env.window_kq[:, :], compare_op=ALU.is_ge, fill=MASKED,
                               base=0, pattern=[[1, WINQ]], channel_multiplier=-1).then_inc(s.shaped, 1)
            pool.wait_ge(s.shaped, 6)
            pool.affine_select(out=env.window_qk[:, :], in_=env.window_qk[:, :], compare_op=ALU.is_ge, fill=MASKED,
                               base=WIN, pattern=[[-1, WINQ]], channel_multiplier=1).then_inc(s.shaped, 1)
            pool.affine_select(out=env.window_kq[:, :], in_=env.window_kq[:, :], compare_op=ALU.is_ge, fill=MASKED,
                               base=WIN - 1, pattern=[[-1, WINQ]], channel_multiplier=1).then_inc(s.shaped, 1)


def residual_norm(nc, env, branch_matmuls=None, branch=None, bias=None):
    TC = CH // P
    with ExitStack() as st:
        s = sems(nc, "y_ready summed mean_ready centred squared var_ready rooted inverted spread rstd_ready normed")
        y_ps = psum(nc, st, "y_ps", [P, 2, KT, CH])
        mean_ps = psum(nc, st, "mean_ps", [P, CH])
        var_ps = psum(nc, st, "var_ps", [P, 2, TC])
        rstd_ps = psum(nc, st, "rstd_ps", [P, 2, CH])
        dev = sbuf(nc, st, "dev", [P, NCH, KT, CH])
        sq = sbuf(nc, st, "sq", [P, 2, KT, CH])
        std = sbuf(nc, st, "std", [P, NCH, TC])
        rstd = sbuf(nc, st, "rstd", [P, NCH, TC])
        diag = sbuf(nc, st, "diag", [P, 2, TC, P])
        block = st.enter_context(nc.Block())

        @block.tensor
        def _(pe):
            for n in range(NCH + 3):
                if n < NCH and branch_matmuls:
                    if n >= 2:
                        pe.wait_ge(s.summed, n - 1)
                    branch_matmuls(pe, n, y_ps[:, n % 2]).then_inc(s.y_ready, 1)
                if 1 <= n <= NCH:
                    m = n - 1
                    pe.wait_ge(s.summed, m + 1)
                    if m >= 1:
                        pe.wait_ge(s.centred, m)
                    for k in range(KT):
                        mm = pe.matmul(mean_ps[:, :], env.avg[:, :], env.xT[:, k, m * CH:(m + 1) * CH],
                                       start=(k == 0), stop=(k == KT - 1))
                    mm.then_inc(s.mean_ready, 1)
                if 2 <= n <= NCH + 1:
                    m = n - 2
                    pe.wait_ge(s.squared, m + 1)
                    if m >= 1:
                        pe.wait_ge(s.rooted, m)
                    for t in range(TC):
                        for k in range(KT):
                            mm = pe.matmul(var_ps[:, m % 2, t:t + 1], sq[:, m % 2, k, t * P:(t + 1) * P], env.avg[:, 0:1],
                                           start=(k == 0), stop=(k == KT - 1))
                    mm.then_inc(s.var_ready, 1)
                if n >= 3:
                    m = n - 3
                    pe.wait_ge(s.spread, TC * (m + 1))
                    if m >= 2:
                        pe.wait_ge(s.normed, m - 1)
                    for t in range(TC):
                        mm = pe.matmul(rstd_ps[:, m % 2, t * P:(t + 1) * P], env.ones[:, :], diag[:, m % 2, t, :],
                                       start=True, stop=True)
                    mm.then_inc(s.rstd_ready, 1)

        @block.scalar
        def _(act):
            for n in range(NCH):
                act.wait_ge(s.centred, n + 1)
                if n >= 2:
                    act.wait_ge(s.var_ready, n - 1)
                act.activation(sq[:, n % 2], dev[:, n], ACT.Square).then_inc(s.squared, 1)
                act.wait_ge(s.var_ready, n + 1)
                act.activation(std[:, n, :], var_ps[:, n % 2, :], ACT.Sqrt, bias=env.eps[:, 0:1]).then_inc(s.rooted, 1)

        @block.gpsimd
        def _(pool):
            for n in range(NCH):
                pool.wait_ge(s.inverted, n + 1)
                if n >= 2:
                    pool.wait_ge(s.rstd_ready, n - 1)
                for t in range(TC):
                    pool.tensor_scalar(diag[:, n % 2, t, :], env.ident[:, :], rstd[:, n, t:t + 1], None, ALU.mult)\
                        .then_inc(s.spread, 1)

        @block.vector
        def _(dve):
            for n in range(NCH + 3):
                if n < NCH:
                    x = env.xT[:, :, n * CH:(n + 1) * CH]
                    if branch_matmuls:
                        dve.wait_ge(s.y_ready, n + 1)
                        y = y_ps[:, n % 2]
                    else:
                        y = branch[:, :, n * CH:(n + 1) * CH]
                    if bias is None:
                        dve.tensor_tensor(x, y, x, ALU.add).then_inc(s.summed, 1)
                    else:
                        for k in range(KT):
                            add = dve.scalar_tensor_tensor(out=x[:, k], in0=y[:, k], scalar=bias[:, k:k + 1],
                                                           in1=x[:, k], op0=ALU.add, op1=ALU.add)
                        add.then_inc(s.summed, 1)
                if 1 <= n <= NCH:
                    m = n - 1
                    dve.wait_ge(s.mean_ready, m + 1)
                    dve.tensor_tensor(dev[:, m], env.xT[:, :, m * CH:(m + 1) * CH], over(mean_ps[:, :], KT),
                                      ALU.subtract).then_inc(s.centred, 1)
                if 2 <= n <= NCH + 1:
                    m = n - 2
                    dve.wait_ge(s.rooted, m + 1)
                    dve.reciprocal(rstd[:, m, :], std[:, m, :]).then_inc(s.inverted, 1)
                if n >= 3:
                    m = n - 3
                    dve.wait_ge(s.rstd_ready, m + 1)
                    dve.tensor_tensor(env.xT[:, :, m * CH:(m + 1) * CH], dev[:, m], over(rstd_ps[:, m % 2, :], KT),
                                      ALU.mult).then_inc(s.normed, 1)


def min_gru(nc, env, dram):
    with ExitStack() as st:
        w = {n: sbuf(nc, st, f"w_{n}", [P, KT]) for n in "fih"}
        neg = {n: sbuf(nc, st, f"neg_{n}", [P, KT]) for n in "fi"}
        h_out = sbuf(nc, st, "h_out", [P, KT, T])
        s = sems(nc, "loaded negated abs_done exp_done ln_done relu_done soft_done diff_done gates_done low_done sig_done "
                         "g_done v_done scanned")
        mag = sbuf(nc, st, "mag", [P, 2, 2, S])
        soft = sbuf(nc, st, "soft", [P, 2, 2, S])
        relu = sbuf(nc, st, "relu", [P, 2, 2, S])
        diff = sbuf(nc, st, "diff", [P, 2, S])
        gate = sbuf(nc, st, "gate", [P, 2, 2, S])
        low = sbuf(nc, st, "low", [P, 2, S])
        hid = sbuf(nc, st, "hid", [P, 2, S])
        with nc.Block() as block:
            items = [(k, b) for k in range(KT) for b in range(NB)]

            @block.sync
            def _(sp):
                for n in "fih":
                    sp.dma_start(w[n][:, :], dram["w_" + n]).then_inc(s.loaded, 16)

            @block.scalar
            def _(act):
                act.wait_ge(s.loaded, 48)
                for n, (k, b) in enumerate(items):
                    x = env.xT[:, k, b * S:(b + 1) * S]
                    z = n % 2
                    if n >= 2:
                        act.wait_ge(s.soft_done, 2 * (n - 1))
                    for a, g in enumerate("fi"):
                        act.activation(mag[:, z, a, :], x, ACT.Abs, scale=w[g][:, k:k + 1]).then_inc(s.abs_done, 1)
                    act.wait_ge(s.abs_done, 2 * (n + 1))
                    act.activation(mag[:, z], mag[:, z], ACT.Exp, scale=-1.0).then_inc(s.exp_done, 1)
                    act.wait_ge(s.exp_done, n + 1)
                    act.activation(soft[:, z], mag[:, z], ACT.Ln, bias=1.0).then_inc(s.ln_done, 1)
                for n, (k, b) in enumerate(items):
                    z = n % 2
                    act.wait_ge(s.diff_done, n + 1)
                    if n >= 2:
                        act.wait_ge(s.scanned, n - 1)
                    act.activation(gate[:, z, 0, :], diff[:, z, :], ACT.Sigmoid, scale=-1.0).then_inc(s.gates_done, 1)
                    act.activation(gate[:, z, 1, :], diff[:, z, :], ACT.Sigmoid).then_inc(s.gates_done, 1)
                    act.wait_ge(s.low_done, n + 1)
                    act.activation(low[:, z, :], low[:, z, :], ACT.Sigmoid).then_inc(s.sig_done, 1)

            @block.vector
            def _(dve):
                dve.wait_ge(s.loaded, 48)
                for g in "fi":
                    dve.tensor_scalar(neg[g][:, :], w[g][:, :], -1.0, None, ALU.mult).then_inc(s.negated, 1)
                dve.wait_ge(s.negated, 2)

                def softplus_gap(n):
                    k, b = items[n]
                    z = n % 2
                    x = env.xT[:, k, b * S:(b + 1) * S]
                    for a, g in enumerate("fi"):
                        dve.tensor_scalar(relu[:, z, a, :], x, neg[g][:, k:k + 1], 0.0, ALU.mult, ALU.max)\
                           .then_inc(s.relu_done, 1)
                    dve.wait_ge(s.relu_done, 2 * (n + 1))
                    dve.wait_ge(s.ln_done, n + 1)
                    for a in range(2):
                        dve.tensor_tensor(relu[:, z, a, :], relu[:, z, a, :], soft[:, z, a, :], ALU.add)\
                           .then_inc(s.soft_done, 1)
                    dve.wait_ge(s.soft_done, 2 * (n + 1))
                    if n >= 2:
                        dve.wait_ge(s.gates_done, 2 * (n - 1))
                    dve.tensor_tensor(diff[:, z, :], relu[:, z, 0, :], relu[:, z, 1, :], ALU.subtract)\
                       .then_inc(s.diff_done, 1)

                def hidden(n):
                    k, b = items[n]
                    z = n % 2
                    x = env.xT[:, k, b * S:(b + 1) * S]
                    dve.tensor_scalar(low[:, z, :], x, w["h"][:, k:k + 1], 0.0, ALU.mult, ALU.min).then_inc(s.low_done, 1)
                    dve.tensor_scalar(hid[:, z, :], x, w["h"][:, k:k + 1], 0.0, ALU.mult, ALU.max).then_inc(s.g_done, 1)

                def scan(n):
                    k, b = items[n]
                    z = n % 2
                    dve.wait_ge(s.sig_done, n + 1)
                    dve.wait_ge(s.g_done, 3 * n + 1)
                    dve.tensor_tensor(hid[:, z, :], hid[:, z, :], low[:, z, :], ALU.add).then_inc(s.g_done, 1)
                    dve.wait_ge(s.gates_done, 2 * (n + 1))
                    dve.wait_ge(s.g_done, 3 * n + 2)
                    dve.tensor_tensor(hid[:, z, :], hid[:, z, :], gate[:, z, 1, :], ALU.mult).then_inc(s.g_done, 1)
                    dve.wait_ge(s.g_done, 3 * n + 3)
                    dve.tensor_tensor_scan(h_out[:, k, b * S:(b + 1) * S], gate[:, z, 0, :], hid[:, z, :], 0.0,
                                           ALU.mult, ALU.add).then_inc(s.scanned, 1)

                for n in range(len(items)):
                    if n >= 2:
                        hidden(n - 2)
                    softplus_gap(n) if n < 2 else (scan(n - 2), softplus_gap(n))
                for n in range(len(items) - 2, len(items)):
                    hidden(n)
                    scan(n)
        residual_norm(nc, env, branch=h_out)


def wide_cross(nc, env, dram):
    scale = float(32 ** -0.5)
    NK = NB * M
    HT = NT // NB
    with ExitStack() as st:
        wq = sbuf(nc, st, "wq", [P, KT, D])
        wkT = sbuf(nc, st, "wkT", [P, KT, D])
        wvT = sbuf(nc, st, "wvT", [P, KT, D])
        projT = sbuf(nc, st, "projT", [P, KT, D])
        proj_b = sbuf(nc, st, "proj_b", [P, KT])
        mask_i = sbuf(nc, st, "mask_i", [M, 1], I32)
        keep = sbuf(nc, st, "keep", [M, 1])
        keyT = sbuf(nc, st, "keyT", [P, KT, NK])
        qkT = sbuf(nc, st, "qkT", [P, KT, NK])
        v = sbuf(nc, st, "v", [M, NB, D])
        sc = sbuf(nc, st, "sc", [P, HT, M])
        rowmax = sbuf(nc, st, "rowmax", [P, NB, HT])
        rowsum = sbuf(nc, st, "rowsum", [P, NB, HT])
        inv = sbuf(nc, st, "inv", [P, NB, HT])
        pr = sbuf(nc, st, "pr", [P, NB, HT, M])
        prT = sbuf(nc, st, "prT", [M, NB, HT, P])
        o = sbuf(nc, st, "o", [P, NT, D])
        with ExitStack() as inner:
            s = sems(nc, "loaded kept key_ready key_kept qk_ready qk_kept v_ready v_kept score_ready max_done sub_done "
                                "exp_done sum_done inv_done prob_done turned turned_kept out_ready out_kept")
            small_ps = psum(nc, inner, "small_ps", [P, 2, CH])
            score_ps = psum(nc, inner, "score_ps", [P, HT, P])
            turn_ps = psum(nc, inner, "turn_ps", [P, 2, HT // 2, P])
            out_ps = psum(nc, inner, "out_ps", [P, 2, CH])
            block = inner.enter_context(nc.Block())

            @block.sync
            def _(sp):
                sp.dma_start(wkT[:, :, :], dram.wkT.rearrange("(k p) n -> p k n", p=P)).then_inc(s.loaded, 16)
                sp.dma_start(wq[:, :, :], dram.wq.rearrange("(k p) n -> p k n", p=P)).then_inc(s.loaded, 16)
                sp.dma_start(wvT[:, :, :], dram.wvT.rearrange("(k p) n -> p k n", p=P)).then_inc(s.loaded, 16)
                sp.dma_start(projT[:, :, :], dram.projT.rearrange("(k p) n -> p k n", p=P)).then_inc(s.loaded, 16)
                sp.dma_start(proj_b[:, :], dram.proj_b).then_inc(s.loaded, 16)
                sp.dma_start(mask_i[:, :], dram.mask.rearrange("(m a) -> m a", a=1)).then_inc(s.loaded, 16)

            @block.tensor
            def _(pe):
                pe.wait_ge(s.loaded, 96)
                for m in range(KT):
                    for k in range(KT):
                        mm = pe.matmul(small_ps[:, m, 0:NK], wkT[:, k, m * P:(m + 1) * P], env.ctxT[:, k, :],
                                       start=(k == 0), stop=(k == KT - 1))
                mm.then_inc(s.key_ready, 1)
                pe.wait_ge(s.key_kept, 1)
                for m in range(KT):
                    for k in range(KT):
                        mm = pe.matmul(small_ps[:, m, 0:NK], wq[:, k, m * P:(m + 1) * P], keyT[:, k, :],
                                       start=(k == 0), stop=(k == KT - 1))
                mm.then_inc(s.qk_ready, 1)
                pe.wait_ge(s.qk_kept, 1)
                for b in range(NB):
                    for k in range(KT):
                        mm = pe.matmul(small_ps[0:M, b, 0:D], env.ctxT[:, k, b * M:(b + 1) * M], wvT[:, k, :],
                                       start=(k == 0), stop=(k == KT - 1))
                mm.then_inc(s.v_ready, 1)
                for b in range(NB):
                    if b:
                        pe.wait_ge(s.sub_done, b)
                    for t in range(HT):
                        tok = (b * HT + t) * P
                        for k in range(KT):
                            mm = pe.matmul(score_ps[:, t, 0:M], env.xT[:, k, tok:tok + P], qkT[:, k, b * M:(b + 1) * M],
                                           start=(k == 0), stop=(k == KT - 1))
                    mm.then_inc(s.score_ready, 1)
                for b in range(NB):
                    pe.wait_ge(s.prob_done, b + 1)
                    if b:
                        pe.wait_ge(s.turned_kept, b)
                    for t in range(HT):
                        mm = pe.transpose(turn_ps[0:M, t // (HT // 2), t % (HT // 2), :], pr[:, b, t, :], env.ident[:, :])
                    mm.then_inc(s.turned, 1)
                    pe.wait_ge(s.turned_kept, b + 1)
                    pe.wait_ge(s.v_kept, 1)
                    for t in range(HT):
                        i = b * HT + t
                        if i >= 2:
                            pe.wait_ge(s.out_kept, i - 1)
                        pe.matmul(out_ps[:, i % 2, 0:D], prT[:, b, t, :], v[:, b, :], start=True, stop=True)\
                          .then_inc(s.out_ready, 1)

            @block.scalar
            def _(act):
                for b in range(NB):
                    act.wait_ge(s.sub_done, b + 1)
                    act.activation(pr[:, b], sc[:, :, :], ACT.Exp, scale=scale).then_inc(s.exp_done, 1)
                for i in range(NT):
                    act.wait_ge(s.out_ready, i + 1)
                    act.activation(o[:, i, :], out_ps[:, i % 2, 0:D], ACT.Copy).then_inc(s.out_kept, 1)

            @block.vector
            def _(dve):
                dve.wait_ge(s.loaded, 96)
                dve.tensor_scalar(keep[:, :], mask_i[:, :], 0, None, ALU.not_equal).then_inc(s.kept, 1)
                dve.wait_ge(s.key_ready, 1)
                dve.tensor_copy(keyT[:, :, :], small_ps[:, :, 0:NK]).then_inc(s.key_kept, 1)
                dve.wait_ge(s.qk_ready, 1)
                dve.tensor_copy(qkT[:, :, :], small_ps[:, :, 0:NK]).then_inc(s.qk_kept, 1)
                dve.wait_ge(s.v_ready, 1)
                dve.wait_ge(s.kept, 1)
                dve.tensor_scalar(v[:, :, :], small_ps[0:M, :, 0:D], keep[:, 0:1], None, ALU.mult).then_inc(s.v_kept, 1)
                for b in range(NB):
                    dve.wait_ge(s.score_ready, b + 1)
                    dve.tensor_reduce(rowmax[:, b, :], score_ps[:, :, 0:M], AX.X, ALU.max).then_inc(s.max_done, 1)
                    dve.wait_ge(s.max_done, b + 1)
                    if b:
                        dve.wait_ge(s.exp_done, b)
                    dve.tensor_tensor(sc[:, :, :], score_ps[:, :, 0:M], last(rowmax[:, b, :], M), ALU.subtract)\
                       .then_inc(s.sub_done, 1)
                for b in range(NB):
                    dve.wait_ge(s.exp_done, b + 1)
                    dve.tensor_reduce(rowsum[:, b, :], pr[:, b], AX.X, ALU.add).then_inc(s.sum_done, 1)
                    dve.wait_ge(s.sum_done, b + 1)
                    dve.reciprocal(inv[:, b, :], rowsum[:, b, :]).then_inc(s.inv_done, 1)
                    dve.wait_ge(s.inv_done, b + 1)
                    dve.tensor_tensor(pr[:, b], pr[:, b], last(inv[:, b, :], M), ALU.mult).then_inc(s.prob_done, 1)
                    dve.wait_ge(s.turned, b + 1)
                    dve.tensor_copy(prT[:, b].rearrange("m t p -> m (t p)"),
                                    turn_ps[0:M].rearrange("m a t p -> m (a t p)")).then_inc(s.turned_kept, 1)

        J = S // D

        def proj(pe, n, out):
            b, half = n // 2, n % 2
            for m in range(KT):
                for j in range(J):
                    for k in range(KT):
                        mm = pe.matmul(out[:, m, j:CH:J], projT[:, k, m * P:(m + 1) * P],
                                       o[:, b * HT + KT * j + k, half * P:(half + 1) * P],
                                       start=(j == 0 and k == 0), stop=(j == J - 1 and k == KT - 1), skip_group_check=True)
            return mm

        residual_norm(nc, env, branch_matmuls=proj, bias=proj_b)


def butterfly_ffn(nc, env, dram):
    F = 1024
    NF = F // P
    NS = 10
    with ExitStack() as st:
        up_w = sbuf(nc, st, "up_w", [P, KT, F])
        up_b = sbuf(nc, st, "up_b", [P, NF])
        conW = sbuf(nc, st, "conW", [P, NF, D])
        y_bias = sbuf(nc, st, "y_bias", [P, KT])
        with ExitStack() as inner:
            down_w = sbuf(nc, inner, "down_w", [P, KT, F])
            brow = sbuf(nc, inner, "brow", [1, F])
            tmp_u = sbuf(nc, inner, "tmp_u", [P, KT, F])
            tmp_d = sbuf(nc, inner, "tmp_d", [P, KT, F])
            tmp_b = sbuf(nc, inner, "tmp_b", [1, F])
            coef_u = sbuf(nc, inner, "coef_u", [P, 2, 2, F])
            coef_d = sbuf(nc, inner, "coef_d", [P, 2, 2, F])
            bias2 = sbuf(nc, inner, "bias2", [P, NF + 2 * KT])
            s = sems(nc, "loaded coef_u0 coef_u1 coef_d0 coef_d1 u_step d_step b_step con_ready con_kept bias_ready bias_kept "
                                "side_bias")
            con_ps = psum(nc, inner, "con_ps", [P, NF, D])
            bias_ps = psum(nc, inner, "bias_ps", [P, NF])
            coef_u_ready, coef_d_ready = (s.coef_u0, s.coef_u1), (s.coef_d0, s.coef_d1)
            block = inner.enter_context(nc.Block())

            def stage(eng, y, tmp, coef, stride, step, n0):
                def pairs(a, i):
                    ap = a.rearrange("p k (n two s) -> p k n two s", two=2, s=stride)[:, :, :, i, :]
                    return ap
                own = coef[:, 0, :].unsqueeze(1).broadcast_to(list(y.shape))
                par = coef[:, 1, :].unsqueeze(1).broadcast_to(list(y.shape))
                for i in range(2):
                    eng.tensor_tensor(pairs(tmp, i), pairs(y, 1 - i), pairs(par, i), ALU.mult).then_inc(step, 1)
                eng.wait_ge(step, n0 + 2)
                eng.tensor_tensor(y, y, own, ALU.mult).then_inc(step, 1)
                eng.wait_ge(step, n0 + 3)
                eng.tensor_tensor(y, y, tmp, ALU.add).then_inc(step, 1)
                eng.wait_ge(step, n0 + 4)
                return n0 + 4

            @block.sync
            def _(sp):
                sp.dma_start(up_w[:, :, :], dram.W_exp.rearrange("(k p) n -> p k n", p=P)).then_inc(s.loaded, 16)
                sp.dma_start(brow[:, :], dram.b_exp.rearrange("(a n) -> a n", a=1)).then_inc(s.loaded, 16)
                sp.dma_start(down_w[:, :, :], dram.W_conT.rearrange("(k p) n -> p k n", p=P)).then_inc(s.loaded, 16)
                sp.dma_start(bias2[:, 0:NF], dram.up_bias).then_inc(s.side_bias, 16)
                sp.dma_start(bias2[:, NF:NF + KT], dram.b_con).then_inc(s.side_bias, 16)
                sp.dma_start(bias2[:, NF + KT:], dram.down_bias).then_inc(s.side_bias, 16)
                for i in range(NS):
                    if i >= 2:
                        sp.wait_ge(s.u_step, 4 * (i - 1))
                        sp.wait_ge(s.b_step, 4 * (i - 1))
                    sp.dma_start(coef_u[:, i % 2], dram.up_coef[i].partition_broadcast(P)).then_inc(coef_u_ready[i % 2], 16)
                    if i >= 2:
                        sp.wait_ge(s.d_step, 4 * (i - 1))
                    sp.dma_start(coef_d[:, i % 2], dram.down_coef[NS - 1 - i].partition_broadcast(P)).then_inc(coef_d_ready[i % 2], 16)

            @block.vector
            def _(dve):
                dve.wait_ge(s.loaded, 48)
                n = nb = 0
                for i in range(NS):
                    dve.wait_ge(coef_u_ready[i % 2], 16 * (i // 2 + 1))
                    n = stage(dve, up_w[:, :, :], tmp_u[:, :, :], coef_u[:, i % 2], 2 ** i, s.u_step, n)
                    nb = stage(dve, brow[:, :].unsqueeze(1), tmp_b[:, :].unsqueeze(1), coef_u[0:1, i % 2], 2 ** i, s.b_step, nb)
                dve.wait_ge(s.side_bias, 48)
                dve.wait_ge(s.bias_ready, 1)
                dve.tensor_tensor(up_b[:, :], bias_ps[:, :], bias2[:, 0:NF], ALU.add).then_inc(s.bias_kept, 1)
                dve.tensor_tensor(y_bias[:, :], bias2[:, NF:NF + KT], bias2[:, NF + KT:], ALU.add).then_inc(s.bias_kept, 1)
                dve.wait_ge(s.con_ready, 1)
                dve.tensor_copy(conW[:, :, :], con_ps[:, :, :]).then_inc(s.con_kept, 1)

            @block.gpsimd
            def _(pool):
                pool.wait_ge(s.loaded, 48)
                n = 0
                for i in range(NS):
                    pool.wait_ge(coef_d_ready[i % 2], 16 * (i // 2 + 1))
                    n = stage(pool, down_w[:, :, :], tmp_d[:, :, :], coef_d[:, i % 2], 2 ** (NS - 1 - i), s.d_step, n)

            @block.tensor
            def _(pe):
                pe.wait_ge(s.b_step, 4 * NS)
                for f in range(NF):
                    mm = pe.matmul(bias_ps[:, f:f + 1], brow[:, f * P:(f + 1) * P], env.ident[0:1, 0:1], start=True, stop=True)
                mm.then_inc(s.bias_ready, 1)
                pe.wait_ge(s.d_step, 4 * NS)
                for f in range(NF):
                    for k in range(KT):
                        mm = pe.transpose(con_ps[:, f, k * P:(k + 1) * P], down_w[:, k, f * P:(f + 1) * P], env.ident[:, :])
                mm.then_inc(s.con_ready, 1)

        y = sbuf(nc, st, "y", [P, KT, T])
        with ExitStack() as inner:
            hid = sbuf(nc, inner, "hid", [P, 2, NF, CH])
            s = sems(nc, "hid_ready gelu_done y_ready y_kept")
            hid_ps = psum(nc, inner, "hid_ps", [P, 4, CH])
            y_ps = psum(nc, inner, "y_ps", [P, 2, KT, CH])
            block = inner.enter_context(nc.Block())

            @block.tensor
            def _(pe):
                for n in range(NCH + 1):
                    if n < NCH:
                        for f in range(NF):
                            i = n * NF + f
                            if i >= 4:
                                pe.wait_ge(s.gelu_done, i - 3)
                            for k in range(KT):
                                mm = pe.matmul(hid_ps[:, i % 4, :], up_w[:, k, f * P:(f + 1) * P],
                                               env.xT[:, k, n * CH:(n + 1) * CH], start=(k == 0), stop=(k == KT - 1))
                            mm.then_inc(s.hid_ready, 1)
                    if n >= 1:
                        c = n - 1
                        pe.wait_ge(s.gelu_done, (c + 1) * NF)
                        if c >= 2:
                            pe.wait_ge(s.y_kept, c - 1)
                        for m in range(KT):
                            for f in range(NF):
                                mm = pe.matmul(y_ps[:, c % 2, m, :], conW[:, f, m * P:(m + 1) * P], hid[:, c % 2, f, :],
                                               start=(f == 0), stop=(f == NF - 1))
                        mm.then_inc(s.y_ready, 1)

            @block.scalar
            def _(act):
                for i in range(NCH * NF):
                    n, f = i // NF, i % NF
                    act.wait_ge(s.hid_ready, i + 1)
                    if n >= 2:
                        act.wait_ge(s.y_ready, n - 1)
                    act.activation(hid[:, n % 2, f, :], hid_ps[:, i % 4, :], ACT.Gelu, bias=up_b[:, f:f + 1])\
                       .then_inc(s.gelu_done, 1)

            @block.vector
            def _(dve):
                for n in range(NCH):
                    dve.wait_ge(s.y_ready, n + 1)
                    dve.tensor_copy(y[:, :, n * CH:(n + 1) * CH], y_ps[:, n % 2]).then_inc(s.y_kept, 1)

        residual_norm(nc, env, branch=y, bias=y_bias)


def steps_of(kind, half):
    lo, hi = half * CH, (half + 1) * CH
    if kind == "full":
        return [(j, lo, hi) for j in range(S // P)]
    if kind == "causal":
        return [(j, max(lo, j * P), hi) for j in range(hi // P)]
    if kind == "window":
        tiles = [(j, max(lo, j * P), min(hi, j * P + WINQ)) for j in range(S // P)]
        return [t for t in tiles if t[1] < t[2]]
    return [(0, lo, hi)]


def max_pieces(kind):
    out = []
    for t in range(S // P):
        if kind in ("full", "causal"):
            keys = S if kind == "full" else (t + 1) * P
            out += [(t, h, 1, k, min(CH, keys - k), k // CH) for h in range(HU) for k in range(0, keys, CH)]
        elif kind == "window":
            first = max(0, t * P - WIN)
            out += [(t, h, 2, first, (t + 1) * P - first, 0) for h in range(0, HU, 2)]
        else:
            out.append((t, 0, HU, 0, M, 0))
    return out


def attention(nc, env, dram, kind, scale, mask=None):
    cross = kind in ("cross", "xcausal", "xmask")
    nk = M if cross else S
    nkp = M + 1 if cross else S
    kp = M if cross else P
    nkt = 1 if cross else S // P
    halves = S // CH
    steps = [(half, i == 0, i == len(steps_of(kind, half)) - 1, *t)
             for half in range(halves) for i, t in enumerate(steps_of(kind, half))]
    nsteps = len(steps)
    pieces = max_pieces(kind)
    NP = max(p[5] for p in pieces) + 1
    per_unit = len(pieces) + 1
    units = [(b, u) for b in range(NB) for u in range(NU)]
    piece_steps = range(0, 1) if cross else range(nsteps // 5, nsteps - 2)
    turn_step = piece_steps[-1] + 1

    def pieces_at(i, spot):
        if i not in piece_steps:
            return range(0)
        n, i = 4 * len(piece_steps), 4 * piece_steps.index(i) + spot
        return range(i * len(pieces) // n, (i + 1) * len(pieces) // n)

    MAXB = 3
    RING = 2 if kind == "window" else 4
    SLOTS = {"window": 3}.get(kind, 4 if cross else 2)
    LEAD = 2 if cross else 1
    items = []
    for b in range(NB):
        for m in range(KT):
            items += [(b, "q", m, c * CH, CH) for c in range(S // CH)]
            items += [(b, "k", m, 0, M)] if cross else [(b, "k", m, c * CH, CH) for c in range(S // CH)]
        items += [(b, "v", j, 0, 0) for j in range(nkt)]
    qk_items = [i for i, item in enumerate(items) if item[1] != "v"]

    with ExitStack() as st:
        wo = sbuf(nc, st, "wo", [P, NU, D])
        bo = sbuf(nc, st, "bo", [P, KT])
        o = sbuf(nc, st, "o", [P, NU, T])
        with ExitStack() as inner:
            wq = sbuf(nc, inner, "wq", [P, KT, D])
            wk = sbuf(nc, inner, "wk", [P, KT, D])
            wv = sbuf(nc, inner, "wv", [P, KT, D])
            bq = sbuf(nc, inner, "bq", [P, KT])
            bk = sbuf(nc, inner, "bk", [P, KT])
            bv = sbuf(nc, inner, "bv", [P, D]) if "bv" in dram else None
            parts = sbuf(nc, inner, "parts", [P, RING, 2, CH], F32R)
            v = sbuf(nc, inner, "v", [kp, NB, nkt, H, 2 * HD])
            qst = sbuf(nc, inner, "qst", [P, SLOTS, HU, S], F32R)
            kst = sbuf(nc, inner, "kst", [P, SLOTS, HU, nkp], F32R)
            prob = sbuf(nc, inner, "prob", [kp, 2, HU, max(hi - lo for _, _, _, _, lo, hi in steps)])
            cmax = sbuf(nc, inner, "cmax", [P, HU, S // P, NP])
            negc = sbuf(nc, inner, "negc", [P, HU * S // P])
            crow = sbuf(nc, inner, "crow", [HU * S // P, P], F32R)
            byq = sbuf(nc, inner, "byq", [P, CH])
            inv = sbuf(nc, inner, "inv", [P, CH // (2 * HD)])
            s = sems(nc, "loaded biased cleared proj_ready hi_kept kept written0 written1 written2 written3 stacked0 stacked1 stacked2 stacked3 "
                                "max_ready max_done neg_ready c_loaded s_ready exp_done av_done turned inverted divided evacuated")
            max_ps = psum(nc, inner, "max_ps", [P, MAXB, CH])
            st_ps = psum(nc, inner, "st_ps", [P, 2, 2, CH])
            acc = psum(nc, inner, "acc", [P, CH])
            block = inner.enter_context(nc.Block())
            src = env.ctxT if cross else env.xT
            stacked = (s.stacked0, s.stacked1, s.stacked2, s.stacked3)
            written = (s.written0, s.written1, s.written2, s.written3)[:RING]
            PARTS = 4 * 2 + 1
            nload = 4 + sum(n in dram for n in ("bq", "bk", "bo", "bv"))
            nbias = sum(n not in dram for n in ("bq", "bk", "bo"))
            CLEARED = 6

            def proj_ps(i):
                return st_ps[:, i % 4 // 2, i % 2, :]

            @block.sync
            def _(sp):
                for t, n in ((wq, "Wq"), (wk, "Wk"), (wv, "Wv")):
                    sp.dma_start(t[:, :, :], dram[n].rearrange("(k p) n -> p k n", p=P)).then_inc(s.loaded, 16)
                for t, n in ((bq, "bq"), (bk, "bk"), (bo, "bo")):
                    if n in dram:
                        sp.dma_start(t[:, :], dram[n]).then_inc(s.loaded, 16)
                if "bv" in dram:
                    sp.dma_start(bv[:, :], dram["bv"].partition_broadcast(P)).then_inc(s.loaded, 16)
                sp.dma_start(wo[:, :, :], dram["Wo"].rearrange("(g p) n -> p g n", p=P)).then_inc(s.loaded, 16)

                def store(batch):
                    for j, i in enumerate(qk_items):
                        b, what, m, c, n = items[i]
                        if b == batch:
                            to, n = (env.q_dram, n) if what == "q" else (env.k_dram, n + n % 2)
                            sp.wait_ge(s.kept, i + 1)
                            sp.dma_start(to[b, :, m * P:(m + 1) * P, c:c + n].rearrange("a p n -> p a n"),
                                         parts[:, j % RING, :, 0:n].bitcast(F32)).then_inc(written[j % RING], 16)

                def stack(g):
                    b, u = units[g]
                    if g >= SLOTS:
                        sp.wait_ge(s.av_done, nsteps * (g - SLOTS + 1))
                    if u == 0:
                        for r in range(RING):
                            sp.wait_ge(written[r], 16 * len([j for j, i in enumerate(qk_items) if j % RING == r and items[i][0] <= b]))
                    rows = slice(u * HU * HD, (u + 1) * HU * HD)
                    for part in range(2):
                        for twice in range(2):
                            d = slice((2 * part + twice) * HD, (2 * part + twice + 1) * HD)
                            sp.dma_start(qst[d, g % SLOTS, :, :].bitcast(F32),
                                         env.q_dram[b, part, rows, :].rearrange("(h d) n -> d h n", d=HD)).then_inc(stacked[g % SLOTS], 16)
                    for twice in range(2):
                        for part in range(2):
                            d = slice((2 * twice + part) * HD, (2 * twice + part + 1) * HD)
                            sp.dma_start(kst[d, g % SLOTS, :, :].bitcast(F32),
                                         env.k_dram[b, part, rows, 0:nkp].rearrange("(h d) n -> d h n", d=HD)).then_inc(stacked[g % SLOTS], 16)
                    sp.dma_start(qst[STACK:STACK + 1, g % SLOTS, :, :].bitcast(F32),
                                 qst[P - 1:P, g % SLOTS, :, :].bitcast(F32)).then_inc(stacked[g % SLOTS], 16)

                store(0)
                sp.wait_ge(s.cleared, CLEARED)
                stack(0)
                stack(1)
                store(1)
                for g in range(2, len(units)):
                    stack(g)

            @block.gpsimd
            def _(pool):
                for t, n in ((bq, "bq"), (bk, "bk"), (bo, "bo")):
                    if n not in dram:
                        pool.memset(t[:, :], 0.0).then_inc(s.biased, 1)
                pool.memset(parts[:, :, :, :].bitcast(F32), 0.0).then_inc(s.cleared, 1)
                pool.memset(v[:, :, :, :, :], 1.0).then_inc(s.cleared, 1)
                pool.memset(kst[:, :, :, :].bitcast(F32), 0.0).then_inc(s.cleared, 1)
                pool.memset(qst[:, :, :, :].bitcast(F32), 0.0).then_inc(s.cleared, 1)
                pool.memset(cmax[:, :, :, :], -3e38).then_inc(s.cleared, 1)
                pool.wait_ge(s.cleared, CLEARED - 1)
                pool.memset(kst[STACK:STACK + 1, :, :, :].bitcast(F32), 1.0).then_inc(s.cleared, 1)
                pool.wait_ge(s.cleared, CLEARED)
                for g in range(len(units)):
                    pool.wait_ge(s.max_done, per_unit * (g + 1))
                    pool.dma_start(qst[STACK:STACK + 1, g % SLOTS, :, :].bitcast(F32), crow[:, :].bitcast(F32)).then_inc(s.c_loaded, 16)

            @block.tensor
            def _(pe):
                def piece(gu, i):
                    b = units[gu][0]
                    t, h, nh, k0, n, _ = pieces[i]
                    g = gu * per_unit + i
                    if g >= MAXB:
                        pe.wait_ge(s.max_done, g - MAXB + 1)
                    if i == 0:
                        pe.wait_ge(stacked[gu % SLOTS], 16 * PARTS * (gu // SLOTS + 1))
                    masked = (kind == "causal" and k0 + n == (t + 1) * P) or kind in ("window", "xmask") or \
                             (kind == "xcausal" and t == 0)
                    for a in range(nh):
                        at = a * (CH // nh)
                        ne = n + n % 2
                        mm = pe.matmul(max_ps[:, g % MAXB, at:at + ne], qst[:, gu % SLOTS, h + a, t * P:(t + 1) * P],
                                       kst[:, gu % SLOTS, h + a, k0:k0 + ne], start=(a == 0), stop=(not masked),
                                       skip_group_check=True)
                        if kind == "causal" and masked:
                            mm = pe.matmul(max_ps[:, g % MAXB, n - P:n], env.identb[:, :], env.causal_qk[:, :],
                                           start=False, stop=True, skip_group_check=True)
                        elif kind == "window":
                            mm = pe.matmul(max_ps[:, g % MAXB, at:at + n], env.identb[:, :], env.window_qk[:, WINQ - n:],
                                           start=False, stop=True, skip_group_check=True)
                        elif masked:
                            rows = env.causal_qk[:, 0:M] if kind == "xcausal" else mask.qk[:, b, t, :]
                            mm = pe.matmul(max_ps[:, g % MAXB, at:at + n], env.identb[:, :], rows,
                                           start=False, stop=True, skip_group_check=True)
                    mm.then_inc(s.max_ready, 1)

                def turn(gu):
                    g = gu * per_unit + len(pieces)
                    pe.wait_ge(s.max_done, g - MAXB + 1)
                    pe.wait_ge(s.neg_ready, gu + 1)
                    pe.transpose(max_ps[0:HU * S // P, g % MAXB, 0:P], negc[:, :], env.ident[:, :]).then_inc(s.max_ready, 1)

                def scores(gu, i):
                    b = units[gu][0]
                    half, _, _, j, lo, hi = steps[i]
                    g = gu * nsteps + i
                    masked = (kind == "causal" and lo == j * P) or kind in ("window", "xmask") or \
                             (kind == "xcausal" and half == 0)
                    if g == 0:
                        pe.wait_ge(s.kept, len(items))
                    for p in range(2):
                        if p and gu + LEAD < len(units):
                            for n in pieces_at(i, 0):
                                piece(gu + LEAD, n)
                        if g >= 1:
                            pe.wait_ge(s.exp_done, 2 * (g - 1) + p + 1)
                        for a in range(2):
                            h = 2 * p + a
                            out = st_ps[0:kp, p, a, 0:hi - lo]
                            mm = pe.matmul(out, kst[:, gu % SLOTS, h, j * P:j * P + kp], qst[:, gu % SLOTS, h, lo:hi],
                                           start=True, stop=(not masked), skip_group_check=True)
                            if masked and kind in ("causal", "xcausal"):
                                mm = pe.matmul(out[:, 0:P], env.identb[:, 0:kp], env.causal_kq[:, :],
                                               start=False, stop=True, skip_group_check=True)
                            elif kind == "window":
                                mm = pe.matmul(out, env.identb[:, :], env.window_kq[:, lo - j * P:hi - j * P],
                                               start=False, stop=True, skip_group_check=True)
                            elif masked:
                                mm = pe.matmul(out, env.identb[0:M, 0:M], mask.kq[:, b, lo:hi],
                                               start=False, stop=True, skip_group_check=True)
                        mm.then_inc(s.s_ready, 1)

                def values(gu, i):
                    b, u = units[gu]
                    half, first, final, j, lo, hi = steps[i]
                    g = gu * nsteps + i
                    hc = gu * halves + half
                    pe.wait_ge(s.exp_done, 2 * (g + 1))
                    if first and hc >= 1:
                        pe.wait_ge(s.turned, hc)
                    for a in range(HU):
                        if a == 2 and gu + LEAD < len(units):
                            for n in pieces_at(i + 1, 2):
                                piece(gu + LEAD, n)
                        mm = pe.matmul(acc[32 * a:32 * a + 32, lo - half * CH:hi - half * CH],
                                       v[:, b, j, u * HU + a, :], prob[:, g % 2, a, 0:hi - lo],
                                       start=first, stop=final, skip_group_check=True)
                    mm.then_inc(s.av_done, 1)

                pe.wait_ge(s.loaded, 16 * nload)
                for i, (b, what, m, c, n) in enumerate(items):
                    if i >= 4:
                        pe.wait_ge(s.kept, i - 3)
                    for k in range(KT):
                        if what == "q":
                            mm = pe.matmul(proj_ps(i)[:, 0:n], wq[:, k, m * P:(m + 1) * P],
                                           env.xT[:, k, b * S + c:b * S + c + n], start=(k == 0), stop=(k == KT - 1))
                        elif what == "k":
                            mm = pe.matmul(proj_ps(i)[:, 0:n], wk[:, k, m * P:(m + 1) * P],
                                           src[:, k, b * nk + c:b * nk + c + n], start=(k == 0), stop=(k == KT - 1))
                        else:
                            mm = pe.matmul(proj_ps(i)[0:kp, 0:D], src[:, k, b * nk + m * kp:b * nk + (m + 1) * kp],
                                           wv[:, k, :], start=(k == 0), stop=(k == KT - 1))
                    mm.then_inc(s.proj_ready, 1)
                pe.wait_ge(s.cleared, CLEARED)
                for gu in range(LEAD):
                    for i in range(len(pieces)):
                        piece(gu, i)
                    turn(gu)
                for gu in range(len(units)):
                    pe.wait_ge(s.c_loaded, 16 * (gu + 1))
                    for i in range(nsteps):
                        scores(gu, i)
                        if gu + LEAD < len(units):
                            for n in pieces_at(i, 1):
                                piece(gu + LEAD, n)
                        if i:
                            values(gu, i - 1)
                        if gu + LEAD < len(units):
                            for n in pieces_at(i, 3) if i else (*pieces_at(i, 2), *pieces_at(i, 3)):
                                piece(gu + LEAD, n)
                            if i == turn_step:
                                turn(gu + LEAD)
                    values(gu, nsteps - 1)

            @block.scalar
            def _(act):
                act.wait_ge(s.loaded, 16 * nload)
                if nbias:
                    act.wait_ge(s.biased, nbias)
                act.wait_ge(s.cleared, 1)
                for j, i in enumerate(qk_items):
                    b, what, m, c, n = items[i]
                    bias = bq if what == "q" else bk
                    if j >= RING:
                        act.wait_ge(written[j % RING], 16 * (j // RING))
                    act.wait_ge(s.proj_ready, i + 1)
                    act.activation(parts[:, j % RING, 0, 0:n], proj_ps(i)[:, 0:n], ACT.Identity, bias=bias[:, m:m + 1])\
                       .then_inc(s.hi_kept, 1)
                for gu in range(len(units)):
                    for i, (_, _, _, _, lo, hi) in enumerate(steps):
                        g = gu * nsteps + i
                        for p in range(2):
                            if g >= 2:
                                act.wait_ge(s.av_done, g - 1)
                            act.wait_ge(s.s_ready, 2 * g + p + 1)
                            act.activation(prob[:, g % 2, 2 * p:2 * p + 2, 0:hi - lo], st_ps[0:kp, p, :, 0:hi - lo],
                                           ACT.Exp, scale=scale).then_inc(s.exp_done, 1)

            @block.vector
            def _(dve):
                def piece(gu, i):
                    t, h, nh, _, n, part = pieces[i]
                    g = gu * per_unit + i
                    dve.wait_ge(s.max_ready, g + 1)
                    if i == 0 and gu >= 1:
                        dve.wait_ge(s.neg_ready, gu)
                    dve.tensor_reduce(cmax[:, h:h + nh, t, part],
                                      max_ps[:, g % MAXB, :].rearrange("p (a n) -> p a n", a=nh)[:, :, 0:n],
                                      AX.X, ALU.max).then_inc(s.max_done, 1)

                def turn(gu):
                    g = gu * per_unit + len(pieces)
                    dve.wait_ge(s.max_done, g)
                    if gu >= 1:
                        dve.wait_ge(s.max_ready, g - per_unit + 1)
                    dve.tensor_reduce(negc[:, :], cmax[:, :, :, :].rearrange("p h t a -> p (h t) a"), AX.X, ALU.max,
                                      negate=True).then_inc(s.neg_ready, 1)
                    dve.wait_ge(s.max_ready, g + 1)
                    if gu >= 1:
                        dve.wait_ge(s.c_loaded, 16 * gu)
                    dve.tensor_copy(crow[:, :], max_ps[0:HU * S // P, g % MAXB, 0:P]).then_inc(s.max_done, 1)

                def evacuate(gu, half, step):
                    b, u = units[gu]
                    hc = gu * halves + half
                    dve.wait_ge(s.av_done, gu * nsteps + step + 1)
                    if hc >= 1:
                        dve.wait_ge(s.evacuated, hc)
                    dve.transpose(byq[:, :], acc[:, :]).then_inc(s.turned, 1)
                    dve.wait_ge(s.turned, hc + 1)
                    blocks = byq[:, :].rearrange("p (n r) -> p n r", r=2 * HD)
                    dve.reciprocal(inv[:, :], blocks[:, :, HD]).then_inc(s.inverted, 1)
                    dve.wait_ge(s.inverted, hc + 1)
                    dve.tensor_tensor(blocks, blocks, last(inv[:, :], 2 * HD), ALU.mult).then_inc(s.divided, 1)
                    dve.wait_ge(s.divided, hc + 1)
                    dve.transpose(o[:, u, b * S + half * CH:b * S + (half + 1) * CH], byq[:, :]).then_inc(s.evacuated, 1)

                dve.wait_ge(s.loaded, 16 * nload)
                if nbias:
                    dve.wait_ge(s.biased, nbias)
                dve.wait_ge(s.cleared, 2)
                j = 0
                for i, (b, what, m, c, n) in enumerate(items):
                    if what == "v":
                        dve.wait_ge(s.proj_ready, i + 1)
                        to, product = v[:, b, m, :, 0:HD], proj_ps(i)[0:kp, 0:D].rearrange("p (h d) -> p h d", h=H)
                        if bv is None:
                            dve.tensor_copy(to, product).then_inc(s.kept, 1)
                        else:
                            dve.tensor_tensor(to, product, bv[0:kp, :].rearrange("p (h d) -> p h d", h=H), ALU.add)\
                               .then_inc(s.kept, 1)
                    else:
                        bias = bq if what == "q" else bk
                        dve.wait_ge(s.hi_kept, j + 1)
                        dve.scalar_tensor_tensor(out=parts[:, j % RING, 1, 0:n], in0=proj_ps(i)[:, 0:n], scalar=bias[:, m:m + 1],
                                                 in1=parts[:, j % RING, 0, 0:n].bitcast(F32), op0=ALU.add, op1=ALU.subtract)\
                           .then_inc(s.kept, 1)
                        j += 1
                dve.wait_ge(s.cleared, CLEARED)
                for gu in range(LEAD):
                    for i in range(len(pieces)):
                        piece(gu, i)
                    turn(gu)
                for gu in range(len(units)):
                    for i in range(nsteps):
                        for spot in range(4):
                            if spot == 3 and i and steps[i - 1][2]:
                                evacuate(gu, steps[i - 1][0], i - 1)
                            if gu + LEAD < len(units):
                                for n in pieces_at(i, spot):
                                    piece(gu + LEAD, n)
                        if gu + LEAD < len(units) and i == turn_step:
                            turn(gu + LEAD)
                    evacuate(gu, steps[-1][0], nsteps - 1)

        def project(pe, n, out):
            for m in range(KT):
                for g in range(NU):
                    mm = pe.matmul(out[:, m, :], wo[:, g, m * P:(m + 1) * P], o[:, g, n * CH:(n + 1) * CH],
                                   start=(g == 0), stop=(g == NU - 1))
            return mm

        residual_norm(nc, env, branch_matmuls=project, bias=bo)


def mask_tiles(nc, st, env, m_qk, m_kq, cols, dt, op, value, name):
    t = named(qk=sbuf(nc, st, name + "_qk", [P, NB, S // P, M], BF16), kq=sbuf(nc, st, name + "_kq", [M, NB, S], BF16))
    with ExitStack() as inner:
        raw_qk = sbuf(nc, inner, "raw_qk", [P, NB, S // P, M], dt)
        raw_kq = sbuf(nc, inner, "raw_kq", [M, NB, cols], dt)
        s = sems(nc, "loaded")
        block = inner.enter_context(nc.Block())

        @block.sync
        def _(sp):
            for b in range(NB):
                sp.dma_start(raw_qk[:, b], m_qk(b)).then_inc(s.loaded, 16)
                sp.dma_start(raw_kq[:, b], m_kq(b)).then_inc(s.loaded, 16)

        @block.vector
        def _(dve):
            dve.wait_ge(s.loaded, 64)
            for b in range(NB):
                dve.tensor_scalar(t.qk[:, b], raw_qk[:, b], 0, value, op, ALU.mult)
                dve.tensor_scalar(t.kq[:, b], raw_kq[:, b].broadcast_to([M, S]), 0, value, op, ALU.mult)
    return t


def moe(nc, env, dram, E, F, topk, glu, score, shared, per=1):
    NF = per * F // P
    NG = (E + shared) // per
    CT = 1024
    HV = CT // CH
    peel = NG - 2 * ((NG - 2) // 2)
    biased = "b1" in dram
    NW = 2 if glu else 1
    NWE = NW * KT * per * F + NF * D
    R = 2 if glu else 4
    with ExitStack() as st:
        y = sbuf(nc, st, "y", [P, KT, T])
        y_bias = sbuf(nc, st, "y_bias", [P, KT])
        with ExitStack() as inner:
            x_hi = sbuf(nc, inner, "x_hi", [P, KT, T], F32R)
            x_lo = sbuf(nc, inner, "x_lo", [P, KT, T], F32R)
            gT = sbuf(nc, inner, "gT", [E, T])
            b2 = sbuf(nc, inner, "b2", [E, D])
            wr = sbuf(nc, inner, "wr", [P, KT, E])
            rb = sbuf(nc, inner, "rb", [P, E])
            rs = sbuf(nc, inner, "rs", [P, 1])
            sc = sbuf(nc, inner, "sc", [P, NT, E])
            rowmax = sbuf(nc, inner, "rowmax", [P, NT])
            before = sbuf(nc, inner, "before", [P, E, E])
            rank = sbuf(nc, inner, "rank", [P, NT, E])
            above = sbuf(nc, inner, "above", [P, NT, E])
            total = sbuf(nc, inner, "total", [P, NT])
            raw = sbuf(nc, inner, "raw", [P, 2, NWE])
            w_hi = sbuf(nc, inner, "w_hi", [P, 2, NWE], F32R)
            w_lo = sbuf(nc, inner, "w_lo", [P, 2, NWE], F32R)
            gate = sbuf(nc, inner, "gate", [P, 2, per, CT])
            b1 = sbuf(nc, inner, "b1", [P, 2, NF])
            lift = sbuf(nc, inner, "lift", [P, 4, CH])
            hid_hi = sbuf(nc, inner, "hid_hi", [P, HV, NF, CH], F32R)
            hid_lo = sbuf(nc, inner, "hid_lo", [P, HV, NF, CH], F32R)
            beats = y[:, :, :].rearrange("p k t -> p (k t)")[:, 0:NT * E * E].rearrange("p (t a b) -> p t a b", a=E, b=E)
            s = sems(nc, "loaded ones_ready before_ready x_hi_ready x_lo_ready logit_ready chain acted gate_ready turned kept stored "
                         "w_ready0 w_ready1 g_ready0 g_ready1 w_hi_done w_split hid_ready hid_free act_ready gated hid_hi_done "
                         "mul_done y_done chunk_done")
            hid_ps = psum(nc, inner, "hid_ps", [P, R, NW, CH])
            y_ps = psum(nc, inner, "y_ps", [P, HV, KT, CH])
            log_ps = hid_ps[:, 0, 0, 0:NT * E].rearrange("p (t e) -> p t e", e=E)
            gT_ps = y_ps[0:E].rearrange("e h m n -> e (h m n)")
            block = inner.enter_context(nc.Block())
            loads = 1 + ("router_b" in dram) + ("route_scale" in dram) + ("b2" in dram) + ("bs2" in dram)
            w_ready = (s.w_ready0, s.w_ready1)
            g_ready = (s.g_ready0, s.g_ready1)
            gates = dram["gates"].rearrange("(g e) t -> g e t", e=per)

            def up_w(w, slot, a, kk, f):
                at = (a * KT + kk) * per * F + f * P
                return w[:, slot, at:at + P]

            def down_w(w, slot, f, m):
                at = NW * KT * per * F + f * D + m * P
                return w[:, slot, at:at + P]

            def bank(slot, half, f, ring):
                return ((slot * HV + half) * NF + f) % ring

            def turns(eng, first, turn):
                for i in range(peel):
                    turn(first + i, i, (first + i) % 2, (first + i) // 2 + 1)
                if NG > peel:
                    with eng.Fori(0, (NG - peel) // 2) as i:
                        for j in range(2):
                            k = i * 2 + (first + peel + j)
                            turn(k, i * 2 + (peel + j), (first + peel + j) % 2, i + ((first + peel + j) // 2 + 1))

            @block.sync
            def _(sp):
                sp.dma_start(wr[:, :, :], dram["Wr"].rearrange("(k p) n -> p k n", p=P)).then_inc(s.loaded, 16)
                if "router_b" in dram:
                    sp.dma_start(rb[:, :], dram["router_b"].partition_broadcast(P)).then_inc(s.loaded, 16)
                if "route_scale" in dram:
                    sp.dma_start(rs[:, :], dram["route_scale"].partition_broadcast(P)).then_inc(s.loaded, 16)
                if "b2" in dram:
                    sp.dma_start(b2[:, :], dram["b2"]).then_inc(s.loaded, 16)
                if "bs2" in dram:
                    sp.dma_start(y_bias[:, :], dram["bs2"]).then_inc(s.loaded, 16)
                opened = [False]

                for c in range(T // CT):
                    def turn(k, e, slot, uses):
                        sp.wait_ge(s.w_split, k + 1)
                        for a, n in enumerate(("W1", "Wu")[:NW]):
                            to = raw[:, slot, a * KT * per * F:(a + 1) * KT * per * F].rearrange("p (k f) -> p k f", k=KT)
                            sp.dma_start(to, dram[n][e].rearrange("(k p) f -> p k f", p=P)).then_inc(w_ready[slot], 16)
                        to = raw[:, slot, NW * KT * per * F:].rearrange("p (f n) -> p f n", n=D)
                        sp.dma_start(to, dram["W2"][e].rearrange("(f p) n -> p f n", p=P)).then_inc(w_ready[slot], 16)
                        if not opened[0]:
                            if shared:
                                sp.dma_start(dram["gates"][0].rearrange("(p n) -> p n", p=P), env.ones[:, 0:T // P]).then_inc(s.stored, 16)
                            sp.wait_ge(s.kept, 1)
                            sp.dma_start(dram["gates"][shared:, :], gT[:, :]).then_inc(s.stored, 16)
                            sp.wait_ge(s.stored, 16 * (1 + shared))
                            opened[0] = True
                        sp.wait_ge(s.y_done, k * HV)
                        if biased:
                            sp.dma_start(b1[:, slot], dram["b1"][e]).then_inc(g_ready[slot], 16)
                        sp.dma_start(gate[:, slot], gates[e, :, c * CT:(c + 1) * CT].partition_broadcast(P)).then_inc(g_ready[slot], 16)
                    turns(sp, c * NG, turn)

            @block.gpsimd
            def _(pool):
                pool.sem_inc(s.w_split, 2)
                pool.sem_inc(s.y_done, 2)
                pool.sem_inc(s.hid_free if glu else s.act_ready, R)
                pool.sem_inc(s.mul_done, 4)
                pool.memset(before[:, :, :], 1.0).then_inc(s.ones_ready, 1)
                pool.wait_ge(s.ones_ready, 1)
                pool.affine_select(out=before[:, :, :], in_=before[:, :, :], compare_op=ALU.is_gt, fill=0.0, base=0,
                                   pattern=[[1, E], [-1, E]], channel_multiplier=0).then_inc(s.before_ready, 1)
                pool.wait_ge(s.before_ready, 1)
                for c in range(T // CT):
                    def turn(k, e, slot, uses):
                        pool.wait_ge(w_ready[slot], uses * (16 * (NW + 1)))
                        pool.wait_ge(s.y_done, k * HV)
                        pool.tensor_tensor(w_hi[:, slot, :], raw[:, slot, :], env.ones[:, 0:1].broadcast_to([P, NWE]),
                                           ALU.mult).then_inc(s.w_hi_done, 1)
                        pool.wait_ge(s.w_hi_done, k + 1)
                        pool.tensor_tensor(w_lo[:, slot, :], raw[:, slot, :], w_hi[:, slot, :].bitcast(F32), ALU.subtract)\
                            .then_inc(s.w_split, 1)
                        pool.wait_ge(s.w_split, k + 3)
                    turns(pool, c * NG, turn)

            @block.tensor
            def _(pe):
                pe.wait_ge(s.loaded, 16 * loads)
                for t in range(NT):
                    for k in range(KT):
                        mm = pe.matmul(log_ps[:, t, :], env.xT[:, k, t * P:(t + 1) * P], wr[:, k, :],
                                       start=(k == 0), stop=(k == KT - 1))
                mm.then_inc(s.logit_ready, 1)
                pe.wait_ge(s.gate_ready, 1)
                for t in range(NT):
                    mm = pe.transpose(gT_ps[:, t * P:(t + 1) * P], sc[:, t, :], env.ident[:, :])
                mm.then_inc(s.turned, 1)
                pe.wait_ge(s.x_lo_ready, KT)
                pe.wait_ge(s.kept, 1)
                for c in range(T // CT):
                    def hidden(k, slot, half):
                        for f in range(NF):
                            n = (k * HV + half) * NF + f
                            pe.wait_ge(s.hid_free if glu else s.act_ready, n + 1)
                            for a in range(NW):
                                for kk in range(KT):
                                    for i, (w, x) in enumerate(((w_hi, x_hi), (w_hi, x_lo), (w_lo, x_hi))):
                                        mm = pe.matmul(hid_ps[:, bank(slot, half, f, R), a, :], up_w(w, slot, a, kk, f),
                                                       x[:, kk, c * CT + half * CH:c * CT + (half + 1) * CH],
                                                       start=(kk == 0 and i == 0), stop=(kk == KT - 1 and i == 2))
                            mm.then_inc(s.hid_ready, 1)

                    def down(k, slot, half, opens, closes):
                        pe.wait_ge(s.mul_done, (k * HV + half) * NF + (NF + 4))
                        for m in range(KT):
                            for f in range(NF):
                                for i, (w, h) in enumerate(((w_hi, hid_hi), (w_hi, hid_lo), (w_lo, hid_hi))):
                                    mm = pe.matmul(y_ps[:, half, m, :], down_w(w, slot, f, m), h[:, half, f, :],
                                                   start=(opens and f == 0 and i == 0), stop=(closes and f == NF - 1 and i == 2),
                                                   skip_group_check=True)
                        mm.then_inc(s.y_done, 1)

                    if c:
                        pe.wait_ge(s.chunk_done, HV * c)
                    if "b2" in dram:
                        for half in range(HV):
                            for m in range(KT):
                                pe.matmul(y_ps[:, half, m, :], b2[:, m * P:(m + 1) * P],
                                          gT[:, c * CT + half * CH:c * CT + (half + 1) * CH], start=True, stop=False,
                                          skip_group_check=True)
                    opens_with = "b2" not in dram
                    first = [True]
                    first_down = [True]

                    def turn(k, e, slot, uses):
                        pe.wait_ge(s.w_split, k + 3)
                        hidden(k, slot, 0)
                        if not first[0]:
                            down(k - 1, 1 - slot, 1, opens_with and first_down[0], False)
                            first_down[0] = False
                        hidden(k, slot, 1)
                        down(k, slot, 0, opens_with and first[0], False)
                        first[0] = False

                    turns(pe, c * NG, turn)
                    k = (c + 1) * NG - 1
                    down(k, k % 2, 1, False, True)

            @block.scalar
            def _(act):
                for k in range(KT):
                    act.activation(x_hi[:, k, :], env.xT[:, k, :], ACT.Copy).then_inc(s.x_hi_ready, 1)
                act.wait_ge(s.chain, 3 if score == "softmax" else 1)
                act.activation(sc[:, :, :], sc[:, :, :], ACT.Exp if score == "softmax" else ACT.Sigmoid).then_inc(s.acted, 1)
                for c in range(T // CT):
                    def turn(k, e, slot, uses):
                        if biased:
                            act.wait_ge(g_ready[slot], uses * (16 * 2))
                        for half in range(HV):
                            for f in range(NF):
                                n = (k * HV + half) * NF + f
                                act.wait_ge(s.hid_ready, n + 1)
                                act.wait_ge(s.mul_done, n + 1)
                                ins = hid_ps[:, bank(slot, half, f, R), 0, :]
                                out = lift[:, bank(slot, half, f, 4), :]
                                if glu:
                                    act.activation(out, ins, ACT.Silu).then_inc(s.act_ready, 1)
                                else:
                                    act.activation(out, ins, ACT.Gelu, bias=b1[:, slot, f:f + 1]).then_inc(s.act_ready, 1)
                    turns(act, c * NG, turn)

            @block.vector
            def _(dve):
                done = [0]

                def link(ins):
                    done[0] += 1
                    ins.then_inc(s.chain, 1)
                    dve.wait_ge(s.chain, done[0])

                dve.wait_ge(s.loaded, 16 * loads)
                dve.wait_ge(s.logit_ready, 1)
                if "router_b" in dram:
                    link(dve.tensor_tensor(sc[:, :, :], log_ps, over(rb[:, :], NT), ALU.add))
                else:
                    link(dve.tensor_copy(sc[:, :, :], log_ps))
                if score == "softmax":
                    link(dve.tensor_reduce(rowmax[:, :], sc[:, :, :], AX.X, ALU.max))
                    link(dve.tensor_tensor(sc[:, :, :], sc[:, :, :], last(rowmax[:, :], E), ALU.subtract))
                for k in range(KT):
                    dve.wait_ge(s.x_hi_ready, k + 1)
                    dve.tensor_tensor(x_lo[:, k, :], env.xT[:, k, :], x_hi[:, k, :].bitcast(F32), ALU.subtract).then_inc(s.x_lo_ready, 1)
                dve.wait_ge(s.acted, 1)
                if "route_scale" in dram:
                    link(dve.tensor_scalar(sc[:, :, :], sc[:, :, :], rs[:, 0:1], None, ALU.mult))
                own = sc[:, :, :].unsqueeze(3).broadcast_to([P, NT, E, E])
                other = sc[:, :, :].unsqueeze(2).broadcast_to([P, NT, E, E])
                dve.wait_ge(s.before_ready, 1)
                link(dve.tensor_tensor(beats, other, own, ALU.is_equal))
                link(dve.tensor_tensor(beats, beats, before[:, :, :].unsqueeze(1).broadcast_to([P, NT, E, E]), ALU.mult))
                link(dve.tensor_reduce(rank[:, :, :], beats, AX.X, ALU.add))
                link(dve.tensor_tensor(beats, other, own, ALU.is_gt))
                link(dve.tensor_reduce(above[:, :, :], beats, AX.X, ALU.add))
                link(dve.tensor_tensor(rank[:, :, :], rank[:, :, :], above[:, :, :], ALU.add))
                link(dve.tensor_scalar(rank[:, :, :], rank[:, :, :], float(topk), None, ALU.is_lt))
                link(dve.tensor_tensor(sc[:, :, :], sc[:, :, :], rank[:, :, :], ALU.mult))
                link(dve.tensor_reduce(total[:, :], sc[:, :, :], AX.X, ALU.add))
                link(dve.reciprocal(total[:, :], total[:, :]))
                dve.tensor_tensor(sc[:, :, :], sc[:, :, :], last(total[:, :], E), ALU.mult).then_inc(s.gate_ready, 1)
                dve.wait_ge(s.turned, 1)
                dve.tensor_copy(gT[:, :], gT_ps).then_inc(s.kept, 1)

                for c in range(T // CT):
                    def turn(k, e, slot, uses):
                        dve.wait_ge(g_ready[slot], uses * (16 * (1 + biased)))
                        for half in range(HV):
                            dve.wait_ge(s.y_done, k * HV + (half + 1))
                            for f in range(NF):
                                n = (k * HV + half) * NF + f
                                dve.wait_ge(s.act_ready, n + (1 if glu else R + 1))
                                up = lift[:, bank(slot, half, f, 4), :]
                                if glu:
                                    dve.tensor_tensor(up, up, hid_ps[:, bank(slot, half, f, R), 1, :], ALU.mult).then_inc(s.hid_free, 1)
                                    dve.wait_ge(s.hid_free, n + (R + 1))
                                dve.tensor_tensor(up, up, gate[:, slot, f * per // NF, half * CH:(half + 1) * CH], ALU.mult).then_inc(s.gated, 1)
                                dve.wait_ge(s.gated, n + 1)
                                dve.tensor_copy(hid_hi[:, half, f, :], up).then_inc(s.hid_hi_done, 1)
                                dve.wait_ge(s.hid_hi_done, n + 1)
                                dve.tensor_tensor(hid_lo[:, half, f, :], up, hid_hi[:, half, f, :].bitcast(F32), ALU.subtract)\
                                   .then_inc(s.mul_done, 1)
                    turns(dve, c * NG, turn)
                    dve.wait_ge(s.y_done, (c + 1) * NG * HV + 2)
                    for half in range(HV):
                        at = c * CT + half * CH
                        dve.tensor_copy(y[:, :, at:at + CH], y_ps[:, half]).then_inc(s.chunk_done, 1)

        residual_norm(nc, env, branch=y, bias=y_bias if "bs2" in dram else None)


def decoder(nc, d, out, stages=STAGES):
    def group(prefix):
        return {n[len(prefix):]: a for n, a in d.items() if n.startswith(prefix)}

    def space(prefix):
        return named(**group(prefix))

    with ExitStack() as st:
        env = named(
            q_dram=d["q_dram"], k_dram=d["k_dram"],
            xT=sbuf(nc, st, "xT", [P, KT, T]), ctxT=sbuf(nc, st, "ctxT", [P, KT, NB * M]),
            ident=sbuf(nc, st, "ident", [P, P]), identb=sbuf(nc, st, "identb", [P, P], BF16),
            avg=sbuf(nc, st, "avg", [P, P]), eps=sbuf(nc, st, "eps", [P, 1]), ones=sbuf(nc, st, "ones", [P, P]),
            causal_qk=sbuf(nc, st, "causal_qk", [P, P], BF16), causal_kq=sbuf(nc, st, "causal_kq", [P, P], BF16),
            window_qk=sbuf(nc, st, "window_qk", [P, WINQ], BF16), window_kq=sbuf(nc, st, "window_kq", [P, WINQ], BF16))
        stored = st.enter_context(nc.semaphore("stored"))
        setup(nc, env, space("in_"))

        def pad_attention():
            def pad_mask(b):
                return d["pad_mask"][b].unsqueeze(0).unsqueeze(0).broadcast_to([P, S // P, M])
            with ExitStack() as ms:
                t = mask_tiles(nc, ms, env, pad_mask, lambda b: d["pad_mask"][b].unsqueeze(1), 1, U8,
                               ALU.not_equal, MASKED, "pad")
                attention(nc, env, group("L2x_"), "xmask", float(8 ** -0.5), t)

        def masked_attention():
            with ExitStack() as ms:
                t = mask_tiles(nc, ms, env, lambda b: d["mask_qk"][b].rearrange("(t p) m -> p t m", p=P),
                               lambda b: d["mask_kq"][b], S, I32, ALU.is_equal, NEG, "seen")
                attention(nc, env, group("L3x_"), "xmask", float(HD ** -0.5), t)

        plan = [
            lambda: min_gru(nc, env, group("L0a_")),
            lambda: wide_cross(nc, env, space("L0x_")),
            lambda: butterfly_ffn(nc, env, space("L0f_")),
            lambda: attention(nc, env, group("L1a_"), "causal", float(HD ** -0.5)),
            lambda: attention(nc, env, group("L1x_"), "xcausal", float(HD ** -0.5)),
            lambda: moe(nc, env, group("L1f_"), 8, 512, 2, True, "softmax", 1),
            lambda: attention(nc, env, group("L2a_"), "full", float(D ** -0.5)),
            pad_attention,
            lambda: moe(nc, env, group("L2f_"), 8, 128, 2, False, "sigmoid", 1, per=3),
            lambda: attention(nc, env, group("L3a_"), "window", float(HD ** -0.5)),
            masked_attention,
            lambda: moe(nc, env, group("L3f_"), 16, 512, 4, False, "softmax", 0),
        ]
        for stage in plan[:stages] if isinstance(stages, int) else [plan[i] for i in stages]:
            with nc.cleanup_on_exit():
                stage()
        with nc.Block() as block:
            @block.sync
            def _(sp):
                sp.dma_start(out.rearrange("(k p) t -> p k t", p=P), env.xT[:, :, :]).then_inc(stored, 16)
                sp.wait_ge(stored, 16)


def layouts(i):
    import numpy as np

    c = np.ascontiguousarray
    a = {n: np.asarray(x) for n, x in i.items()}
    r = {}

    def columns(b):
        return c(np.swapaxes(b.reshape(*b.shape[:-1], -1, P), -1, -2))

    r["in_xT"] = c(a["x"].reshape(T, D).T)
    r["in_ctxT"] = c(a["ctx_1024"].reshape(NB * M, D).T)
    r["pad_mask"] = c(a["mask_BxS2_bf0"])
    r["mask_qk"] = c(a["mask_Bx1xSxS2_ik1"][:, 0])
    r["mask_kq"] = c(a["mask_Bx1xSxS2_ik1"][:, 0].transpose(0, 2, 1))
    for n in "ifh":
        r["L0a_w_" + n] = columns(a["L0_attn_w_" + n])
    qkv = a["L0_xattn_qkv_w"]
    r["L0x_wq"], r["L0x_wkT"], r["L0x_wvT"] = c(qkv[:D]), c(qkv[D:2 * D].T), c(qkv[2 * D:].T)
    r["L0x_projT"], r["L0x_proj_b"], r["L0x_mask"] = c(a["L0_xattn_proj_w"].T), columns(a["L0_xattn_proj_b"]), a["mask_S2_ik0"]
    for n in ("W_exp", "b_exp"):
        r["L0f_" + n] = a["L0_ffn_" + n]
    for n in ("up_bias", "b_con", "down_bias"):
        r["L0f_" + n] = columns(a["L0_ffn_" + n])
    r["L0f_W_conT"] = c(a["L0_ffn_W_con"].T)
    for n, w, flip in (("up", a["L0_ffn_up_weights"], False), ("down", a["L0_ffn_down_weights"], True)):
        coef = np.empty((w.shape[0], 2, 2 * w.shape[1]), w.dtype)
        for s in range(w.shape[0]):
            ws = w[s].reshape(-1, 2 ** s, 2, 2)
            own = np.stack([ws[..., 0, 0], ws[..., 1, 1]], 1)
            par = np.stack([ws[..., 1, 0], ws[..., 0, 1]] if flip else [ws[..., 0, 1], ws[..., 1, 0]], 1)
            coef[s, 0], coef[s, 1] = own.reshape(-1), par.reshape(-1)
        r[f"L0f_{n}_coef"] = coef

    def padded_rows(w):
        out = np.zeros((2 * D, w.shape[1]), w.dtype)
        out.reshape(H, 2 * HD, -1)[:, :HD] = w.reshape(H, HD, -1)
        return out

    for n in ("Wq", "Wk", "Wv", "bv"):
        r["L1a_" + n] = a["L1_attn_" + n]
    for n in ("bq", "bk", "bo"):
        r["L1a_" + n] = columns(a["L1_attn_" + n])
    r["L1a_Wo"] = padded_rows(a["L1_attn_Wo"])
    for p, q in (("L1x_", "L1_xattn_"), ("L3a_", "L3_attn_"), ("L3x_", "L3_xattn_")):
        for n in ("Wq", "Wk", "Wv"):
            r[p + n] = c(a[q + n].T)
        r[p + "Wo"] = padded_rows(a[q + "Wo"].T)
    for n in ("Wq", "Wk", "Wv"):
        big = np.zeros((H, HD, H, HD), a["L2_attn_" + n].dtype)
        for h in range(H):
            big[h, :, h, :] = a["L2_attn_" + n].T
        r["L2a_" + n] = big.reshape(D, D)
    r["L2a_Wo"], r["L2a_bo"] = padded_rows(a["L2_attn_W_out"].T), columns(a["L2_attn_b_out"])
    for n in ("q", "k"):
        w, bias = a["L2_xattn_W" + n], a["L2_xattn_b" + n]
        big, bb = np.zeros((D, H, HD), w.dtype), np.zeros((H, HD), bias.dtype)
        hq = w.shape[1] // (H // 2)
        big[:, :, :hq] = np.repeat(w.reshape(D, H // 2, hq), 2, 1)
        bb[:, :hq] = np.repeat(bias.reshape(H // 2, hq), 2, 0)
        r["L2x_W" + n], r["L2x_b" + n] = big.reshape(D, D), columns(bb.reshape(D))
    r["L2x_Wv"] = np.eye(D, dtype=np.float32)
    r["L2x_Wo"] = padded_rows(np.eye(D, dtype=np.float32))

    def grouped(shared, experts, per, rows):
        w = np.concatenate([shared[None], experts])
        w = w.reshape(-1, per, *w.shape[1:])
        w = w if rows else w.swapaxes(1, 2)
        return c(w.reshape(w.shape[0], -1, w.shape[-1]) if rows else w.reshape(*w.shape[:2], -1))

    r["L1f_Wr"] = a["L1_ffn_Wr"]
    for n, m, sm in (("W1", "Wg", "Sg"), ("Wu", "Wu", "Su"), ("W2", "Wd", "Sd")):
        r["L1f_" + n] = grouped(a["L1_ffn_" + sm].reshape(a["L1_ffn_" + m].shape[1:]), a["L1_ffn_" + m], 1, True)
    for n, m in (("Wr", "gate_W"), ("b2", "b2")):
        r["L2f_" + n] = a["L2_ffn_" + m]
    for n, m, sm, rows in (("W1", "W1", "Ws1", False), ("W2", "W2", "Ws2", True)):
        r["L2f_" + n] = grouped(a["L2_ffn_" + sm].reshape(a["L2_ffn_" + m].shape[1:]), a["L2_ffn_" + m], 3, rows)
    r["L2f_bs2"] = columns(a["L2_ffn_bs2"])
    r["L2f_b1"] = columns(np.concatenate([a["L2_ffn_bs1"].reshape(1, -1), a["L2_ffn_b1"]]).reshape(3, -1))
    r["L2f_route_scale"] = a["L2_ffn_route_scale"].reshape(1)
    for n, m in (("Wr", "router_w"), ("router_b", "router_b"), ("W1", "w1"), ("W2", "w2"), ("b2", "b2")):
        r["L3f_" + n] = c(a["L3_ffn_" + m])
    r["L3f_b1"] = columns(a["L3_ffn_b1"])
    return r


def kernel(**inputs):
    import numpy as np
    import concourse.bacc as bacc
    from concourse.bass_utils import run_bass_kernel_spmd

    nc = bacc.Bacc("TRN2", target_bir_lowering=False, num_devices=1)
    arrays, aps = {}, {}
    for name, a in layouts(inputs).items():
        arrays[name + "_dram"] = a
        aps[name] = nc.dram_tensor(name + "_dram", a.shape, mybir.dt.from_np(a.dtype), kind="ExternalInput").ap()
    for p, e in (("L1f_", 9), ("L2f_", 9), ("L3f_", 16)):
        aps[p + "gates"] = nc.dram_tensor(p + "gates_dram", [e, T], F32, kind="Internal").ap()
    for n in "qk":
        aps[n + "_dram"] = nc.dram_tensor(n + "_parts_dram", [NB, 2, D, S], F32, kind="Internal").ap()
    out = nc.dram_tensor("out_dram", [D, T], F32, kind="ExternalOutput").ap()
    decoder(nc, aps, out)
    r = run_bass_kernel_spmd(nc, [arrays], core_ids=[0])
    return np.ascontiguousarray(r.results[0]["out_dram"].T).reshape(NB, S, D)
```

```python
from contextlib import ExitStack

import concourse.bass as bass
from concourse import mybir

F32 = mybir.dt.float32
F32R = mybir.dt.float32r
BF16 = mybir.dt.bfloat16
I32 = mybir.dt.int32
U8 = mybir.dt.uint8
ALU = mybir.AluOpType
ACT = mybir.ActivationFunctionType
AX = mybir.AxisListType

P = 128
D = 256
KT = D // P
NB = 2
S = 1024
T = NB * S
NT = T // P
CH = 512
NCH = T // CH
M = 77
H = 16
HD = D // H
HU = 4
NU = H // HU
WIN = 64
WINQ = P + WIN
EPS = 1e-5
MASKED = -1e30
NEG = -1e9
STACK = 4 * HD
STAGES = 10
TAGS = []


def tag():
    TAGS.append(0)
    return len(TAGS)


def named(**items):
    return type("Named", (), items)


def sems(nc, names):
    return named(**{n: nc.alloc_semaphore(f"{n}_{tag()}") for n in names.split()})


def sbuf(nc, st, name, shape, dt=F32):
    return st.enter_context(nc.sbuf_tensor(f"{name}_{tag()}", shape, dt))


def psum(nc, st, name, shape, dt=F32):
    return st.enter_context(nc.psum_tensor(f"{name}_{tag()}", shape, dt))


def over(ap, n):
    return ap.unsqueeze(1).broadcast_to([ap.shape[0], n, ap.shape[1]])


def last(ap, n):
    return ap.unsqueeze(2).broadcast_to([ap.shape[0], ap.shape[1], n])


def setup(nc, env, dram):
    with ExitStack() as st:
        s = sems(nc, "loaded cleared shaped")
        block = st.enter_context(nc.Block())

        @block.sync
        def _(sp):
            sp.dma_start(env.xT[:, :, :], dram.xT.rearrange("(k p) t -> p k t", p=P)).then_inc(s.loaded, 16)
            sp.dma_start(env.ctxT[:, :, :], dram.ctxT.rearrange("(k p) t -> p k t", p=P)).then_inc(s.loaded, 16)
            sp.wait_ge(s.loaded, 32)

        @block.gpsimd
        def _(pool):
            tiles = (env.ident, env.identb, env.causal_qk, env.causal_kq, env.window_qk, env.window_kq)
            for t in tiles:
                pool.memset(t[:, :], 0.0).then_inc(s.cleared, 1)
            pool.memset(env.avg[:, :], 1.0 / D).then_inc(s.cleared, 1)
            pool.memset(env.eps[:, :], EPS).then_inc(s.cleared, 1)
            pool.memset(env.ones[:, :], 1.0).then_inc(s.cleared, 1)
            pool.wait_ge(s.cleared, len(tiles) + 3)
            for t in (env.ident, env.identb):
                pool.affine_select(out=t[:, :], in_=t[:, :], compare_op=ALU.not_equal, fill=1.0, base=0,
                                   pattern=[[-1, P]], channel_multiplier=1).then_inc(s.shaped, 1)
            pool.affine_select(out=env.causal_qk[:, :], in_=env.causal_qk[:, :], compare_op=ALU.is_ge, fill=MASKED,
                               base=0, pattern=[[-1, P]], channel_multiplier=1).then_inc(s.shaped, 1)
            pool.affine_select(out=env.causal_kq[:, :], in_=env.causal_kq[:, :], compare_op=ALU.is_ge, fill=MASKED,
                               base=0, pattern=[[1, P]], channel_multiplier=-1).then_inc(s.shaped, 1)
            pool.affine_select(out=env.window_qk[:, :], in_=env.window_qk[:, :], compare_op=ALU.is_ge, fill=MASKED,
                               base=-1, pattern=[[1, WINQ]], channel_multiplier=-1).then_inc(s.shaped, 1)
            pool.affine_select(out=env.window_kq[:, :], in_=env.window_kq[:, :], compare_op=ALU.is_ge, fill=MASKED,
                               base=0, pattern=[[1, WINQ]], channel_multiplier=-1).then_inc(s.shaped, 1)
            pool.wait_ge(s.shaped, 6)
            pool.affine_select(out=env.window_qk[:, :], in_=env.window_qk[:, :], compare_op=ALU.is_ge, fill=MASKED,
                               base=WIN, pattern=[[-1, WINQ]], channel_multiplier=1).then_inc(s.shaped, 1)
            pool.affine_select(out=env.window_kq[:, :], in_=env.window_kq[:, :], compare_op=ALU.is_ge, fill=MASKED,
                               base=WIN - 1, pattern=[[-1, WINQ]], channel_multiplier=1).then_inc(s.shaped, 1)


def residual_norm(nc, env, branch_matmuls=None, branch=None, bias=None):
    TC = CH // P
    with ExitStack() as st:
        s = sems(nc, "y_ready summed mean_ready centred squared var_ready rooted inverted spread rstd_ready normed")
        y_ps = psum(nc, st, "y_ps", [P, 2, KT, CH])
        mean_ps = psum(nc, st, "mean_ps", [P, CH])
        var_ps = psum(nc, st, "var_ps", [P, 2, TC])
        rstd_ps = psum(nc, st, "rstd_ps", [P, 2, CH])
        dev = sbuf(nc, st, "dev", [P, NCH, KT, CH])
        sq = sbuf(nc, st, "sq", [P, 2, KT, CH])
        std = sbuf(nc, st, "std", [P, NCH, TC])
        rstd = sbuf(nc, st, "rstd", [P, NCH, TC])
        diag = sbuf(nc, st, "diag", [P, 2, TC, P])
        block = st.enter_context(nc.Block())

        @block.tensor
        def _(pe):
            for n in range(NCH + 3):
                if n < NCH and branch_matmuls:
                    if n >= 2:
                        pe.wait_ge(s.summed, n - 1)
                    branch_matmuls(pe, n, y_ps[:, n % 2]).then_inc(s.y_ready, 1)
                if 1 <= n <= NCH:
                    m = n - 1
                    pe.wait_ge(s.summed, m + 1)
                    if m >= 1:
                        pe.wait_ge(s.centred, m)
                    for k in range(KT):
                        mm = pe.matmul(mean_ps[:, :], env.avg[:, :], env.xT[:, k, m * CH:(m + 1) * CH],
                                       start=(k == 0), stop=(k == KT - 1))
                    mm.then_inc(s.mean_ready, 1)
                if 2 <= n <= NCH + 1:
                    m = n - 2
                    pe.wait_ge(s.squared, m + 1)
                    if m >= 1:
                        pe.wait_ge(s.rooted, m)
                    for t in range(TC):
                        for k in range(KT):
                            mm = pe.matmul(var_ps[:, m % 2, t:t + 1], sq[:, m % 2, k, t * P:(t + 1) * P], env.avg[:, 0:1],
                                           start=(k == 0), stop=(k == KT - 1))
                    mm.then_inc(s.var_ready, 1)
                if n >= 3:
                    m = n - 3
                    pe.wait_ge(s.spread, m + 1)
                    if m >= 2:
                        pe.wait_ge(s.normed, m - 1)
                    for t in range(TC):
                        mm = pe.matmul(rstd_ps[:, m % 2, t * P:(t + 1) * P], env.ones[:, :], diag[:, m % 2, t, :],
                                       start=True, stop=True)
                    mm.then_inc(s.rstd_ready, 1)

        @block.scalar
        def _(act):
            for n in range(NCH):
                act.wait_ge(s.centred, n + 1)
                if n >= 2:
                    act.wait_ge(s.var_ready, n - 1)
                act.activation(sq[:, n % 2], dev[:, n], ACT.Square).then_inc(s.squared, 1)
                act.wait_ge(s.var_ready, n + 1)
                act.activation(std[:, n, :], var_ps[:, n % 2, :], ACT.Sqrt, bias=env.eps[:, 0:1]).then_inc(s.rooted, 1)

        @block.vector
        def _(dve):
            for n in range(NCH + 3):
                if n < NCH:
                    x = env.xT[:, :, n * CH:(n + 1) * CH]
                    if branch_matmuls:
                        dve.wait_ge(s.y_ready, n + 1)
                        y = y_ps[:, n % 2]
                    else:
                        y = branch[:, :, n * CH:(n + 1) * CH]
                    if bias is None:
                        dve.tensor_tensor(x, y, x, ALU.add).then_inc(s.summed, 1)
                    else:
                        for k in range(KT):
                            add = dve.scalar_tensor_tensor(out=x[:, k], in0=y[:, k], scalar=bias[:, k:k + 1],
                                                           in1=x[:, k], op0=ALU.add, op1=ALU.add)
                        add.then_inc(s.summed, 1)
                if 1 <= n <= NCH:
                    m = n - 1
                    dve.wait_ge(s.mean_ready, m + 1)
                    dve.tensor_tensor(dev[:, m], env.xT[:, :, m * CH:(m + 1) * CH], over(mean_ps[:, :], KT),
                                      ALU.subtract).then_inc(s.centred, 1)
                if 2 <= n <= NCH + 1:
                    m = n - 2
                    dve.wait_ge(s.rooted, m + 1)
                    dve.reciprocal(rstd[:, m, :], std[:, m, :]).then_inc(s.inverted, 1)
                    dve.wait_ge(s.inverted, m + 1)
                    if m >= 2:
                        dve.wait_ge(s.rstd_ready, m - 1)
                    dve.tensor_tensor(diag[:, m % 2], over(env.ident[:, :], TC), last(rstd[:, m, :], P), ALU.mult)\
                       .then_inc(s.spread, 1)
                if n >= 3:
                    m = n - 3
                    dve.wait_ge(s.rstd_ready, m + 1)
                    dve.tensor_tensor(env.xT[:, :, m * CH:(m + 1) * CH], dev[:, m], over(rstd_ps[:, m % 2, :], KT),
                                      ALU.mult).then_inc(s.normed, 1)


FF = 1024
NS = 10


def butterfly_stage(eng, y, tmp, coef, stride, step, n0):
    def pairs(a, i):
        return a.rearrange("p k (n two s) -> p k n two s", two=2, s=stride)[:, :, :, i, :]

    own = coef[:, 0, :].unsqueeze(1).broadcast_to(list(y.shape))
    par = coef[:, 1, :].unsqueeze(1).broadcast_to(list(y.shape))
    for i in range(2):
        eng.tensor_tensor(pairs(tmp, i), pairs(y, 1 - i), pairs(par, i), ALU.mult).then_inc(step, 1)
    eng.wait_ge(step, n0 + 2)
    eng.tensor_tensor(y, y, own, ALU.mult).then_inc(step, 1)
    eng.wait_ge(step, n0 + 3)
    eng.tensor_tensor(y, y, tmp, ALU.add).then_inc(step, 1)
    eng.wait_ge(step, n0 + 4)
    return n0 + 4


def down_stages(nc, dram, down, first, n):
    s = sems(nc, "down_loaded coef_d0 coef_d1 d_step")
    coef_ready = (s.coef_d0, s.coef_d1)

    def load(sp):
        if first == 0:
            sp.dma_start(down.w[:, :, :], dram["W_conT"].rearrange("(k p) n -> p k n", p=P)).then_inc(s.down_loaded, 16)
        for i in range(n):
            if i >= 2:
                sp.wait_ge(s.d_step, 4 * (i - 1))
            sp.dma_start(down.coef[:, i % 2], dram["down_coef"][NS - 1 - first - i].partition_broadcast(P)).then_inc(coef_ready[i % 2], 16)

    def run(pool):
        if first == 0:
            pool.wait_ge(s.down_loaded, 16)
        done = 0
        for i in range(n):
            pool.wait_ge(coef_ready[i % 2], 16 * (i // 2 + 1))
            done = butterfly_stage(pool, down.w[:, :, :], down.tmp[:, :, :], down.coef[:, i % 2], 2 ** (NS - 1 - first - i),
                                   s.d_step, done)

    return load, run


def min_gru(nc, env, dram, beside):
    with ExitStack() as st:
        w = {n: sbuf(nc, st, f"w_{n}", [P, KT]) for n in "fih"}
        neg = {n: sbuf(nc, st, f"neg_{n}", [P, KT]) for n in "fi"}
        h_out = sbuf(nc, st, "h_out", [P, KT, T])
        s = sems(nc, "loaded negated abs_done exp_done ln_done relu_done soft_done diff_done gates_done low_done sig_done "
                         "g_done v_done scanned")
        mag = sbuf(nc, st, "mag", [P, 2, 2, S])
        soft = sbuf(nc, st, "soft", [P, 2, 2, S])
        relu = sbuf(nc, st, "relu", [P, 2, 2, S])
        diff = sbuf(nc, st, "diff", [P, 2, S])
        gate = sbuf(nc, st, "gate", [P, 2, 2, S])
        low = sbuf(nc, st, "low", [P, 2, S])
        hid = sbuf(nc, st, "hid", [P, 2, S])
        with nc.Block() as block:
            items = [(k, b) for k in range(KT) for b in range(NB)]

            @block.sync
            def _(sp):
                for n in "fih":
                    sp.dma_start(w[n][:, :], dram["w_" + n]).then_inc(s.loaded, 16)
                beside[0](sp)

            @block.gpsimd
            def _(pool):
                beside[1](pool)

            @block.scalar
            def _(act):
                act.wait_ge(s.loaded, 48)
                for n, (k, b) in enumerate(items):
                    x = env.xT[:, k, b * S:(b + 1) * S]
                    z = n % 2
                    if n >= 2:
                        act.wait_ge(s.soft_done, 2 * (n - 1))
                    for a, g in enumerate("fi"):
                        act.activation(mag[:, z, a, :], x, ACT.Abs, scale=w[g][:, k:k + 1]).then_inc(s.abs_done, 1)
                    act.wait_ge(s.abs_done, 2 * (n + 1))
                    act.activation(mag[:, z], mag[:, z], ACT.Exp, scale=-1.0).then_inc(s.exp_done, 1)
                    act.wait_ge(s.exp_done, n + 1)
                    act.activation(soft[:, z], mag[:, z], ACT.Ln, bias=1.0).then_inc(s.ln_done, 1)
                for n, (k, b) in enumerate(items):
                    z = n % 2
                    act.wait_ge(s.diff_done, n + 1)
                    if n >= 2:
                        act.wait_ge(s.scanned, n - 1)
                    act.activation(gate[:, z, 0, :], diff[:, z, :], ACT.Sigmoid, scale=-1.0).then_inc(s.gates_done, 1)
                    act.activation(gate[:, z, 1, :], diff[:, z, :], ACT.Sigmoid).then_inc(s.gates_done, 1)
                    act.wait_ge(s.low_done, n + 1)
                    act.activation(low[:, z, :], low[:, z, :], ACT.Sigmoid).then_inc(s.sig_done, 1)

            @block.vector
            def _(dve):
                dve.wait_ge(s.loaded, 48)
                for g in "fi":
                    dve.tensor_scalar(neg[g][:, :], w[g][:, :], -1.0, None, ALU.mult).then_inc(s.negated, 1)
                dve.wait_ge(s.negated, 2)

                def softplus_gap(n):
                    k, b = items[n]
                    z = n % 2
                    x = env.xT[:, k, b * S:(b + 1) * S]
                    for a, g in enumerate("fi"):
                        dve.tensor_scalar(relu[:, z, a, :], x, neg[g][:, k:k + 1], 0.0, ALU.mult, ALU.max)\
                           .then_inc(s.relu_done, 1)
                    dve.wait_ge(s.relu_done, 2 * (n + 1))
                    dve.wait_ge(s.ln_done, n + 1)
                    for a in range(2):
                        dve.tensor_tensor(relu[:, z, a, :], relu[:, z, a, :], soft[:, z, a, :], ALU.add)\
                           .then_inc(s.soft_done, 1)
                    dve.wait_ge(s.soft_done, 2 * (n + 1))
                    if n >= 2:
                        dve.wait_ge(s.gates_done, 2 * (n - 1))
                    dve.tensor_tensor(diff[:, z, :], relu[:, z, 0, :], relu[:, z, 1, :], ALU.subtract)\
                       .then_inc(s.diff_done, 1)

                def hidden(n):
                    k, b = items[n]
                    z = n % 2
                    x = env.xT[:, k, b * S:(b + 1) * S]
                    dve.tensor_scalar(low[:, z, :], x, w["h"][:, k:k + 1], 0.0, ALU.mult, ALU.min).then_inc(s.low_done, 1)
                    dve.tensor_scalar(hid[:, z, :], x, w["h"][:, k:k + 1], 0.0, ALU.mult, ALU.max).then_inc(s.g_done, 1)

                def scan(n):
                    k, b = items[n]
                    z = n % 2
                    dve.wait_ge(s.sig_done, n + 1)
                    dve.wait_ge(s.g_done, 3 * n + 1)
                    dve.tensor_tensor(hid[:, z, :], hid[:, z, :], low[:, z, :], ALU.add).then_inc(s.g_done, 1)
                    dve.wait_ge(s.gates_done, 2 * (n + 1))
                    dve.wait_ge(s.g_done, 3 * n + 2)
                    dve.tensor_tensor(hid[:, z, :], hid[:, z, :], gate[:, z, 1, :], ALU.mult).then_inc(s.g_done, 1)
                    dve.wait_ge(s.g_done, 3 * n + 3)
                    dve.tensor_tensor_scan(h_out[:, k, b * S:(b + 1) * S], gate[:, z, 0, :], hid[:, z, :], 0.0,
                                           ALU.mult, ALU.add).then_inc(s.scanned, 1)

                for n in range(len(items)):
                    if n >= 2:
                        hidden(n - 2)
                    softplus_gap(n) if n < 2 else (scan(n - 2), softplus_gap(n))
                for n in range(len(items) - 2, len(items)):
                    hidden(n)
                    scan(n)
        residual_norm(nc, env, branch=h_out)


def wide_cross(nc, env, dram, beside):
    scale = float(32 ** -0.5)
    NK = NB * M
    HT = NT // NB
    with ExitStack() as st:
        wq = sbuf(nc, st, "wq", [P, KT, D])
        wkT = sbuf(nc, st, "wkT", [P, KT, D])
        wvT = sbuf(nc, st, "wvT", [P, KT, D])
        projT = sbuf(nc, st, "projT", [P, KT, D])
        proj_b = sbuf(nc, st, "proj_b", [P, KT])
        mask_i = sbuf(nc, st, "mask_i", [M, 1], I32)
        keep = sbuf(nc, st, "keep", [M, 1])
        keyT = sbuf(nc, st, "keyT", [P, KT, NK])
        qkT = sbuf(nc, st, "qkT", [P, KT, NK])
        v = sbuf(nc, st, "v", [M, NB, D])
        sc = sbuf(nc, st, "sc", [P, HT, M])
        rowmax = sbuf(nc, st, "rowmax", [P, NB, HT])
        rowsum = sbuf(nc, st, "rowsum", [P, NB, HT])
        inv = sbuf(nc, st, "inv", [P, NB, HT])
        pr = sbuf(nc, st, "pr", [P, NB, HT, M])
        prT = sbuf(nc, st, "prT", [M, NB, HT, P])
        o = sbuf(nc, st, "o", [P, NT, D])
        with ExitStack() as inner:
            s = sems(nc, "loaded kept key_ready key_kept qk_ready qk_kept v_ready v_kept score_ready max_done sub_done "
                                "exp_done sum_done inv_done prob_done turned turned_kept out_ready out_kept")
            small_ps = psum(nc, inner, "small_ps", [P, 2, CH])
            score_ps = psum(nc, inner, "score_ps", [P, HT, P])
            turn_ps = psum(nc, inner, "turn_ps", [P, 2, HT // 2, P])
            out_ps = psum(nc, inner, "out_ps", [P, 2, CH])
            block = inner.enter_context(nc.Block())

            @block.sync
            def _(sp):
                sp.dma_start(wkT[:, :, :], dram.wkT.rearrange("(k p) n -> p k n", p=P)).then_inc(s.loaded, 16)
                sp.dma_start(wq[:, :, :], dram.wq.rearrange("(k p) n -> p k n", p=P)).then_inc(s.loaded, 16)
                sp.dma_start(wvT[:, :, :], dram.wvT.rearrange("(k p) n -> p k n", p=P)).then_inc(s.loaded, 16)
                sp.dma_start(projT[:, :, :], dram.projT.rearrange("(k p) n -> p k n", p=P)).then_inc(s.loaded, 16)
                sp.dma_start(proj_b[:, :], dram.proj_b).then_inc(s.loaded, 16)
                sp.dma_start(mask_i[:, :], dram.mask.rearrange("(m a) -> m a", a=1)).then_inc(s.loaded, 16)
                beside[0](sp)

            @block.gpsimd
            def _(pool):
                beside[1](pool)

            @block.tensor
            def _(pe):
                pe.wait_ge(s.loaded, 96)
                for m in range(KT):
                    for k in range(KT):
                        mm = pe.matmul(small_ps[:, m, 0:NK], wkT[:, k, m * P:(m + 1) * P], env.ctxT[:, k, :],
                                       start=(k == 0), stop=(k == KT - 1))
                mm.then_inc(s.key_ready, 1)
                pe.wait_ge(s.key_kept, 1)
                for m in range(KT):
                    for k in range(KT):
                        mm = pe.matmul(small_ps[:, m, 0:NK], wq[:, k, m * P:(m + 1) * P], keyT[:, k, :],
                                       start=(k == 0), stop=(k == KT - 1))
                mm.then_inc(s.qk_ready, 1)
                pe.wait_ge(s.qk_kept, 1)
                for b in range(NB):
                    for k in range(KT):
                        mm = pe.matmul(small_ps[0:M, b, 0:D], env.ctxT[:, k, b * M:(b + 1) * M], wvT[:, k, :],
                                       start=(k == 0), stop=(k == KT - 1))
                mm.then_inc(s.v_ready, 1)
                for b in range(NB):
                    if b:
                        pe.wait_ge(s.sub_done, b)
                    for t in range(HT):
                        tok = (b * HT + t) * P
                        for k in range(KT):
                            mm = pe.matmul(score_ps[:, t, 0:M], env.xT[:, k, tok:tok + P], qkT[:, k, b * M:(b + 1) * M],
                                           start=(k == 0), stop=(k == KT - 1))
                    mm.then_inc(s.score_ready, 1)
                for b in range(NB):
                    pe.wait_ge(s.prob_done, b + 1)
                    if b:
                        pe.wait_ge(s.turned_kept, b)
                    for t in range(HT):
                        mm = pe.transpose(turn_ps[0:M, t // (HT // 2), t % (HT // 2), :], pr[:, b, t, :], env.ident[:, :])
                    mm.then_inc(s.turned, 1)
                    pe.wait_ge(s.turned_kept, b + 1)
                    pe.wait_ge(s.v_kept, 1)
                    for t in range(HT):
                        i = b * HT + t
                        if i >= 2:
                            pe.wait_ge(s.out_kept, i - 1)
                        pe.matmul(out_ps[:, i % 2, 0:D], prT[:, b, t, :], v[:, b, :], start=True, stop=True)\
                          .then_inc(s.out_ready, 1)

            @block.scalar
            def _(act):
                for b in range(NB):
                    act.wait_ge(s.sub_done, b + 1)
                    act.activation(pr[:, b], sc[:, :, :], ACT.Exp, scale=scale).then_inc(s.exp_done, 1)
                for i in range(NT):
                    act.wait_ge(s.out_ready, i + 1)
                    act.activation(o[:, i, :], out_ps[:, i % 2, 0:D], ACT.Copy).then_inc(s.out_kept, 1)

            @block.vector
            def _(dve):
                dve.wait_ge(s.loaded, 96)
                dve.tensor_scalar(keep[:, :], mask_i[:, :], 0, None, ALU.not_equal).then_inc(s.kept, 1)
                dve.wait_ge(s.key_ready, 1)
                dve.tensor_copy(keyT[:, :, :], small_ps[:, :, 0:NK]).then_inc(s.key_kept, 1)
                dve.wait_ge(s.qk_ready, 1)
                dve.tensor_copy(qkT[:, :, :], small_ps[:, :, 0:NK]).then_inc(s.qk_kept, 1)
                dve.wait_ge(s.v_ready, 1)
                dve.wait_ge(s.kept, 1)
                dve.tensor_scalar(v[:, :, :], small_ps[0:M, :, 0:D], keep[:, 0:1], None, ALU.mult).then_inc(s.v_kept, 1)
                for b in range(NB):
                    dve.wait_ge(s.score_ready, b + 1)
                    dve.tensor_reduce(rowmax[:, b, :], score_ps[:, :, 0:M], AX.X, ALU.max).then_inc(s.max_done, 1)
                    dve.wait_ge(s.max_done, b + 1)
                    if b:
                        dve.wait_ge(s.exp_done, b)
                    dve.tensor_tensor(sc[:, :, :], score_ps[:, :, 0:M], last(rowmax[:, b, :], M), ALU.subtract)\
                       .then_inc(s.sub_done, 1)
                for b in range(NB):
                    dve.wait_ge(s.exp_done, b + 1)
                    dve.tensor_reduce(rowsum[:, b, :], pr[:, b], AX.X, ALU.add).then_inc(s.sum_done, 1)
                    dve.wait_ge(s.sum_done, b + 1)
                    dve.reciprocal(inv[:, b, :], rowsum[:, b, :]).then_inc(s.inv_done, 1)
                    dve.wait_ge(s.inv_done, b + 1)
                    dve.tensor_tensor(pr[:, b], pr[:, b], last(inv[:, b, :], M), ALU.mult).then_inc(s.prob_done, 1)
                    dve.wait_ge(s.turned, b + 1)
                    dve.tensor_copy(prT[:, b].rearrange("m t p -> m (t p)"),
                                    turn_ps[0:M].rearrange("m a t p -> m (a t p)")).then_inc(s.turned_kept, 1)

        J = S // D

        def proj(pe, n, out):
            b, half = n // 2, n % 2
            for m in range(KT):
                for j in range(J):
                    for k in range(KT):
                        mm = pe.matmul(out[:, m, j:CH:J], projT[:, k, m * P:(m + 1) * P],
                                       o[:, b * HT + KT * j + k, half * P:(half + 1) * P],
                                       start=(j == 0 and k == 0), stop=(j == J - 1 and k == KT - 1), skip_group_check=True)
            return mm

        residual_norm(nc, env, branch_matmuls=proj, bias=proj_b)


def butterfly_ffn(nc, env, dram, down):
    F = FF
    NF = F // P
    with ExitStack() as st:
        up_hi = sbuf(nc, st, "up_hi", [P, KT, F], F32R)
        up_lo = sbuf(nc, st, "up_lo", [P, KT, F], F32R)
        con_hi = sbuf(nc, st, "con_hi", [P, NF, D], F32R)
        con_lo = sbuf(nc, st, "con_lo", [P, NF, D], F32R)
        x_hi = sbuf(nc, st, "x_hi", [P, KT, T], F32R)
        x_lo = sbuf(nc, st, "x_lo", [P, KT, T], F32R)
        up_b = sbuf(nc, st, "up_b", [P, NF])
        y_bias = sbuf(nc, st, "y_bias", [P, KT])
        with ExitStack() as inner:
            up_w = sbuf(nc, inner, "up_w", [P, KT, F])
            brow = sbuf(nc, inner, "brow", [1, F])
            tmp_u = sbuf(nc, inner, "tmp_u", [P, KT, F])
            tmp_b = sbuf(nc, inner, "tmp_b", [1, F])
            coef_u = sbuf(nc, inner, "coef_u", [P, 3, 2, F])
            bias2 = sbuf(nc, inner, "bias2", [P, NF + 2 * KT])
            s = sems(nc, "up_loaded row_loaded coef_u0 coef_u1 coef_u2 u_step b_step con_ready con_kept bias_ready bias_kept side_bias x_hi_done "
                         "con_hi_done up_hi_done split")
            con_ps = psum(nc, inner, "con_ps", [P, NF, D])
            bias_ps = psum(nc, inner, "bias_ps", [P, NF])
            coef_ready = (s.coef_u0, s.coef_u1, s.coef_u2)
            block = inner.enter_context(nc.Block())

            @block.sync
            def _(sp):
                sp.dma_start(up_w[:, :, :], dram.W_exp.rearrange("(k p) n -> p k n", p=P)).then_inc(s.up_loaded, 16)
                sp.dma_start(brow[:, :], dram.b_exp.rearrange("(a n) -> a n", a=1)).then_inc(s.row_loaded, 16)
                for i in range(NS):
                    if i >= 3:
                        sp.wait_ge(s.u_step, 4 * (i - 2))
                        sp.wait_ge(s.b_step, 4 * (i - 2))
                    sp.dma_start(coef_u[:, i % 3], dram.up_coef[i].partition_broadcast(P)).then_inc(coef_ready[i % 3], 16)
                sp.dma_start(bias2[:, 0:NF], dram.up_bias).then_inc(s.side_bias, 16)
                sp.dma_start(bias2[:, NF:NF + KT], dram.b_con).then_inc(s.side_bias, 16)
                sp.dma_start(bias2[:, NF + KT:], dram.down_bias).then_inc(s.side_bias, 16)

            @block.scalar
            def _(act):
                act.activation(x_hi[:, :, :], env.xT[:, :, :], ACT.Copy).then_inc(s.x_hi_done, 1)
                act.wait_ge(s.con_ready, 1)
                act.activation(con_hi[:, :, :], con_ps[:, :, :], ACT.Copy).then_inc(s.con_hi_done, 1)
                act.wait_ge(s.u_step, 4 * NS)
                act.activation(up_hi[:, :, :], up_w[:, :, :], ACT.Copy).then_inc(s.up_hi_done, 1)

            @block.vector
            def _(dve):
                dve.wait_ge(s.up_loaded, 16)
                n = 0
                for i in range(NS):
                    dve.wait_ge(coef_ready[i % 3], 16 * (i // 3 + 1))
                    n = butterfly_stage(dve, up_w[:, :, :], tmp_u[:, :, :], coef_u[:, i % 3], 2 ** i, s.u_step, n)
                dve.wait_ge(s.x_hi_done, 1)
                dve.tensor_tensor(x_lo[:, :, :], env.xT[:, :, :], x_hi[:, :, :].bitcast(F32), ALU.subtract).then_inc(s.split, 1)
                dve.wait_ge(s.up_hi_done, 1)
                dve.tensor_tensor(up_lo[:, :, :], up_w[:, :, :], up_hi[:, :, :].bitcast(F32), ALU.subtract).then_inc(s.split, 1)
                dve.wait_ge(s.con_hi_done, 1)
                dve.tensor_tensor(con_lo[:, :, :], con_ps[:, :, :], con_hi[:, :, :].bitcast(F32), ALU.subtract).then_inc(s.split, 1)
                dve.wait_ge(s.side_bias, 48)
                dve.wait_ge(s.bias_ready, 1)
                dve.tensor_tensor(up_b[:, :], bias_ps[:, :], bias2[:, 0:NF], ALU.add).then_inc(s.bias_kept, 1)
                dve.tensor_tensor(y_bias[:, :], bias2[:, NF:NF + KT], bias2[:, NF + KT:], ALU.add).then_inc(s.bias_kept, 1)

            @block.gpsimd
            def _(pool):
                pool.wait_ge(s.row_loaded, 16)
                n = 0
                for i in range(NS):
                    pool.wait_ge(coef_ready[i % 3], 16 * (i // 3 + 1))
                    n = butterfly_stage(pool, brow[:, :].unsqueeze(1), tmp_b[:, :].unsqueeze(1), coef_u[0:1, i % 3], 2 ** i, s.b_step, n)

            @block.tensor
            def _(pe):
                for f in range(NF):
                    for k in range(KT):
                        mm = pe.transpose(con_ps[:, f, k * P:(k + 1) * P], down.w[:, k, f * P:(f + 1) * P], env.ident[:, :])
                mm.then_inc(s.con_ready, 1)
                pe.wait_ge(s.b_step, 4 * NS)
                for f in range(NF):
                    mm = pe.matmul(bias_ps[:, f:f + 1], brow[:, f * P:(f + 1) * P], env.ident[0:1, 0:1], start=True, stop=True)
                mm.then_inc(s.bias_ready, 1)

        y = sbuf(nc, st, "y", [P, KT, T])
        with ExitStack() as inner:
            lift = sbuf(nc, inner, "lift", [P, 4, CH])
            hid_hi = sbuf(nc, inner, "hid_hi", [P, 2, NF, CH], F32R)
            hid_lo = sbuf(nc, inner, "hid_lo", [P, 2, NF, CH], F32R)
            s = sems(nc, "hid_ready gelu_done hi_done lo_done y_ready y_kept")
            hid_ps = psum(nc, inner, "hid_ps", [P, 4, CH])
            y_ps = psum(nc, inner, "y_ps", [P, 2, KT, CH])
            block = inner.enter_context(nc.Block())

            @block.tensor
            def _(pe):
                for n in range(NCH + 1):
                    if n < NCH:
                        for f in range(NF):
                            i = n * NF + f
                            if i >= 4:
                                pe.wait_ge(s.gelu_done, i - 3)
                            for k in range(KT):
                                for j, (w, x) in enumerate(((up_hi, x_hi), (up_hi, x_lo), (up_lo, x_hi))):
                                    mm = pe.matmul(hid_ps[:, i % 4, :], w[:, k, f * P:(f + 1) * P], x[:, k, n * CH:(n + 1) * CH],
                                                   start=(k == 0 and j == 0), stop=(k == KT - 1 and j == 2))
                            mm.then_inc(s.hid_ready, 1)
                    if n >= 1:
                        c = n - 1
                        pe.wait_ge(s.lo_done, (c + 1) * NF)
                        if c >= 2:
                            pe.wait_ge(s.y_kept, c - 1)
                        for m in range(KT):
                            for f in range(NF):
                                for j, (w, h) in enumerate(((con_hi, hid_hi), (con_hi, hid_lo), (con_lo, hid_hi))):
                                    mm = pe.matmul(y_ps[:, c % 2, m, :], w[:, f, m * P:(m + 1) * P], h[:, c % 2, f, :],
                                                   start=(f == 0 and j == 0), stop=(f == NF - 1 and j == 2))
                        mm.then_inc(s.y_ready, 1)

            @block.scalar
            def _(act):
                for i in range(NCH * NF):
                    n, f = i // NF, i % NF
                    act.wait_ge(s.hid_ready, i + 1)
                    if i >= 4:
                        act.wait_ge(s.lo_done, i - 3)
                    act.activation(lift[:, i % 4, :], hid_ps[:, i % 4, :], ACT.Gelu, bias=up_b[:, f:f + 1])\
                       .then_inc(s.gelu_done, 1)

            @block.vector
            def _(dve):
                for n in range(NCH + 1):
                    for f in range(NF if n < NCH else 0):
                        i = n * NF + f
                        dve.wait_ge(s.gelu_done, i + 1)
                        if n >= 2:
                            dve.wait_ge(s.y_ready, n - 1)
                        dve.tensor_copy(hid_hi[:, n % 2, f, :], lift[:, i % 4, :]).then_inc(s.hi_done, 1)
                        dve.wait_ge(s.hi_done, i + 1)
                        dve.tensor_tensor(hid_lo[:, n % 2, f, :], lift[:, i % 4, :], hid_hi[:, n % 2, f, :].bitcast(F32),
                                          ALU.subtract).then_inc(s.lo_done, 1)
                    if n:
                        dve.wait_ge(s.y_ready, n)
                        dve.tensor_copy(y[:, :, (n - 1) * CH:n * CH], y_ps[:, (n - 1) % 2]).then_inc(s.y_kept, 1)

        residual_norm(nc, env, branch=y, bias=y_bias)


def steps_of(kind, half):
    lo, hi = half * CH, (half + 1) * CH
    if kind == "full":
        return [(j, lo, hi) for j in range(S // P)]
    if kind == "causal":
        return [(j, max(lo, j * P), hi) for j in range(hi // P)]
    if kind == "window":
        tiles = [(j, max(lo, j * P), min(hi, j * P + WINQ)) for j in range(S // P)]
        return [t for t in tiles if t[1] < t[2]]
    return [(0, lo, hi)]


def max_pieces(kind):
    out = []
    for t in range(S // P):
        if kind in ("full", "causal"):
            keys = S if kind == "full" else (t + 1) * P
            out += [(t, h, 1, k, min(CH, keys - k), k // CH) for h in range(HU) for k in range(0, keys, CH)]
        elif kind == "window":
            first = max(0, t * P - WIN)
            out += [(t, h, 2, first, (t + 1) * P - first, 0) for h in range(0, HU, 2)]
        else:
            out.append((t, 0, HU, 0, M, 0))
    return out


def attention(nc, env, dram, kind, scale, mask=None):
    cross = kind in ("cross", "xcausal", "xmask")
    nk = M if cross else S
    nkp = M + 1 if cross else S
    kp = M if cross else P
    nkt = 1 if cross else S // P
    halves = S // CH
    steps = [(half, i == 0, i == len(steps_of(kind, half)) - 1, *t)
             for half in range(halves) for i, t in enumerate(steps_of(kind, half))]
    nsteps = len(steps)
    pieces = max_pieces(kind)
    NP = max(p[5] for p in pieces) + 1
    per_unit = len(pieces) + 1
    units = [(b, u) for b in range(NB) for u in range(NU)]
    piece_steps = {"full": range(0, nsteps - 1), "causal": range(0, nsteps - 2),
                   "window": range(2, nsteps - 3)}.get(kind, range(0, 2))
    turn_step = piece_steps[-1] + 1

    def pieces_at(i, spot):
        if i not in piece_steps:
            return range(0)
        n, i = 4 * len(piece_steps), 4 * piece_steps.index(i) + spot
        return range(i * len(pieces) // n, (i + 1) * len(pieces) // n)

    MAXB = 3
    RING = 4
    SLOTS = 4 if cross else 3
    LEAD = 2 if cross else 1
    items = []
    for b in range(NB):
        for m in range(KT):
            items += [(b, "q", m, c * CH, CH) for c in range(S // CH)]
            items += [(b, "k", m, 0, M)] if cross else [(b, "k", m, c * CH, CH) for c in range(S // CH)]
        items += [(b, "v", j, 0, 0) for j in range(nkt)]
    ahead = [i for i, item in enumerate(items) if item[0] == 0]
    later = range(len(ahead) + (1 if cross else 6), len(items))
    opening = [("item", i) for i in range(later[0])]
    for n, i in enumerate(later):
        opening.append(("item", i))
        opening += [("piece", p) for p in range(n * len(pieces) // len(later), (n + 1) * len(pieces) // len(later))]
    qk_items = [i for i, item in enumerate(items) if item[1] != "v"]

    with ExitStack() as st:
        wo = sbuf(nc, st, "wo", [P, NU // 2, D])
        bo = sbuf(nc, st, "bo", [P, KT])
        o = sbuf(nc, st, "o", [P, NU // 2, T])
        with ExitStack() as inner:
            wq = sbuf(nc, inner, "wq", [P, KT, D])
            wk = sbuf(nc, inner, "wk", [P, KT, D])
            wv = sbuf(nc, inner, "wv", [P, KT, D])
            bq = sbuf(nc, inner, "bq", [P, KT])
            bk = sbuf(nc, inner, "bk", [P, KT])
            bv = sbuf(nc, inner, "bv", [P, D]) if "bv" in dram else None
            parts = sbuf(nc, inner, "parts", [P, RING, 2, CH], F32R)
            v = sbuf(nc, inner, "v", [kp, NB, nkt, H, HD + 1])
            qst = sbuf(nc, inner, "qst", [P, SLOTS, HU, S], F32R)
            kst = sbuf(nc, inner, "kst", [P, SLOTS, HU, nkp], F32R)
            prob = sbuf(nc, inner, "prob", [kp, 2, HU, max(hi - lo for _, _, _, _, lo, hi in steps)])
            cmax = sbuf(nc, inner, "cmax", [P, HU, S // P, NP])
            negc = sbuf(nc, inner, "negc", [P, HU * S // P])
            crow = sbuf(nc, inner, "crow", [HU * S // P, P], F32R)
            byq = sbuf(nc, inner, "byq", [P, CH])
            pair = sbuf(nc, inner, "pair", [P, halves, CH])
            inv = sbuf(nc, inner, "inv", [P, CH // (2 * HD)])
            s = sems(nc, "loaded biased cleared proj_ready hi_kept kept written0 written1 written2 written3 stacked0 stacked1 stacked2 stacked3 "
                                "max_ready max_done neg_ready c_loaded s_ready exp_done av_done turned inverted divided evacuated "
                                "acc_cleared")
            max_ps = psum(nc, inner, "max_ps", [P, MAXB, CH])
            st_ps = psum(nc, inner, "st_ps", [P, 2, 2, CH])
            acc = psum(nc, inner, "acc", [P, CH])
            block = inner.enter_context(nc.Block())
            src = env.ctxT if cross else env.xT
            stacked = (s.stacked0, s.stacked1, s.stacked2, s.stacked3)
            written = (s.written0, s.written1, s.written2, s.written3)[:RING]
            PARTS = 4 * 2 + 1
            nload = 4 + sum(n in dram for n in ("bq", "bk", "bo", "bv"))
            nbias = sum(n not in dram for n in ("bq", "bk", "bo"))

            def cleared(slot):
                return 3 + 3 * (slot + 1)

            def proj_ps(i):
                return st_ps[:, i % 4 // 2, i % 2, :]

            @block.sync
            def _(sp):
                for t, n in ((wq, "Wq"), (wk, "Wk"), (wv, "Wv")):
                    sp.dma_start(t[:, :, :], dram[n].rearrange("(k p) n -> p k n", p=P)).then_inc(s.loaded, 16)
                for t, n in ((bq, "bq"), (bk, "bk"), (bo, "bo")):
                    if n in dram:
                        sp.dma_start(t[:, :], dram[n]).then_inc(s.loaded, 16)
                if "bv" in dram:
                    sp.dma_start(bv[:, :], dram["bv"].partition_broadcast(P)).then_inc(s.loaded, 16)
                sp.dma_start(wo[:, :, :], dram["Wo"].rearrange("(g p) n -> p g n", p=P)).then_inc(s.loaded, 16)

                def store(batch, feature_tiles):
                    for j, i in enumerate(qk_items):
                        b, what, m, c, n = items[i]
                        if b == batch and m in feature_tiles:
                            to, n = (env.q_dram, n) if what == "q" else (env.k_dram, n + n % 2)
                            sp.wait_ge(s.kept, i + 1)
                            sp.dma_start(to[b, :, m * P:(m + 1) * P, c:c + n].rearrange("a p n -> p a n"),
                                         parts[:, j % RING, :, 0:n].bitcast(F32)).then_inc(written[j % RING], 16)

                def stack(g):
                    b, u = units[g]
                    if u == 0:
                        for r in range(RING):
                            sp.wait_ge(written[r], 16 * len([j for j, i in enumerate(qk_items) if j % RING == r and items[i][0] <= b]))
                    if g >= SLOTS:
                        sp.wait_ge(s.av_done, nsteps * (g - SLOTS + 1))
                    else:
                        sp.wait_ge(s.cleared, cleared(g))
                    rows = slice(u * HU * HD, (u + 1) * HU * HD)
                    for part in range(2):
                        for twice in range(2):
                            d = slice((2 * part + twice) * HD, (2 * part + twice + 1) * HD)
                            sp.dma_start(qst[d, g % SLOTS, :, :].bitcast(F32),
                                         env.q_dram[b, part, rows, :].rearrange("(h d) n -> d h n", d=HD)).then_inc(stacked[g % SLOTS], 16)
                    for twice in range(2):
                        for part in range(2):
                            d = slice((2 * twice + part) * HD, (2 * twice + part + 1) * HD)
                            sp.dma_start(kst[d, g % SLOTS, :, :].bitcast(F32),
                                         env.k_dram[b, part, rows, 0:nkp].rearrange("(h d) n -> d h n", d=HD)).then_inc(stacked[g % SLOTS], 16)
                    sp.dma_start(qst[STACK:STACK + 1, g % SLOTS, :, :].bitcast(F32),
                                 qst[P - 1:P, g % SLOTS, :, :].bitcast(F32)).then_inc(stacked[g % SLOTS], 16)

                store(0, (0, 1))
                stack(0)
                store(1, (0,))
                stack(1)
                store(1, (1,))
                for g in range(2, len(units)):
                    stack(g)

            @block.gpsimd
            def _(pool):
                for t, n in ((bq, "bq"), (bk, "bk"), (bo, "bo")):
                    if n not in dram:
                        pool.memset(t[:, :], 0.0).then_inc(s.biased, 1)
                pool.memset(parts[:, :, :, :].bitcast(F32), 0.0).then_inc(s.cleared, 1)
                pool.memset(v[:, :, :, :, :], 1.0).then_inc(s.cleared, 1)
                pool.memset(cmax[:, :, :, :], -3e38).then_inc(s.cleared, 1)
                for slot in range(SLOTS):
                    pool.memset(kst[:, slot, :, :].bitcast(F32), 0.0).then_inc(s.cleared, 1)
                    pool.memset(qst[:, slot, :, :].bitcast(F32), 0.0).then_inc(s.cleared, 1)
                    pool.wait_ge(s.cleared, cleared(slot) - 1)
                    pool.memset(kst[STACK:STACK + 1, slot, :, :].bitcast(F32), 1.0).then_inc(s.cleared, 1)
                    pool.wait_ge(s.cleared, cleared(slot))
                for g in range(len(units)):
                    pool.wait_ge(s.max_done, per_unit * (g + 1))
                    pool.dma_start(qst[STACK:STACK + 1, g % SLOTS, :, :].bitcast(F32), crow[:, :].bitcast(F32)).then_inc(s.c_loaded, 16)

            @block.tensor
            def _(pe):
                def piece(gu, i):
                    b = units[gu][0]
                    t, h, nh, k0, n, _ = pieces[i]
                    g = gu * per_unit + i
                    if g >= MAXB:
                        pe.wait_ge(s.max_done, g - MAXB + 1)
                    if i == 0:
                        pe.wait_ge(stacked[gu % SLOTS], 16 * PARTS * (gu // SLOTS + 1))
                    masked = (kind == "causal" and k0 + n == (t + 1) * P) or kind in ("window", "xmask") or \
                             (kind == "xcausal" and t == 0)
                    for a in range(nh):
                        at = a * (CH // nh)
                        ne = n + n % 2
                        mm = pe.matmul(max_ps[:, g % MAXB, at:at + ne], qst[:, gu % SLOTS, h + a, t * P:(t + 1) * P],
                                       kst[:, gu % SLOTS, h + a, k0:k0 + ne], start=(a == 0), stop=(not masked),
                                       skip_group_check=True)
                        if kind == "causal" and masked:
                            mm = pe.matmul(max_ps[:, g % MAXB, n - P:n], env.identb[:, :], env.causal_qk[:, :],
                                           start=False, stop=True, skip_group_check=True)
                        elif kind == "window":
                            mm = pe.matmul(max_ps[:, g % MAXB, at:at + n], env.identb[:, :], env.window_qk[:, WINQ - n:],
                                           start=False, stop=True, skip_group_check=True)
                        elif masked:
                            rows = env.causal_qk[:, 0:M] if kind == "xcausal" else mask.qk[:, b, t, :]
                            mm = pe.matmul(max_ps[:, g % MAXB, at:at + n], env.identb[:, :], rows,
                                           start=False, stop=True, skip_group_check=True)
                    mm.then_inc(s.max_ready, 1)

                def turn(gu):
                    g = gu * per_unit + len(pieces)
                    pe.wait_ge(s.max_done, g - MAXB + 1)
                    pe.wait_ge(s.neg_ready, gu + 1)
                    pe.transpose(max_ps[0:HU * S // P, g % MAXB, 0:P], negc[:, :], env.ident[:, :]).then_inc(s.max_ready, 1)

                def scores(gu, i):
                    b = units[gu][0]
                    half, _, _, j, lo, hi = steps[i]
                    g = gu * nsteps + i
                    masked = (kind == "causal" and lo == j * P) or kind in ("window", "xmask") or \
                             (kind == "xcausal" and half == 0)
                    if g == 0:
                        pe.wait_ge(s.kept, len(items))
                    for p in range(2):
                        if p and gu + LEAD < len(units):
                            for n in pieces_at(i, 0):
                                piece(gu + LEAD, n)
                        if g >= 1:
                            pe.wait_ge(s.exp_done, 2 * (g - 1) + p + 1)
                        for a in range(2):
                            h = 2 * p + a
                            out = st_ps[0:kp, p, a, 0:hi - lo]
                            mm = pe.matmul(out, kst[:, gu % SLOTS, h, j * P:j * P + kp], qst[:, gu % SLOTS, h, lo:hi],
                                           start=True, stop=(not masked), skip_group_check=True)
                            if masked and kind in ("causal", "xcausal"):
                                mm = pe.matmul(out[:, 0:P], env.identb[:, 0:kp], env.causal_kq[:, :],
                                               start=False, stop=True, skip_group_check=True)
                            elif kind == "window":
                                mm = pe.matmul(out, env.identb[:, :], env.window_kq[:, lo - j * P:hi - j * P],
                                               start=False, stop=True, skip_group_check=True)
                            elif masked:
                                mm = pe.matmul(out, env.identb[0:M, 0:M], mask.kq[:, b, lo:hi],
                                               start=False, stop=True, skip_group_check=True)
                        mm.then_inc(s.s_ready, 1)

                def values(gu, i):
                    b, u = units[gu]
                    half, first, final, j, lo, hi = steps[i]
                    g = gu * nsteps + i
                    hc = gu * halves + half
                    pe.wait_ge(s.exp_done, 2 * (g + 1))
                    if first and hc >= 1:
                        pe.wait_ge(s.turned, hc)
                    for a in range(HU):
                        if a == 2 and gu + LEAD < len(units):
                            for n in pieces_at(i + 1, 2):
                                piece(gu + LEAD, n)
                        mm = pe.matmul(acc[32 * a:32 * a + HD + 1, lo - half * CH:hi - half * CH],
                                       v[:, b, j, u * HU + a, :], prob[:, g % 2, a, 0:hi - lo],
                                       start=first, stop=final, skip_group_check=True)
                    mm.then_inc(s.av_done, 1)

                pe.wait_ge(s.loaded, 16 * nload)
                def project(i):
                    b, what, m, c, n = items[i]
                    if i >= 4:
                        pe.wait_ge(s.kept, i - 3)
                    for k in range(KT):
                        if what == "q":
                            mm = pe.matmul(proj_ps(i)[:, 0:n], wq[:, k, m * P:(m + 1) * P],
                                           env.xT[:, k, b * S + c:b * S + c + n], start=(k == 0), stop=(k == KT - 1))
                        elif what == "k":
                            mm = pe.matmul(proj_ps(i)[:, 0:n], wk[:, k, m * P:(m + 1) * P],
                                           src[:, k, b * nk + c:b * nk + c + n], start=(k == 0), stop=(k == KT - 1))
                        else:
                            mm = pe.matmul(proj_ps(i)[0:kp, 0:D], src[:, k, b * nk + m * kp:b * nk + (m + 1) * kp],
                                           wv[:, k, :], start=(k == 0), stop=(k == KT - 1))
                    mm.then_inc(s.proj_ready, 1)

                for n, (what, i) in enumerate(opening):
                    if n == later[0]:
                        pe.wait_ge(s.acc_cleared, 1)
                    project(i) if what == "item" else piece(0, i)
                turn(0)
                for gu in range(1, LEAD):
                    for i in range(len(pieces)):
                        piece(gu, i)
                    turn(gu)
                for gu in range(len(units)):
                    pe.wait_ge(s.c_loaded, 16 * (gu + 1))
                    for i in range(nsteps):
                        scores(gu, i)
                        if gu + LEAD < len(units):
                            for n in pieces_at(i, 1):
                                piece(gu + LEAD, n)
                        if i:
                            values(gu, i - 1)
                        if gu + LEAD < len(units):
                            for n in pieces_at(i, 3) if i else (*pieces_at(i, 2), *pieces_at(i, 3)):
                                piece(gu + LEAD, n)
                            if i == turn_step:
                                turn(gu + LEAD)
                    values(gu, nsteps - 1)
                    if gu + LEAD < len(units) and turn_step == nsteps:
                        turn(gu + LEAD)

            @block.scalar
            def _(act):
                act.wait_ge(s.loaded, 16 * nload)
                if nbias:
                    act.wait_ge(s.biased, nbias)
                act.wait_ge(s.cleared, 1)
                for j, i in enumerate(qk_items):
                    b, what, m, c, n = items[i]
                    bias = bq if what == "q" else bk
                    if j >= RING:
                        act.wait_ge(written[j % RING], 16 * (j // RING))
                    act.wait_ge(s.proj_ready, i + 1)
                    act.activation(parts[:, j % RING, 0, 0:n], proj_ps(i)[:, 0:n], ACT.Identity, bias=bias[:, m:m + 1])\
                       .then_inc(s.hi_kept, 1)
                for gu in range(len(units)):
                    for i, (_, _, _, _, lo, hi) in enumerate(steps):
                        g = gu * nsteps + i
                        for p in range(2):
                            if g >= 2:
                                act.wait_ge(s.av_done, g - 1)
                            act.wait_ge(s.s_ready, 2 * g + p + 1)
                            act.activation(prob[:, g % 2, 2 * p:2 * p + 2, 0:hi - lo], st_ps[0:kp, p, :, 0:hi - lo],
                                           ACT.Exp, scale=scale).then_inc(s.exp_done, 1)

            @block.vector
            def _(dve):
                def piece(gu, i):
                    t, h, nh, _, n, part = pieces[i]
                    g = gu * per_unit + i
                    dve.wait_ge(s.max_ready, g + 1)
                    if i == 0 and gu >= 1:
                        dve.wait_ge(s.neg_ready, gu)
                    dve.tensor_reduce(cmax[:, h:h + nh, t, part],
                                      max_ps[:, g % MAXB, :].rearrange("p (a n) -> p a n", a=nh)[:, :, 0:n],
                                      AX.X, ALU.max).then_inc(s.max_done, 1)

                def turn(gu):
                    g = gu * per_unit + len(pieces)
                    dve.wait_ge(s.max_done, g)
                    if gu >= 1:
                        dve.wait_ge(s.max_ready, g - per_unit + 1)
                    dve.tensor_reduce(negc[:, :], cmax[:, :, :, :].rearrange("p h t a -> p (h t) a"), AX.X, ALU.max,
                                      negate=True).then_inc(s.neg_ready, 1)
                    dve.wait_ge(s.max_ready, g + 1)
                    if gu >= 1:
                        dve.wait_ge(s.c_loaded, 16 * gu)
                    dve.tensor_copy(crow[:, :], max_ps[0:HU * S // P, g % MAXB, 0:P]).then_inc(s.max_done, 1)

                def evacuate(gu, half, step):
                    b, u = units[gu]
                    hc = gu * halves + half
                    dve.wait_ge(s.av_done, gu * nsteps + step + 1)
                    if hc >= 1:
                        dve.wait_ge(s.divided, hc)
                    dve.transpose(byq[:, :], acc[:, :]).then_inc(s.turned, 1)
                    dve.wait_ge(s.turned, hc + 1)
                    blocks = byq[:, :].rearrange("p (n r) -> p n r", r=2 * HD)
                    to = pair[:, half, :].rearrange("p (n r) -> p n r", r=2 * HD)[:, :, u % 2 * HD:(u % 2 + 1) * HD]
                    dve.reciprocal(inv[:, :], blocks[:, :, HD]).then_inc(s.inverted, 1)
                    dve.wait_ge(s.inverted, hc + 1)
                    if gu >= 2:
                        dve.wait_ge(s.evacuated, halves * (gu // 2 - 1) + half + 1)
                    dve.tensor_tensor(to, blocks[:, :, 0:HD], last(inv[:, :], HD), ALU.mult).then_inc(s.divided, 1)
                    if u % 2:
                        dve.wait_ge(s.divided, hc + 1)
                        dve.transpose(o[:, u // 2, b * S + half * CH:b * S + (half + 1) * CH], pair[:, half, :]).then_inc(s.evacuated, 1)

                dve.wait_ge(s.loaded, 16 * nload)
                if nbias:
                    dve.wait_ge(s.biased, nbias)
                dve.memset(acc[:, :], 0.0).then_inc(s.acc_cleared, 1)
                dve.wait_ge(s.cleared, 2)
                def project(i):
                    b, what, m, c, n = items[i]
                    if what == "v":
                        dve.wait_ge(s.proj_ready, i + 1)
                        to, product = v[:, b, m, :, 0:HD], proj_ps(i)[0:kp, 0:D].rearrange("p (h d) -> p h d", h=H)
                        if bv is None:
                            dve.tensor_copy(to, product).then_inc(s.kept, 1)
                        else:
                            dve.tensor_tensor(to, product, bv[0:kp, :].rearrange("p (h d) -> p h d", h=H), ALU.add)\
                               .then_inc(s.kept, 1)
                    else:
                        j = qk_items.index(i)
                        bias = bq if what == "q" else bk
                        dve.wait_ge(s.hi_kept, j + 1)
                        dve.scalar_tensor_tensor(out=parts[:, j % RING, 1, 0:n], in0=proj_ps(i)[:, 0:n], scalar=bias[:, m:m + 1],
                                                 in1=parts[:, j % RING, 0, 0:n].bitcast(F32), op0=ALU.add, op1=ALU.subtract)\
                           .then_inc(s.kept, 1)

                for n, (what, i) in enumerate(opening):
                    if n == later[0]:
                        dve.wait_ge(s.cleared, 3)
                    project(i) if what == "item" else piece(0, i)
                turn(0)
                for gu in range(1, LEAD):
                    for i in range(len(pieces)):
                        piece(gu, i)
                    turn(gu)
                for gu in range(len(units)):
                    for i in range(nsteps):
                        for spot in range(4):
                            if spot == 3 and i and steps[i - 1][2]:
                                evacuate(gu, steps[i - 1][0], i - 1)
                            if gu + LEAD < len(units):
                                for n in pieces_at(i, spot):
                                    piece(gu + LEAD, n)
                        if gu + LEAD < len(units) and i == turn_step:
                            turn(gu + LEAD)
                    if gu + LEAD < len(units) and turn_step == nsteps:
                        turn(gu + LEAD)
                    evacuate(gu, steps[-1][0], nsteps - 1)

        def project(pe, n, out):
            for m in range(KT):
                for g in range(NU // 2):
                    mm = pe.matmul(out[:, m, :], wo[:, g, m * P:(m + 1) * P], o[:, g, n * CH:(n + 1) * CH],
                                   start=(g == 0), stop=(g == NU // 2 - 1))
            return mm

        residual_norm(nc, env, branch_matmuls=project, bias=bo)


def mask_tiles(nc, st, env, m_qk, m_kq, cols, dt, op, value, name):
    t = named(qk=sbuf(nc, st, name + "_qk", [P, NB, S // P, M], BF16), kq=sbuf(nc, st, name + "_kq", [M, NB, S], BF16))
    with ExitStack() as inner:
        raw_qk = sbuf(nc, inner, "raw_qk", [P, NB, S // P, M], dt)
        raw_kq = sbuf(nc, inner, "raw_kq", [M, NB, cols], dt)
        s = sems(nc, "loaded")
        block = inner.enter_context(nc.Block())

        @block.sync
        def _(sp):
            for b in range(NB):
                sp.dma_start(raw_qk[:, b], m_qk(b)).then_inc(s.loaded, 16)
                sp.dma_start(raw_kq[:, b], m_kq(b)).then_inc(s.loaded, 16)

        @block.vector
        def _(dve):
            dve.wait_ge(s.loaded, 64)
            for b in range(NB):
                dve.tensor_scalar(t.qk[:, b], raw_qk[:, b], 0, value, op, ALU.mult)
                dve.tensor_scalar(t.kq[:, b], raw_kq[:, b].broadcast_to([M, S]), 0, value, op, ALU.mult)
    return t


def moe(nc, env, dram, E, F, topk, glu, score, shared, per=1):
    NF = per * F // P
    NG = (E + shared) // per
    CT = 1024
    HV = CT // CH
    peel = NG - 2 * ((NG - 2) // 2)
    biased = "b1" in dram
    NW = 2 if glu else 1
    NWE = NW * KT * per * F + NF * D
    R = 2 if glu else 4
    with ExitStack() as st:
        y = sbuf(nc, st, "y", [P, KT, T])
        y_bias = sbuf(nc, st, "y_bias", [P, KT])
        with ExitStack() as inner:
            x_hi = sbuf(nc, inner, "x_hi", [P, KT, T], F32R)
            x_lo = sbuf(nc, inner, "x_lo", [P, KT, T], F32R)
            gT = sbuf(nc, inner, "gT", [E, T])
            b2 = sbuf(nc, inner, "b2", [E, D])
            wr = sbuf(nc, inner, "wr", [P, KT, E])
            rb = sbuf(nc, inner, "rb", [P, E])
            rs = sbuf(nc, inner, "rs", [P, 1])
            sc = sbuf(nc, inner, "sc", [P, NT, E])
            rowmax = sbuf(nc, inner, "rowmax", [P, NT])
            before = sbuf(nc, inner, "before", [P, E, E])
            rank = sbuf(nc, inner, "rank", [P, NT, E])
            above = sbuf(nc, inner, "above", [P, NT, E])
            total = sbuf(nc, inner, "total", [P, NT])
            raw = sbuf(nc, inner, "raw", [P, 2, NWE])
            w_hi = sbuf(nc, inner, "w_hi", [P, 2, NWE], F32R)
            w_lo = sbuf(nc, inner, "w_lo", [P, 2, NWE], F32R)
            gate = sbuf(nc, inner, "gate", [P, 2, per, CT])
            b1 = sbuf(nc, inner, "b1", [P, 2, NF])
            lift = sbuf(nc, inner, "lift", [P, 4, CH])
            hid_hi = sbuf(nc, inner, "hid_hi", [P, HV, NF, CH], F32R)
            hid_lo = sbuf(nc, inner, "hid_lo", [P, HV, NF, CH], F32R)
            beats = y[:, :, :].rearrange("p k t -> p (k t)")[:, 0:NT * E * E].rearrange("p (t a b) -> p t a b", a=E, b=E)
            s = sems(nc, "loaded ones_ready before_ready x_hi_ready x_lo_ready logit_ready chain acted gate_ready turned kept stored "
                         "w_ready0 w_ready1 g_ready0 g_ready1 w_hi_done w_split hid_ready hid_free act_ready gated hid_hi_done "
                         "mul_done y_done chunk_done")
            hid_ps = psum(nc, inner, "hid_ps", [P, R, NW, CH])
            y_ps = psum(nc, inner, "y_ps", [P, HV, KT, CH])
            log_ps = hid_ps[:, 0, 0, 0:NT * E].rearrange("p (t e) -> p t e", e=E)
            gT_ps = y_ps[0:E].rearrange("e h m n -> e (h m n)")
            block = inner.enter_context(nc.Block())
            loads = 1 + ("router_b" in dram) + ("route_scale" in dram) + ("b2" in dram) + ("bs2" in dram)
            w_ready = (s.w_ready0, s.w_ready1)
            g_ready = (s.g_ready0, s.g_ready1)
            gates = dram["gates"].rearrange("(g e) t -> g e t", e=per)

            def up_w(w, slot, a, kk, f):
                at = (a * KT + kk) * per * F + f * P
                return w[:, slot, at:at + P]

            def down_w(w, slot, f, m):
                at = NW * KT * per * F + f * D + m * P
                return w[:, slot, at:at + P]

            def bank(slot, half, f, ring):
                return ((slot * HV + half) * NF + f) % ring

            def turns(eng, first, turn):
                for i in range(peel):
                    turn(first + i, i, (first + i) % 2, (first + i) // 2 + 1)
                if NG > peel:
                    with eng.Fori(0, (NG - peel) // 2) as i:
                        for j in range(2):
                            k = i * 2 + (first + peel + j)
                            turn(k, i * 2 + (peel + j), (first + peel + j) % 2, i + ((first + peel + j) // 2 + 1))

            @block.sync
            def _(sp):
                sp.dma_start(wr[:, :, :], dram["Wr"].rearrange("(k p) n -> p k n", p=P)).then_inc(s.loaded, 16)
                if "router_b" in dram:
                    sp.dma_start(rb[:, :], dram["router_b"].partition_broadcast(P)).then_inc(s.loaded, 16)
                if "route_scale" in dram:
                    sp.dma_start(rs[:, :], dram["route_scale"].partition_broadcast(P)).then_inc(s.loaded, 16)
                if "b2" in dram:
                    sp.dma_start(b2[:, :], dram["b2"]).then_inc(s.loaded, 16)
                if "bs2" in dram:
                    sp.dma_start(y_bias[:, :], dram["bs2"]).then_inc(s.loaded, 16)
                opened = [False]

                for c in range(T // CT):
                    def turn(k, e, slot, uses):
                        sp.wait_ge(s.w_split, k + 1)
                        for a, n in enumerate(("W1", "Wu")[:NW]):
                            to = raw[:, slot, a * KT * per * F:(a + 1) * KT * per * F].rearrange("p (k f) -> p k f", k=KT)
                            sp.dma_start(to, dram[n][e].rearrange("(k p) f -> p k f", p=P)).then_inc(w_ready[slot], 16)
                        to = raw[:, slot, NW * KT * per * F:].rearrange("p (f n) -> p f n", n=D)
                        sp.dma_start(to, dram["W2"][e].rearrange("(f p) n -> p f n", p=P)).then_inc(w_ready[slot], 16)
                        if not opened[0]:
                            if shared:
                                sp.dma_start(dram["gates"][0].rearrange("(p n) -> p n", p=P), env.ones[:, 0:T // P]).then_inc(s.stored, 16)
                            sp.wait_ge(s.kept, 1)
                            sp.dma_start(dram["gates"][shared:, :], gT[:, :]).then_inc(s.stored, 16)
                            sp.wait_ge(s.stored, 16 * (1 + shared))
                            opened[0] = True
                        sp.wait_ge(s.y_done, k * HV)
                        if biased:
                            sp.dma_start(b1[:, slot], dram["b1"][e]).then_inc(g_ready[slot], 16)
                        sp.dma_start(gate[:, slot], gates[e, :, c * CT:(c + 1) * CT].partition_broadcast(P)).then_inc(g_ready[slot], 16)
                    turns(sp, c * NG, turn)

            @block.gpsimd
            def _(pool):
                pool.sem_inc(s.w_split, 2)
                pool.sem_inc(s.y_done, 2)
                pool.sem_inc(s.hid_free if glu else s.act_ready, R)
                pool.sem_inc(s.mul_done, 4)
                pool.memset(before[:, :, :], 1.0).then_inc(s.ones_ready, 1)
                pool.wait_ge(s.ones_ready, 1)
                pool.affine_select(out=before[:, :, :], in_=before[:, :, :], compare_op=ALU.is_gt, fill=0.0, base=0,
                                   pattern=[[1, E], [-1, E]], channel_multiplier=0).then_inc(s.before_ready, 1)
                pool.wait_ge(s.before_ready, 1)
                for c in range(T // CT):
                    def turn(k, e, slot, uses):
                        pool.wait_ge(w_ready[slot], uses * (16 * (NW + 1)))
                        pool.wait_ge(s.y_done, k * HV)
                        pool.tensor_tensor(w_hi[:, slot, :], raw[:, slot, :], env.ones[:, 0:1].broadcast_to([P, NWE]),
                                           ALU.mult).then_inc(s.w_hi_done, 1)
                        pool.wait_ge(s.w_hi_done, k + 1)
                        pool.tensor_tensor(w_lo[:, slot, :], raw[:, slot, :], w_hi[:, slot, :].bitcast(F32), ALU.subtract)\
                            .then_inc(s.w_split, 1)
                        pool.wait_ge(s.w_split, k + 3)
                    turns(pool, c * NG, turn)

            @block.tensor
            def _(pe):
                pe.wait_ge(s.loaded, 16 * loads)
                for t in range(NT):
                    for k in range(KT):
                        mm = pe.matmul(log_ps[:, t, :], env.xT[:, k, t * P:(t + 1) * P], wr[:, k, :],
                                       start=(k == 0), stop=(k == KT - 1))
                mm.then_inc(s.logit_ready, 1)
                pe.wait_ge(s.gate_ready, 1)
                for t in range(NT):
                    mm = pe.transpose(gT_ps[:, t * P:(t + 1) * P], sc[:, t, :], env.ident[:, :])
                mm.then_inc(s.turned, 1)
                pe.wait_ge(s.x_lo_ready, KT)
                pe.wait_ge(s.kept, 1)
                for c in range(T // CT):
                    def hidden(k, slot, half):
                        for f in range(NF):
                            n = (k * HV + half) * NF + f
                            pe.wait_ge(s.hid_free if glu else s.act_ready, n + 1)
                            for a in range(NW):
                                for kk in range(KT):
                                    for i, (w, x) in enumerate(((w_hi, x_hi), (w_hi, x_lo), (w_lo, x_hi))):
                                        mm = pe.matmul(hid_ps[:, bank(slot, half, f, R), a, :], up_w(w, slot, a, kk, f),
                                                       x[:, kk, c * CT + half * CH:c * CT + (half + 1) * CH],
                                                       start=(kk == 0 and i == 0), stop=(kk == KT - 1 and i == 2))
                            mm.then_inc(s.hid_ready, 1)

                    def down(k, slot, half, opens, closes):
                        pe.wait_ge(s.mul_done, (k * HV + half) * NF + (NF + 4))
                        for m in range(KT):
                            for f in range(NF):
                                for i, (w, h) in enumerate(((w_hi, hid_hi), (w_hi, hid_lo), (w_lo, hid_hi))):
                                    mm = pe.matmul(y_ps[:, half, m, :], down_w(w, slot, f, m), h[:, half, f, :],
                                                   start=(opens and f == 0 and i == 0), stop=(closes and f == NF - 1 and i == 2),
                                                   skip_group_check=True)
                        mm.then_inc(s.y_done, 1)

                    if c:
                        pe.wait_ge(s.chunk_done, HV * c)
                    if "b2" in dram:
                        for half in range(HV):
                            for m in range(KT):
                                pe.matmul(y_ps[:, half, m, :], b2[:, m * P:(m + 1) * P],
                                          gT[:, c * CT + half * CH:c * CT + (half + 1) * CH], start=True, stop=False,
                                          skip_group_check=True)
                    opens_with = "b2" not in dram
                    first = [True]
                    first_down = [True]

                    def turn(k, e, slot, uses):
                        pe.wait_ge(s.w_split, k + 3)
                        hidden(k, slot, 0)
                        if not first[0]:
                            down(k - 1, 1 - slot, 1, opens_with and first_down[0], False)
                            first_down[0] = False
                        hidden(k, slot, 1)
                        down(k, slot, 0, opens_with and first[0], False)
                        first[0] = False

                    turns(pe, c * NG, turn)
                    k = (c + 1) * NG - 1
                    down(k, k % 2, 1, False, True)

            @block.scalar
            def _(act):
                for k in range(KT):
                    act.activation(x_hi[:, k, :], env.xT[:, k, :], ACT.Copy).then_inc(s.x_hi_ready, 1)
                act.wait_ge(s.chain, 3 if score == "softmax" else 1)
                act.activation(sc[:, :, :], sc[:, :, :], ACT.Exp if score == "softmax" else ACT.Sigmoid).then_inc(s.acted, 1)
                for c in range(T // CT):
                    def turn(k, e, slot, uses):
                        if biased:
                            act.wait_ge(g_ready[slot], uses * (16 * 2))
                        for half in range(HV):
                            for f in range(NF):
                                n = (k * HV + half) * NF + f
                                act.wait_ge(s.hid_ready, n + 1)
                                act.wait_ge(s.mul_done, n + 1)
                                ins = hid_ps[:, bank(slot, half, f, R), 0, :]
                                out = lift[:, bank(slot, half, f, 4), :]
                                if glu:
                                    act.activation(out, ins, ACT.Silu).then_inc(s.act_ready, 1)
                                else:
                                    act.activation(out, ins, ACT.Gelu, bias=b1[:, slot, f:f + 1]).then_inc(s.act_ready, 1)
                    turns(act, c * NG, turn)

            @block.vector
            def _(dve):
                done = [0]

                def link(ins):
                    done[0] += 1
                    ins.then_inc(s.chain, 1)
                    dve.wait_ge(s.chain, done[0])

                dve.wait_ge(s.loaded, 16 * loads)
                dve.wait_ge(s.logit_ready, 1)
                if "router_b" in dram:
                    link(dve.tensor_tensor(sc[:, :, :], log_ps, over(rb[:, :], NT), ALU.add))
                else:
                    link(dve.tensor_copy(sc[:, :, :], log_ps))
                if score == "softmax":
                    link(dve.tensor_reduce(rowmax[:, :], sc[:, :, :], AX.X, ALU.max))
                    link(dve.tensor_tensor(sc[:, :, :], sc[:, :, :], last(rowmax[:, :], E), ALU.subtract))
                for k in range(KT):
                    dve.wait_ge(s.x_hi_ready, k + 1)
                    dve.tensor_tensor(x_lo[:, k, :], env.xT[:, k, :], x_hi[:, k, :].bitcast(F32), ALU.subtract).then_inc(s.x_lo_ready, 1)
                dve.wait_ge(s.acted, 1)
                if "route_scale" in dram:
                    link(dve.tensor_scalar(sc[:, :, :], sc[:, :, :], rs[:, 0:1], None, ALU.mult))
                own = sc[:, :, :].unsqueeze(3).broadcast_to([P, NT, E, E])
                other = sc[:, :, :].unsqueeze(2).broadcast_to([P, NT, E, E])
                dve.wait_ge(s.before_ready, 1)
                link(dve.tensor_tensor(beats, other, own, ALU.is_equal))
                link(dve.tensor_tensor(beats, beats, before[:, :, :].unsqueeze(1).broadcast_to([P, NT, E, E]), ALU.mult))
                link(dve.tensor_reduce(rank[:, :, :], beats, AX.X, ALU.add))
                link(dve.tensor_tensor(beats, other, own, ALU.is_gt))
                link(dve.tensor_reduce(above[:, :, :], beats, AX.X, ALU.add))
                link(dve.tensor_tensor(rank[:, :, :], rank[:, :, :], above[:, :, :], ALU.add))
                link(dve.tensor_scalar(rank[:, :, :], rank[:, :, :], float(topk), None, ALU.is_lt))
                link(dve.tensor_tensor(sc[:, :, :], sc[:, :, :], rank[:, :, :], ALU.mult))
                link(dve.tensor_reduce(total[:, :], sc[:, :, :], AX.X, ALU.add))
                link(dve.reciprocal(total[:, :], total[:, :]))
                dve.tensor_tensor(sc[:, :, :], sc[:, :, :], last(total[:, :], E), ALU.mult).then_inc(s.gate_ready, 1)
                dve.wait_ge(s.turned, 1)
                dve.tensor_copy(gT[:, :], gT_ps).then_inc(s.kept, 1)

                for c in range(T // CT):
                    def turn(k, e, slot, uses):
                        dve.wait_ge(g_ready[slot], uses * (16 * (1 + biased)))
                        for half in range(HV):
                            dve.wait_ge(s.y_done, k * HV + (half + 1))
                            for f in range(NF):
                                n = (k * HV + half) * NF + f
                                dve.wait_ge(s.act_ready, n + (1 if glu else R + 1))
                                up = lift[:, bank(slot, half, f, 4), :]
                                if glu:
                                    dve.tensor_tensor(up, up, hid_ps[:, bank(slot, half, f, R), 1, :], ALU.mult).then_inc(s.hid_free, 1)
                                    dve.wait_ge(s.hid_free, n + (R + 1))
                                dve.tensor_tensor(up, up, gate[:, slot, f * per // NF, half * CH:(half + 1) * CH], ALU.mult).then_inc(s.gated, 1)
                                dve.wait_ge(s.gated, n + 1)
                                dve.tensor_copy(hid_hi[:, half, f, :], up).then_inc(s.hid_hi_done, 1)
                                dve.wait_ge(s.hid_hi_done, n + 1)
                                dve.tensor_tensor(hid_lo[:, half, f, :], up, hid_hi[:, half, f, :].bitcast(F32), ALU.subtract)\
                                   .then_inc(s.mul_done, 1)
                    turns(dve, c * NG, turn)
                    dve.wait_ge(s.y_done, (c + 1) * NG * HV + 2)
                    for half in range(HV):
                        at = c * CT + half * CH
                        dve.tensor_copy(y[:, :, at:at + CH], y_ps[:, half]).then_inc(s.chunk_done, 1)

        residual_norm(nc, env, branch=y, bias=y_bias if "bs2" in dram else None)


def decoder(nc, d, out, stages=STAGES):
    def group(prefix):
        return {n[len(prefix):]: a for n, a in d.items() if n.startswith(prefix)}

    def space(prefix):
        return named(**group(prefix))

    with ExitStack() as st:
        env = named(
            q_dram=d["q_dram"], k_dram=d["k_dram"],
            xT=sbuf(nc, st, "xT", [P, KT, T]), ctxT=sbuf(nc, st, "ctxT", [P, KT, NB * M]),
            ident=sbuf(nc, st, "ident", [P, P]), identb=sbuf(nc, st, "identb", [P, P], BF16),
            avg=sbuf(nc, st, "avg", [P, P]), eps=sbuf(nc, st, "eps", [P, 1]), ones=sbuf(nc, st, "ones", [P, P]),
            causal_qk=sbuf(nc, st, "causal_qk", [P, P], BF16), causal_kq=sbuf(nc, st, "causal_kq", [P, P], BF16),
            window_qk=sbuf(nc, st, "window_qk", [P, WINQ], BF16), window_kq=sbuf(nc, st, "window_kq", [P, WINQ], BF16))
        stored = st.enter_context(nc.semaphore("stored"))
        setup(nc, env, space("in_"))

        def pad_attention():
            def pad_mask(b):
                return d["pad_mask"][b].unsqueeze(0).unsqueeze(0).broadcast_to([P, S // P, M])
            with ExitStack() as ms:
                t = mask_tiles(nc, ms, env, pad_mask, lambda b: d["pad_mask"][b].unsqueeze(1), 1, U8,
                               ALU.not_equal, MASKED, "pad")
                attention(nc, env, group("L2x_"), "xmask", float(8 ** -0.5), t)

        def masked_attention():
            with ExitStack() as ms:
                t = mask_tiles(nc, ms, env, lambda b: d["mask_qk"][b].rearrange("(t p) m -> p t m", p=P),
                               lambda b: d["mask_kq"][b], S, I32, ALU.is_equal, NEG, "seen")
                attention(nc, env, group("L3x_"), "xmask", float(HD ** -0.5), t)

        def layer0():
            with ExitStack() as ws:
                down = named(w=sbuf(nc, ws, "down_w", [P, KT, FF]), tmp=sbuf(nc, ws, "down_tmp", [P, KT, FF]),
                             coef=sbuf(nc, ws, "down_coef", [P, 2, 2, FF]))
                weights = group("L0f_")
                min_gru(nc, env, group("L0a_"), down_stages(nc, weights, down, 0, NS // 2))
                wide_cross(nc, env, space("L0x_"), down_stages(nc, weights, down, NS // 2, NS - NS // 2))
                butterfly_ffn(nc, env, space("L0f_"), down)

        plan = [
            layer0,
            lambda: attention(nc, env, group("L1a_"), "causal", float(HD ** -0.5)),
            lambda: attention(nc, env, group("L1x_"), "xcausal", float(HD ** -0.5)),
            lambda: moe(nc, env, group("L1f_"), 8, 512, 2, True, "softmax", 1),
            lambda: attention(nc, env, group("L2a_"), "full", float(D ** -0.5)),
            pad_attention,
            lambda: moe(nc, env, group("L2f_"), 8, 128, 2, False, "sigmoid", 1, per=3),
            lambda: attention(nc, env, group("L3a_"), "window", float(HD ** -0.5)),
            masked_attention,
            lambda: moe(nc, env, group("L3f_"), 16, 512, 4, False, "softmax", 0),
        ]
        for stage in plan[:stages] if isinstance(stages, int) else [plan[i] for i in stages]:
            with nc.cleanup_on_exit():
                stage()
        with nc.Block() as block:
            @block.sync
            def _(sp):
                sp.dma_start(out.rearrange("(k p) t -> p k t", p=P), env.xT[:, :, :]).then_inc(stored, 16)
                sp.wait_ge(stored, 16)


def layouts(i):
    import numpy as np

    c = np.ascontiguousarray
    a = {n: np.asarray(x) for n, x in i.items()}
    r = {}

    def columns(b):
        return c(np.swapaxes(b.reshape(*b.shape[:-1], -1, P), -1, -2))

    r["in_xT"] = c(a["x"].reshape(T, D).T)
    r["in_ctxT"] = c(a["ctx_1024"].reshape(NB * M, D).T)
    r["pad_mask"] = c(a["mask_BxS2_bf0"])
    r["mask_qk"] = c(a["mask_Bx1xSxS2_ik1"][:, 0])
    r["mask_kq"] = c(a["mask_Bx1xSxS2_ik1"][:, 0].transpose(0, 2, 1))
    for n in "ifh":
        r["L0a_w_" + n] = columns(a["L0_attn_w_" + n])
    qkv = a["L0_xattn_qkv_w"]
    r["L0x_wq"], r["L0x_wkT"], r["L0x_wvT"] = c(qkv[:D]), c(qkv[D:2 * D].T), c(qkv[2 * D:].T)
    r["L0x_projT"], r["L0x_proj_b"], r["L0x_mask"] = c(a["L0_xattn_proj_w"].T), columns(a["L0_xattn_proj_b"]), a["mask_S2_ik0"]
    for n in ("W_exp", "b_exp"):
        r["L0f_" + n] = a["L0_ffn_" + n]
    for n in ("up_bias", "b_con", "down_bias"):
        r["L0f_" + n] = columns(a["L0_ffn_" + n])
    r["L0f_W_conT"] = c(a["L0_ffn_W_con"].T)
    for n, w, flip in (("up", a["L0_ffn_up_weights"], False), ("down", a["L0_ffn_down_weights"], True)):
        coef = np.empty((w.shape[0], 2, 2 * w.shape[1]), w.dtype)
        for s in range(w.shape[0]):
            ws = w[s].reshape(-1, 2 ** s, 2, 2)
            own = np.stack([ws[..., 0, 0], ws[..., 1, 1]], 1)
            par = np.stack([ws[..., 1, 0], ws[..., 0, 1]] if flip else [ws[..., 0, 1], ws[..., 1, 0]], 1)
            coef[s, 0], coef[s, 1] = own.reshape(-1), par.reshape(-1)
        r[f"L0f_{n}_coef"] = coef

    def paired_rows(w):
        return c(w.reshape(NU // 2, 2, HU, HD, -1).swapaxes(1, 2).reshape(w.shape))

    for n in ("Wq", "Wk", "Wv", "bv"):
        r["L1a_" + n] = a["L1_attn_" + n]
    for n in ("bq", "bk", "bo"):
        r["L1a_" + n] = columns(a["L1_attn_" + n])
    r["L1a_Wo"] = paired_rows(a["L1_attn_Wo"])
    for p, q in (("L1x_", "L1_xattn_"), ("L3a_", "L3_attn_"), ("L3x_", "L3_xattn_")):
        for n in ("Wq", "Wk", "Wv"):
            r[p + n] = c(a[q + n].T)
        r[p + "Wo"] = paired_rows(a[q + "Wo"].T)
    for n in ("Wq", "Wk", "Wv"):
        big = np.zeros((H, HD, H, HD), a["L2_attn_" + n].dtype)
        for h in range(H):
            big[h, :, h, :] = a["L2_attn_" + n].T
        r["L2a_" + n] = big.reshape(D, D)
    r["L2a_Wo"], r["L2a_bo"] = paired_rows(a["L2_attn_W_out"].T), columns(a["L2_attn_b_out"])
    for n in ("q", "k"):
        w, bias = a["L2_xattn_W" + n], a["L2_xattn_b" + n]
        big, bb = np.zeros((D, H, HD), w.dtype), np.zeros((H, HD), bias.dtype)
        hq = w.shape[1] // (H // 2)
        big[:, :, :hq] = np.repeat(w.reshape(D, H // 2, hq), 2, 1)
        bb[:, :hq] = np.repeat(bias.reshape(H // 2, hq), 2, 0)
        r["L2x_W" + n], r["L2x_b" + n] = big.reshape(D, D), columns(bb.reshape(D))
    r["L2x_Wv"] = np.eye(D, dtype=np.float32)
    r["L2x_Wo"] = paired_rows(np.eye(D, dtype=np.float32))

    def grouped(shared, experts, per, rows):
        w = np.concatenate([shared[None], experts])
        w = w.reshape(-1, per, *w.shape[1:])
        w = w if rows else w.swapaxes(1, 2)
        return c(w.reshape(w.shape[0], -1, w.shape[-1]) if rows else w.reshape(*w.shape[:2], -1))

    r["L1f_Wr"] = a["L1_ffn_Wr"]
    for n, m, sm in (("W1", "Wg", "Sg"), ("Wu", "Wu", "Su"), ("W2", "Wd", "Sd")):
        r["L1f_" + n] = grouped(a["L1_ffn_" + sm].reshape(a["L1_ffn_" + m].shape[1:]), a["L1_ffn_" + m], 1, True)
    for n, m in (("Wr", "gate_W"), ("b2", "b2")):
        r["L2f_" + n] = a["L2_ffn_" + m]
    for n, m, sm, rows in (("W1", "W1", "Ws1", False), ("W2", "W2", "Ws2", True)):
        r["L2f_" + n] = grouped(a["L2_ffn_" + sm].reshape(a["L2_ffn_" + m].shape[1:]), a["L2_ffn_" + m], 3, rows)
    r["L2f_bs2"] = columns(a["L2_ffn_bs2"])
    r["L2f_b1"] = columns(np.concatenate([a["L2_ffn_bs1"].reshape(1, -1), a["L2_ffn_b1"]]).reshape(3, -1))
    r["L2f_route_scale"] = a["L2_ffn_route_scale"].reshape(1)
    for n, m in (("Wr", "router_w"), ("router_b", "router_b"), ("W1", "w1"), ("W2", "w2"), ("b2", "b2")):
        r["L3f_" + n] = c(a["L3_ffn_" + m])
    r["L3f_b1"] = columns(a["L3_ffn_b1"])
    return r


def kernel(**inputs):
    import numpy as np
    import concourse.bacc as bacc
    from concourse.bass_utils import run_bass_kernel_spmd

    nc = bacc.Bacc("TRN2", target_bir_lowering=False, num_devices=1)
    arrays, aps = {}, {}
    for name, a in layouts(inputs).items():
        arrays[name + "_dram"] = a
        aps[name] = nc.dram_tensor(name + "_dram", a.shape, mybir.dt.from_np(a.dtype), kind="ExternalInput").ap()
    for p, e in (("L1f_", 9), ("L2f_", 9), ("L3f_", 16)):
        aps[p + "gates"] = nc.dram_tensor(p + "gates_dram", [e, T], F32, kind="Internal").ap()
    for n in "qk":
        aps[n + "_dram"] = nc.dram_tensor(n + "_parts_dram", [NB, 2, D, S], F32, kind="Internal").ap()
    out = nc.dram_tensor("out_dram", [D, T], F32, kind="ExternalOutput").ap()
    decoder(nc, aps, out)
    r = run_bass_kernel_spmd(nc, [arrays], core_ids=[0])
    return np.ascontiguousarray(r.results[0]["out_dram"].T).reshape(NB, S, D)
```
